# Optimizing a Trainium2 kernel written in Bass

```python
import numpy as np
import jax
import jax.numpy as jnp

def _softmax(x, axis=-1):
    return jax.nn.softmax(x, axis=axis)

def _gelu(x):
    return jax.nn.gelu(x, approximate=True)

def _silu(x):
    return jax.nn.silu(x)

def _sigmoid(x):
    return jax.nn.sigmoid(x)

def _layernorm(x, axis=-1, eps=1e-05):
    m = jnp.mean(x, axis=axis, keepdims=True)
    v = jnp.var(x, axis=axis, keepdims=True)
    return (x - m) / jnp.sqrt(v + eps)

def _scatter_add(tgt, idx, src, axis=0):
    return tgt.at[idx].add(src)

def _segment_sum(src, seg, n):
    return jax.ops.segment_sum(src, seg, n)
kernel_name = 'mk_decoder_postln_d2_seqx_r4_07759c'

def setup_inputs(seed: int=0):
    np.random.seed(seed)
    _w = jnp.asarray

    def _rec_inputs():
        import jax
        import jax.numpy as jnp
        _rk = jax.random.key(seed)
        x = -0.0002928 + 1 * jax.random.normal(jax.random.fold_in(_rk, 1), (64, 256, 256), jnp.float32)
        _lenS = 256 - jax.random.randint(jax.random.fold_in(_rk, 7), (64,), 0, max(1, 256 // 4) + 1, jnp.int32)
        _lenS2 = 77 - jax.random.randint(jax.random.fold_in(_rk, 8), (64,), 0, max(1, 77 // 4) + 1, jnp.int32)
        _ctx_1024P = jax.random.normal(jax.random.fold_in(_rk, 11), (64, 16, 256), jnp.float32)
        _ctx_1024c = jax.random.dirichlet(jax.random.fold_in(_rk, 511), 0.3 * jnp.ones((16,), jnp.float32), (64, 77))
        _ctx_1024t = jnp.einsum('bsk,bkd->bsd', _ctx_1024c, _ctx_1024P)
        _ctx_1024t = _ctx_1024t * jax.lax.rsqrt(jnp.mean(jnp.square(_ctx_1024t)) + 1e-12) * 0.953939
        ctx_1024 = -1.39393e-06 + 0.999914 * (_ctx_1024t + 0.3 * jax.random.normal(jax.random.fold_in(_rk, 611), (64, 77, 256), jnp.float32))
        return (x, ctx_1024)
    x, ctx_1024 = _rec_inputs()

    def _L0_attn_setup():
        import jax, jax.numpy as jnp
        import numpy as np
        NUM_HEADS = 16
        key = jax.random.key(seed)
        kx, kq, kk, kv = jax.random.split(key, 4)
        N, S, D = (2, 1024, 256)
        scale = 1.0 / np.sqrt(D)
        x = jax.random.normal(kx, (N, S, D), dtype=jnp.float32)
        Wq = jax.random.normal(kq, (D, D), dtype=jnp.float32) * scale
        Wk = jax.random.normal(kk, (D, D), dtype=jnp.float32) * scale
        Wv = jax.random.normal(kv, (D, D), dtype=jnp.float32) * scale
        return {'x': x, 'Wq': Wq, 'Wk': Wk, 'Wv': Wv}
    _L0_attn_all = _L0_attn_setup()
    _L0_attn_in = {k: v for k, v in _L0_attn_all.items() if k in ('Wq', 'Wk', 'Wv')}
    del _L0_attn_all

    def _L0_xattn_setup():
        import jax, jax.numpy as jnp
        import numpy as np
        D_MODEL = 256
        HEAD = 16
        D_K = D_MODEL // HEAD
        key = jax.random.key(seed)
        ks = jax.random.split(key, 11)
        B, S = (2, 512)
        scale = 1.0 / np.sqrt(D_MODEL)
        inp = {'q': jax.random.normal(ks[0], (B, S, D_MODEL), dtype=jnp.float32), 'k': jax.random.normal(ks[1], (B, S, D_MODEL), dtype=jnp.float32), 'v': jax.random.normal(ks[2], (B, S, D_MODEL), dtype=jnp.float32), 'wq': jax.random.normal(ks[3], (D_MODEL, D_MODEL), dtype=jnp.float32) * scale, 'bq': jnp.zeros((D_MODEL,), dtype=jnp.float32), 'wk': jax.random.normal(ks[4], (D_MODEL, D_MODEL), dtype=jnp.float32) * scale, 'bk': jnp.zeros((D_MODEL,), dtype=jnp.float32), 'wv': jax.random.normal(ks[5], (D_MODEL, D_MODEL), dtype=jnp.float32) * scale, 'bv': jnp.zeros((D_MODEL,), dtype=jnp.float32), 'wo': jax.random.normal(ks[6], (D_MODEL, D_MODEL), dtype=jnp.float32) * scale, 'bo': jnp.zeros((D_MODEL,), dtype=jnp.float32)}
        return inp
    _L0_xattn_all = _L0_xattn_setup()
    _L0_xattn_in = {k: v for k, v in _L0_xattn_all.items() if k in ('wq', 'bq', 'wk', 'bk', 'wv', 'bv', 'wo', 'bo')}
    del _L0_xattn_all

    def _L0_ffn_setup():
        import jax, jax.numpy as jnp
        import numpy as np
        HIDDEN = 256
        INNER = 1024

        def _weight_quant(w):
            scale = 1.0 / jnp.clip(jnp.mean(jnp.abs(w)), 1e-05)
            wq = jnp.clip(jnp.round(w * scale), -1.0, 1.0) / scale
            return w + jax.lax.stop_gradient(wq - w)

        def _act_quant(x):
            scale = 127.0 / jnp.clip(jnp.max(jnp.abs(x), axis=-1, keepdims=True), 1e-05)
            xq = jnp.clip(jnp.round(x * scale), -128.0, 127.0) / scale
            return x + jax.lax.stop_gradient(xq - x)

        def _bitlinear(x, w):
            return jnp.einsum('bsi,oi->bso', _act_quant(x), _weight_quant(w))
        key = jax.random.key(seed)
        k0, k1, k2, k3 = jax.random.split(key, 4)
        x = jax.random.normal(k0, (4, 512, HIDDEN), dtype=jnp.float32)
        w_gate = jax.random.normal(k1, (INNER, HIDDEN), dtype=jnp.float32) / np.sqrt(HIDDEN)
        w_up = jax.random.normal(k2, (INNER, HIDDEN), dtype=jnp.float32) / np.sqrt(HIDDEN)
        w_down = jax.random.normal(k3, (HIDDEN, INNER), dtype=jnp.float32) / np.sqrt(INNER)
        return {'x': x, 'w_gate': w_gate, 'w_up': w_up, 'w_down': w_down}
    _L0_ffn_all = _L0_ffn_setup()
    _L0_ffn_in = {k: v for k, v in _L0_ffn_all.items() if k in ('w_gate', 'w_up', 'w_down')}
    del _L0_ffn_all

    def _L1_attn_setup():
        import jax, jax.numpy as jnp
        import numpy as np
        DIM = 256
        NUM_HEADS = 16
        HEAD_DIM = DIM // NUM_HEADS
        ROPE_BASE = 10000.0

        def rope_cos_sin(seq_len, dim):
            inv_freq = 1.0 / ROPE_BASE ** (jnp.arange(0, dim, 2, dtype=jnp.float32) / dim)
            t = jnp.arange(seq_len, dtype=jnp.float32)
            freqs = t[:, None] * inv_freq[None, :]
            emb = jnp.concatenate([freqs, freqs], axis=-1)
            return (jnp.cos(emb), jnp.sin(emb))

        def apply_rotary(x, cos, sin):
            x1 = x[..., ::2]
            x2 = x[..., 1::2]
            x_rot = jnp.stack((-x2, x1), axis=-1).reshape(x.shape)
            return x * cos + x_rot * sin
        key = jax.random.key(seed)
        ks = jax.random.split(key, 5)
        B, L, C = (4, 512, DIM)
        s = 1.0 / np.sqrt(C)
        return {'x': jax.random.normal(ks[0], (B, L, C), dtype=jnp.float32), 'qkv_w': jax.random.normal(ks[1], (3 * C, C), dtype=jnp.float32) * s, 'qkv_b': jax.random.normal(ks[2], (3 * C,), dtype=jnp.float32) * 0.02, 'proj_w': jax.random.normal(ks[3], (C, C), dtype=jnp.float32) * s, 'proj_b': jax.random.normal(ks[4], (C,), dtype=jnp.float32) * 0.02}
    _L1_attn_all = _L1_attn_setup()
    _L1_attn_in = {k: v for k, v in _L1_attn_all.items() if k in ('qkv_w', 'qkv_b', 'proj_w', 'proj_b')}
    del _L1_attn_all

    def _L1_xattn_setup():
        import jax, jax.numpy as jnp
        import numpy as np
        from jax import lax
        BIG = jnp.float32(1e+30)

        def _pairwise_euclidean(a, b):
            aa = jnp.sum(a * a, axis=-1)[:, None]
            bb = jnp.sum(b * b, axis=-1)[None, :]
            ab = a @ b.T
            return jnp.sqrt(jnp.maximum(aa + bb - 2.0 * ab, 0.0))

        def _dtw_cost(D):
            row0 = jnp.cumsum(D[0])

            def row_step(prev_row, d_row):
                first = d_row[0] + prev_row[0]

                def col_step(left, inp):
                    d_ij, up, diag = inp
                    r = d_ij + jnp.minimum(jnp.minimum(up, left), diag)
                    return (r, r)
                _, rest = lax.scan(col_step, first, (d_row[1:], prev_row[1:], prev_row[:-1]))
                row = jnp.concatenate([first[None], rest])
                return (row, row)
            _, rows = lax.scan(row_step, row0, D[1:])
            return jnp.concatenate([row0[None], rows], axis=0)

        def _backtrack(R, T1, T2):
            L = T1 + T2 - 1

            def step(carry, _):
                i, j, done = carry
                valid = jnp.logical_not(done)
                cd = jnp.where((i > 0) & (j > 0), R[jnp.maximum(i - 1, 0), jnp.maximum(j - 1, 0)], BIG)
                cu = jnp.where(i > 0, R[jnp.maximum(i - 1, 0), j], BIG)
                cl = jnp.where(j > 0, R[i, jnp.maximum(j - 1, 0)], BIG)
                choice = jnp.argmin(jnp.stack([cd, cu, cl]))
                ni = jnp.where(choice <= 1, i - 1, i)
                nj = jnp.where((choice == 0) | (choice == 2), j - 1, j)
                at_origin = (i == 0) & (j == 0)
                ni = jnp.where(at_origin, 0, ni)
                nj = jnp.where(at_origin, 0, nj)
                return ((ni, nj, done | at_origin), (i, j, valid))
            init = (jnp.int32(T1 - 1), jnp.int32(T2 - 1), jnp.bool_(False))
            _, (i_idx, j_idx, valid) = lax.scan(step, init, None, length=L)
            return (i_idx, j_idx, valid)

        def _align_one(small, large):
            T_small, d = small.shape
            T_large = large.shape[0]
            D = _pairwise_euclidean(small, large)
            R = _dtw_cost(D)
            i_idx, j_idx, valid = _backtrack(R, T_small, T_large)
            contrib = small[i_idx] * valid[:, None].astype(small.dtype)
            expanded = jnp.zeros((T_large, d), dtype=small.dtype).at[j_idx].add(contrib)
            return expanded
        key = jax.random.key(seed)
        k1, k2 = jax.random.split(key)
        teacher = jax.random.normal(k1, (16, 100, 256), dtype=jnp.float32)
        student = jax.random.normal(k2, (16, 150, 256), dtype=jnp.float32)
        return {'teacher_features': teacher, 'student_features': student}
    _L1_xattn_all = _L1_xattn_setup()
    _L1_xattn_in = {k: v for k, v in _L1_xattn_all.items() if k in ()}
    del _L1_xattn_all

    def _L1_ffn_setup():
        import jax, jax.numpy as jnp
        import numpy as np
        import math
        DIM = 256
        NUM_HEADS = 16
        SHARED_HEADS = 1
        ROUTED_HEADS = 3
        HEAD_DIM = DIM // NUM_HEADS
        B, N = (2, 512)
        key = jax.random.key(seed)
        ks = jax.random.split(key, 16)
        s = 1.0 / math.sqrt(DIM)
        inp = {'x': jax.random.normal(ks[0], (B, N, DIM), dtype=jnp.float32), 'Wq': jax.random.uniform(ks[1], (DIM, DIM), minval=-s, maxval=s), 'bq': jax.random.uniform(ks[2], (DIM,), minval=-s, maxval=s), 'Wk': jax.random.uniform(ks[3], (DIM, DIM), minval=-s, maxval=s), 'bk': jax.random.uniform(ks[4], (DIM,), minval=-s, maxval=s), 'Wv': jax.random.uniform(ks[5], (DIM, DIM), minval=-s, maxval=s), 'bv': jax.random.uniform(ks[6], (DIM,), minval=-s, maxval=s), 'Wp': jax.random.uniform(ks[7], (DIM, DIM), minval=-s, maxval=s), 'bp': jax.random.uniform(ks[8], (DIM,), minval=-s, maxval=s), 'Wr': jax.random.uniform(ks[9], (NUM_HEADS - SHARED_HEADS, DIM), minval=-s, maxval=s), 'br': jax.random.uniform(ks[10], (NUM_HEADS - SHARED_HEADS,), minval=-s, maxval=s), 'Ws': jax.random.uniform(ks[11], (2, DIM), minval=-s, maxval=s), 'bs': jax.random.uniform(ks[12], (2,), minval=-s, maxval=s), 'temperature': jnp.full((NUM_HEADS, 1, 1), float(np.log(np.expm1(1.0 / 0.24))), dtype=jnp.float32), 'query_embedding': 0.02 * jax.random.normal(ks[13], (NUM_HEADS, 1, HEAD_DIM), dtype=jnp.float32)}
        return inp
    _L1_ffn_all = _L1_ffn_setup()
    _L1_ffn_in = {k: v for k, v in _L1_ffn_all.items() if k in ('Wq', 'bq', 'Wk', 'bk', 'Wv', 'bv', 'Wp', 'bp', 'Wr', 'br', 'Ws', 'bs', 'temperature', 'query_embedding')}
    del _L1_ffn_all
    return {'x': x, 'ctx_1024': ctx_1024, 'L0_attn_Wq': _L0_attn_in['Wq'], 'L0_attn_Wk': _L0_attn_in['Wk'], 'L0_attn_Wv': _L0_attn_in['Wv'], 'L0_xattn_wq': _L0_xattn_in['wq'], 'L0_xattn_bq': _L0_xattn_in['bq'], 'L0_xattn_wk': _L0_xattn_in['wk'], 'L0_xattn_bk': _L0_xattn_in['bk'], 'L0_xattn_wv': _L0_xattn_in['wv'], 'L0_xattn_bv': _L0_xattn_in['bv'], 'L0_xattn_wo': _L0_xattn_in['wo'], 'L0_xattn_bo': _L0_xattn_in['bo'], 'L0_ffn_w_gate': _L0_ffn_in['w_gate'], 'L0_ffn_w_up': _L0_ffn_in['w_up'], 'L0_ffn_w_down': _L0_ffn_in['w_down'], 'L1_attn_qkv_w': _L1_attn_in['qkv_w'], 'L1_attn_qkv_b': _L1_attn_in['qkv_b'], 'L1_attn_proj_w': _L1_attn_in['proj_w'], 'L1_attn_proj_b': _L1_attn_in['proj_b'], 'L1_ffn_Wq': _L1_ffn_in['Wq'], 'L1_ffn_bq': _L1_ffn_in['bq'], 'L1_ffn_Wk': _L1_ffn_in['Wk'], 'L1_ffn_bk': _L1_ffn_in['bk'], 'L1_ffn_Wv': _L1_ffn_in['Wv'], 'L1_ffn_bv': _L1_ffn_in['bv'], 'L1_ffn_Wp': _L1_ffn_in['Wp'], 'L1_ffn_bp': _L1_ffn_in['bp'], 'L1_ffn_Wr': _L1_ffn_in['Wr'], 'L1_ffn_br': _L1_ffn_in['br'], 'L1_ffn_Ws': _L1_ffn_in['Ws'], 'L1_ffn_bs': _L1_ffn_in['bs'], 'L1_ffn_temperature': _L1_ffn_in['temperature'], 'L1_ffn_query_embedding': _L1_ffn_in['query_embedding']}

def reference(x, ctx_1024, L0_attn_Wq, L0_attn_Wk, L0_attn_Wv, L0_xattn_wq, L0_xattn_bq, L0_xattn_wk, L0_xattn_bk, L0_xattn_wv, L0_xattn_bv, L0_xattn_wo, L0_xattn_bo, L0_ffn_w_gate, L0_ffn_w_up, L0_ffn_w_down, L1_attn_qkv_w, L1_attn_qkv_b, L1_attn_proj_w, L1_attn_proj_b, L1_ffn_Wq, L1_ffn_bq, L1_ffn_Wk, L1_ffn_bk, L1_ffn_Wv, L1_ffn_bv, L1_ffn_Wp, L1_ffn_bp, L1_ffn_Wr, L1_ffn_br, L1_ffn_Ws, L1_ffn_bs, L1_ffn_temperature, L1_ffn_query_embedding):
    import jax
    import jax.numpy as jnp

    def _L0_attn_ref(x, Wq, Wk, Wv):
        import jax, jax.numpy as jnp
        import numpy as np
        NUM_HEADS = 16
        N, S, D = x.shape
        H = NUM_HEADS
        hd = D // H
        q = (x @ Wq.T).reshape(N, S, H, hd).transpose(0, 2, 1, 3)
        k = (x @ Wk.T).reshape(N, S, H, hd).transpose(0, 2, 1, 3)
        v = (x @ Wv.T).reshape(N, S, H, hd).transpose(0, 2, 1, 3)
        energy = jnp.einsum('nhqd,nhkd->nhqk', q, k)
        attn = jax.nn.softmax(energy / jnp.sqrt(jnp.float32(hd)), axis=3)
        out = jnp.einsum('nhql,nhld->nhqd', attn, v)
        return out.transpose(0, 2, 1, 3).reshape(N, S, D)

    def _L0_xattn_ref(q, k, v, wq, bq, wk, bk, wv, bv, wo, bo):
        import jax, jax.numpy as jnp
        import numpy as np
        D_MODEL = 256
        HEAD = 16
        D_K = D_MODEL // HEAD
        B, S, _ = q.shape

        def proj(x, w, b):
            y = x @ w.T + b
            return y.reshape(B, -1, HEAD, D_K).transpose(0, 2, 1, 3)
        qh, kh, vh = (proj(q, wq, bq), proj(k, wk, bk), proj(v, wv, bv))
        scores = jnp.einsum('bhqd,bhkd->bhqk', qh, kh) / jnp.sqrt(jnp.float32(D_K))
        probs = jax.nn.softmax(scores, axis=-1)
        ctx = jnp.einsum('bhqk,bhkd->bhqd', probs, vh)
        concat = ctx.transpose(0, 2, 1, 3).reshape(B, S, D_MODEL)
        return concat @ wo.T + bo

    def _L0_ffn_ref(x, w_gate, w_up, w_down):
        import jax, jax.numpy as jnp
        import numpy as np
        HIDDEN = 256
        INNER = 1024

        def _weight_quant(w):
            scale = 1.0 / jnp.clip(jnp.mean(jnp.abs(w)), 1e-05)
            wq = jnp.clip(jnp.round(w * scale), -1.0, 1.0) / scale
            return w + jax.lax.stop_gradient(wq - w)

        def _act_quant(x):
            scale = 127.0 / jnp.clip(jnp.max(jnp.abs(x), axis=-1, keepdims=True), 1e-05)
            xq = jnp.clip(jnp.round(x * scale), -128.0, 127.0) / scale
            return x + jax.lax.stop_gradient(xq - x)

        def _bitlinear(x, w):
            return jnp.einsum('bsi,oi->bso', _act_quant(x), _weight_quant(w))
        gate = jax.nn.silu(_bitlinear(x, w_gate))
        up = _bitlinear(x, w_up)
        return _bitlinear(gate * up, w_down)

    def _L1_attn_ref(x, qkv_w, qkv_b, proj_w, proj_b):
        import jax, jax.numpy as jnp
        import numpy as np
        DIM = 256
        NUM_HEADS = 16
        HEAD_DIM = DIM // NUM_HEADS
        ROPE_BASE = 10000.0

        def rope_cos_sin(seq_len, dim):
            inv_freq = 1.0 / ROPE_BASE ** (jnp.arange(0, dim, 2, dtype=jnp.float32) / dim)
            t = jnp.arange(seq_len, dtype=jnp.float32)
            freqs = t[:, None] * inv_freq[None, :]
            emb = jnp.concatenate([freqs, freqs], axis=-1)
            return (jnp.cos(emb), jnp.sin(emb))

        def apply_rotary(x, cos, sin):
            x1 = x[..., ::2]
            x2 = x[..., 1::2]
            x_rot = jnp.stack((-x2, x1), axis=-1).reshape(x.shape)
            return x * cos + x_rot * sin
        B, L, C = x.shape
        H, D = (NUM_HEADS, HEAD_DIM)
        scale = D ** (-0.5)
        qkv = x @ qkv_w.T + qkv_b
        qkv = qkv.reshape(B, L, 3, H, D).transpose(2, 0, 3, 1, 4)
        q, k, v = (qkv[0], qkv[1], qkv[2])
        cos, sin = rope_cos_sin(L, D)
        q = apply_rotary(q, cos, sin)
        k = apply_rotary(k, cos, sin)
        attn = jnp.einsum('bhqd,bhkd->bhqk', q, k) * scale
        attn = jax.nn.softmax(attn, axis=-1)
        out = jnp.einsum('bhqk,bhkd->bhqd', attn, v)
        out = out.transpose(0, 2, 1, 3).reshape(B, L, C)
        return out @ proj_w.T + proj_b

    def _L1_xattn_ref(teacher_features, student_features):
        import jax, jax.numpy as jnp
        import numpy as np
        from jax import lax
        BIG = jnp.float32(1e+30)

        def _pairwise_euclidean(a, b):
            aa = jnp.sum(a * a, axis=-1)[:, None]
            bb = jnp.sum(b * b, axis=-1)[None, :]
            ab = a @ b.T
            return jnp.sqrt(jnp.maximum(aa + bb - 2.0 * ab, 0.0))

        def _dtw_cost(D):
            row0 = jnp.cumsum(D[0])

            def row_step(prev_row, d_row):
                first = d_row[0] + prev_row[0]

                def col_step(left, inp):
                    d_ij, up, diag = inp
                    r = d_ij + jnp.minimum(jnp.minimum(up, left), diag)
                    return (r, r)
                _, rest = lax.scan(col_step, first, (d_row[1:], prev_row[1:], prev_row[:-1]))
                row = jnp.concatenate([first[None], rest])
                return (row, row)
            _, rows = lax.scan(row_step, row0, D[1:])
            return jnp.concatenate([row0[None], rows], axis=0)

        def _backtrack(R, T1, T2):
            L = T1 + T2 - 1

            def step(carry, _):
                i, j, done = carry
                valid = jnp.logical_not(done)
                cd = jnp.where((i > 0) & (j > 0), R[jnp.maximum(i - 1, 0), jnp.maximum(j - 1, 0)], BIG)
                cu = jnp.where(i > 0, R[jnp.maximum(i - 1, 0), j], BIG)
                cl = jnp.where(j > 0, R[i, jnp.maximum(j - 1, 0)], BIG)
                choice = jnp.argmin(jnp.stack([cd, cu, cl]))
                ni = jnp.where(choice <= 1, i - 1, i)
                nj = jnp.where((choice == 0) | (choice == 2), j - 1, j)
                at_origin = (i == 0) & (j == 0)
                ni = jnp.where(at_origin, 0, ni)
                nj = jnp.where(at_origin, 0, nj)
                return ((ni, nj, done | at_origin), (i, j, valid))
            init = (jnp.int32(T1 - 1), jnp.int32(T2 - 1), jnp.bool_(False))
            _, (i_idx, j_idx, valid) = lax.scan(step, init, None, length=L)
            return (i_idx, j_idx, valid)

        def _align_one(small, large):
            T_small, d = small.shape
            T_large = large.shape[0]
            D = _pairwise_euclidean(small, large)
            R = _dtw_cost(D)
            i_idx, j_idx, valid = _backtrack(R, T_small, T_large)
            contrib = small[i_idx] * valid[:, None].astype(small.dtype)
            expanded = jnp.zeros((T_large, d), dtype=small.dtype).at[j_idx].add(contrib)
            return expanded
        return jax.vmap(_align_one)(teacher_features, student_features)

    def _L1_ffn_ref(x, Wq, bq, Wk, bk, Wv, bv, Wp, bp, Wr, br, Ws, bs, temperature, query_embedding):
        import jax, jax.numpy as jnp
        import numpy as np
        import math
        DIM = 256
        NUM_HEADS = 16
        SHARED_HEADS = 1
        ROUTED_HEADS = 3
        HEAD_DIM = DIM // NUM_HEADS
        B, N = (2, 512)
        Bsz, Nn, C = x.shape
        H, hd = (NUM_HEADS, HEAD_DIM)

        def heads(W, b):
            y = x @ W.T + b
            return y.reshape(Bsz, Nn, H, hd).transpose(0, 2, 1, 3)
        q = heads(Wq, bq)
        k = heads(Wk, bk)
        v = heads(Wv, bv)
        q_norm = q / jnp.linalg.norm(q, axis=-1, keepdims=True)
        q_scaled = (q_norm + query_embedding[None]) * jax.nn.softplus(temperature)[None]
        attn = jnp.einsum('bhqd,bhkd->bhqk', q_scaled, k) / math.sqrt(hd)
        attn = jax.nn.softmax(attn, axis=-1)
        h = jnp.einsum('bhqk,bhkd->bhqd', attn, v)
        h = h.transpose(0, 2, 1, 3).reshape(Bsz, Nn, C)
        gates = jax.nn.softmax(h @ Wr.T + br, axis=-1)
        _, idx = jax.lax.top_k(gates, ROUTED_HEADS)
        mask = jax.nn.one_hot(idx, H - SHARED_HEADS, dtype=gates.dtype).sum(axis=-2)
        routed_gates = gates * mask * ROUTED_HEADS
        sw = jax.nn.softmax(h @ Ws.T + bs, axis=-1)
        shared_gates = sw * SHARED_HEADS
        weight_0 = sw * 2.0
        shared_gates = weight_0[..., 0:1] * shared_gates
        routed_gates = weight_0[..., 1:2] * routed_gates
        masked_gates = jnp.concatenate([shared_gates, routed_gates], axis=-1)
        out = h * masked_gates.sum(axis=-1, keepdims=True)
        return out @ Wp.T + bp
    x = _layernorm(x + _L0_attn_ref(x, L0_attn_Wq, L0_attn_Wk, L0_attn_Wv), axis=-1)
    x = _layernorm(x + _L0_xattn_ref(x, ctx_1024, ctx_1024, L0_xattn_wq, L0_xattn_bq, L0_xattn_wk, L0_xattn_bk, L0_xattn_wv, L0_xattn_bv, L0_xattn_wo, L0_xattn_bo), axis=-1)
    x = _layernorm(x + _L0_ffn_ref(x, L0_ffn_w_gate, L0_ffn_w_up, L0_ffn_w_down), axis=-1)
    x = _layernorm(x + _L1_attn_ref(x, L1_attn_qkv_w, L1_attn_qkv_b, L1_attn_proj_w, L1_attn_proj_b), axis=-1)
    x = _layernorm(x + _L1_xattn_ref(ctx_1024, x), axis=-1)
    x = _layernorm(x + _L1_ffn_ref(x, L1_ffn_Wq, L1_ffn_bq, L1_ffn_Wk, L1_ffn_bk, L1_ffn_Wv, L1_ffn_bv, L1_ffn_Wp, L1_ffn_bp, L1_ffn_Wr, L1_ffn_br, L1_ffn_Ws, L1_ffn_bs, L1_ffn_temperature, L1_ffn_query_embedding), axis=-1)
    return x

_drawn_inputs = setup_inputs


def setup_inputs(seed=0):
    import zlib

    import numpy as np

    out = dict(_drawn_inputs(seed))
    spreads = {'L0_xattn_bq': (0.0, 0.1),
     'L0_xattn_bk': (0.0, 2.0),
     'L0_xattn_bv': (0.0, 0.1),
     'L0_xattn_bo': (0.0, 0.1),
     'L1_ffn_temperature': (4.151041507720947, 0.6)}
    factors = {'L1_ffn_bq': 8.0,
     'L1_ffn_bk': 64.0,
     'L1_ffn_Wr': 5.236,
     'L1_ffn_br': 8.0,
     'L1_ffn_Ws': 8.0,
     'L1_ffn_bs': 42.757,
     'L1_ffn_query_embedding': 8.0}
    for name, (base, spread) in spreads.items():
        noise = np.random.default_rng([zlib.crc32(name.encode()), seed]).standard_normal(out[name].shape)
        drawn = base * np.exp(spread * noise) if base else spread * noise
        out[name] = jnp.asarray(drawn.astype(out[name].dtype))
    for name, factor in factors.items():
        out[name] = (out[name] * factor).astype(out[name].dtype)
    return out
```

```python
from contextlib import ExitStack

import concourse.bass as bass
import numpy as np
from concourse import mybir

ALU = mybir.AluOpType
ACT = mybir.ActivationFunctionType
AX = mybir.AxisListType
F32 = mybir.dt.float32
BF16 = mybir.dt.bfloat16

P = 128
D = 256
S = 256
C = 77
H = 16
HD = D // H
FC = D // P
QT = S // P
HID = 1024
HC = HID // P
HALF = 512
VW = HD + 1
EPS = 1e-5
MAGIC = 1.5 * 2.0 ** 23
QMAX = 127.0
BIG = 3.0e38
ROUTED = 3

KEYS = {"A1": S, "A2": C, "A3": S, "A4": S}
ALL_BIASES = ("A2_bo", "A2_bv", "A3_bq", "A3_bk", "A3_bv", "A3_bo", "A4_bq", "A4_bv", "A4_bo")


def key_tiles(att):
    return [(k, min(P, KEYS[att] - k)) for k in range(0, KEYS[att], P)]


def place(h):
    return h // 8, 32 * (h % 8 // 2), h % 2



def before_core(att, s):
    steps = [("q", att, s), ("k", att, s), ("v", att, s)]
    if att == "A3":
        steps += [("rot", att, s), ("qT", att, s), ("kT", att, s)]
    if att == "A4":
        steps += [("rot", att, s), ("qT", att, s)]
    steps += [("max", att, s, h) for h in range(H)]
    steps += [("shift", att, s, 0), ("shift", att, s, 1)]
    return steps


def core(att, s):
    return [("core", att, s, h) for h in range(H + 1)]


def mlp(s):
    steps = [("fq", "F", s), ("xqT", "F", s)]
    for t in range(QT):
        steps += [("gu", "F", s, t, 0), ("gu", "F", s, t, 1), ("hq", "F", s, t), ("hT", "F", s, t)]
    return steps + [("down", "F", s), ("ln", "F", s)]


def after_core(att, s):
    steps = [("norm", att, s)]
    if att == "A2" or att == "A3":
        steps += [("oT", att, s), ("oproj", att, s)]
    if att == "A4":
        steps += [("oT", att, s), ("gate", att, s), ("oproj", att, s)]
    steps += [("ln", att, s)]
    if att == "A1":
        steps += [("xT", att, s)] + before_core("A2", s)
    if att == "A2":
        steps += mlp(s) + [("xT", "F", s)] + before_core("A3", s)
    if att == "A3":
        steps += [("xT", att, s), ("dist", att, s)]
    return steps


def align(s):
    return [("expand", "E", s), ("ln", "E", s), ("xT", "E", s)] + before_core("A4", s)


def weave(core_steps, others, lead=1):
    out, n = list(core_steps[:lead]), len(core_steps) - lead
    done = 0
    for i, step in enumerate(core_steps[lead:]):
        upto = (len(others) * (i + 1) + n - 1) // n
        out += others[done:upto]
        done = upto
        out.append(step)
    return out + list(others[done:])


ORDER_A = (
    before_core("A1", 0)
    + weave(core("A1", 0), before_core("A1", 1))
    + weave(core("A1", 1), after_core("A1", 0))
    + weave(core("A2", 0), after_core("A1", 1))
    + weave(core("A2", 1), after_core("A2", 0))
    + weave(core("A3", 0), after_core("A2", 1))
    + weave(core("A3", 1), after_core("A3", 0))
    + after_core("A3", 1)
)
ORDER_C = (
    align(0)
    + weave(core("A4", 0), align(1))
    + weave(core("A4", 1), after_core("A4", 0))
    + after_core("A4", 1)
)


def bank_uses(step):
    kind = step[0]
    if kind in ("q", "k", "v", "qT", "kT", "shift", "xT", "oT", "oproj", "xqT", "hT", "down",
                "dist", "expand", "gate"):
        return [step]
    if kind == "gu":
        return [step + ("gate",), step + ("up",)]
    return []


def signals(step):
    kind, att = step[0], step[1]
    token_q = att in ("A3", "A4")
    if kind == "q":
        return ["q_tokens"] if token_q else ["q_ready", "qb_ready"]
    if kind == "k":
        return ["q_tokens"] if att == "A3" else ["k_ready"]
    if kind == "v":
        return ["v_ready"]
    if kind == "rot":
        return ["rotated"] if att == "A3" else ["squared", "norms2", "rotated"]
    if kind == "qT":
        return ["q_ready", "qb_ready"]
    if kind == "kT":
        return ["k_ready"]
    if kind == "max":
        return ["max_scores", "max_done"]
    if kind == "shift":
        return ["q_shifted"]
    if kind == "core":
        return (["scores_ready", "probs_ready"] if step[3] < H else ["out_ready"])
    if kind == "norm":
        return ["out_taken"] + ([] if att != "A1" else ["x_used"])
    if kind == "oT":
        return ["attnT_ready"]
    if kind == "gate":
        return ["logits_taken", "logits_ready", "exps_ready"]
    if kind == "ln":
        return ["var_ready", "rstd_ready", "x_ready"]
    if kind == "xT":
        return ["xT_ready"]
    if kind == "fq":
        return ["xq_ready"]
    if kind == "xqT":
        return ["xqT_ready"]
    if kind == "gu":
        return ["tanh_ready", "gated", "hid_ready"]
    if kind == "hq":
        return ["hq_ready"]
    if kind == "hT":
        return ["hqT_ready"]
    if kind == "dist":
        return ["squares_ready", "dist_ready"]
    if kind == "expand":
        return ["x4_used"]
    if kind == "oproj":
        return ["proj_taken"]
    if kind == "down":
        return ["down_taken"]
    return []


def emptied_by(use):
    kind, att = use[0], use[1]
    if kind == "gu":
        return "gated" if use[-1] == "gate" else "hid_ready"
    if kind == "q":
        return "q_tokens" if att in ("A3", "A4") else "q_ready"
    if kind == "k":
        return "q_tokens" if att == "A3" else "k_ready"
    return {"v": "v_ready", "qT": "q_ready", "kT": "k_ready", "shift": "q_shifted", "xT": "xT_ready",
            "oT": "attnT_ready", "oproj": "proj_taken", "xqT": "xqT_ready", "hT": "hqT_ready",
            "down": "down_taken", "dist": "dist_ready", "expand": "x4_used", "gate": "logits_taken"}[kind]


SIGNALS = sorted({x for o in (ORDER_A, ORDER_C) for step in o for x in signals(step)})


class Counts:

    def __init__(self, order):
        self.at, self.per, self.bank, self.bank_per = {}, {x: 0 for x in SIGNALS}, {}, 0
        uses = [use for step in order for use in bank_uses(step)]
        self.before = {use: (uses[i - 2], i < 2) for i, use in enumerate(uses)}
        for step in order:
            for x in signals(step):
                self.per[x] += 1
                self.at[x, step] = self.per[x]
            for use in bank_uses(step):
                self.bank[use] = (self.bank_per % 2, self.bank_per // 2 + 1)
                self.bank_per += 1
        assert self.bank_per % 2 == 0
        self.bank_per //= 2


COUNTS_A, COUNTS_C = Counts(ORDER_A), Counts(ORDER_C)
CHAIN = {"A": {"dve": 0, "pool": 0}, "C": {"dve": 0, "pool": 0}}
CHAIN["A"]["dve"], CHAIN["A"]["pool"] = 58, 14
CHAIN["C"]["dve"], CHAIN["C"]["pool"] = 24, 10


def build(nc, nb, io, out):
    iters = nb // 2
    stack = ExitStack()
    with stack:
        def sem(name):
            return stack.enter_context(nc.semaphore(name))

        def sb(name, shape, dt=F32, where=stack):
            return where.enter_context(nc.sbuf_tensor(name, shape, dt))

        sems = {x: sem(x) for x in SIGNALS}
        bank_full = [sem("bank_full0"), sem("bank_full1")]
        dve_step, pool_step = sem("dve_step"), sem("pool_step")
        consts_loaded, consts_ready = sem("consts_loaded"), sem("consts_ready")
        setup_dve, setup_act, setup_pe, setup_pool = (
            sem("setup_dve"), sem("setup_act"), sem("setup_pe"), sem("setup_pool"))
        x_loaded = [sem("x_loaded0"), sem("x_loaded1")]
        x4_stored = [sem("x4_stored0"), sem("x4_stored1")]
        dist_stored = sem("dist_stored")
        phase_a_done = sem("phase_a_done")
        dist_loaded = [sem(f"dist_loaded{i}") for i in range(2)]
        roots_ready = sem("roots_ready")
        passed = sem("passed")
        on_ready = sem("on_ready")
        dtw_step, path_ready, path_stored = sem("dtw_step"), sem("path_ready"), sem("path_stored")
        path_loaded = [sem("path_loaded0"), sem("path_loaded1")]
        out_stored = [sem("out_stored0"), sem("out_stored1")]
        consts_pool = sem("consts_pool")

        pj = [stack.enter_context(nc.psum_tensor(f"pj{i}", [P, HALF], F32)) for i in range(2)]
        sm = [stack.enter_context(nc.psum_tensor(f"sm{i}", [P, HALF], F32)) for i in range(2)]
        st = [stack.enter_context(nc.psum_tensor(f"st{i}", [P, HALF], F32)) for i in range(2)]
        po = [stack.enter_context(nc.psum_tensor(f"po{i}", [P, HALF], F32)) for i in range(2)]

        x4_dram = nc.dram_tensor("x4_scratch", [nb, P, QT * D], F32, kind="Internal").ap()
        dist_dram = nc.dram_tensor("dist_scratch", [nb, C, S], F32, kind="Internal").ap()
        path_dram = nc.dram_tensor("path_scratch", [nb, C, S], F32, kind="Internal").ap()

        w = {n: sb(n, [P, FC, D]) for n in io["square_weights"]}
        col = {n: sb(n, [P, FC]) for n in ("A2_bq", "A2_bk", "A4_bk")}
        row = {n: sb(n, [P, D]) for n in ALL_BIASES}
        gate_w = sb("gate_w", [P, FC, H + 1])
        gate_b = sb("gate_b", [P, H + 1])
        temp_sp = sb("temp_sp", [P, H])
        qe_sp = sb("qe_sp", [P, H, HD])
        wg, wu = sb("wg", [P, FC, HID], BF16), sb("wu", [P, FC, HID], BF16)
        wd = sb("wd", [P, HC, D], BF16)
        wq_inv = sb("wq_inv", [P, 3])
        ident, ident_b = sb("ident", [P, P]), sb("ident_b", [P, P], BF16)
        mask = sb("mask", [P, 4])
        kbias = {a: sb(f"kbias_{a}", [P, 2, FC]) for a in ("A2", "A4")}
        rope_cos, rope_sin = sb("rope_cos", [P, QT, HD]), sb("rope_sin", [P, QT, HD])
        neg_half = sb("neg_half", [P, S])
        ones = sb("ones", [P, P])
        power = sb("power", [P, QT * H])

        def mask_col(i, n=P):
            return mask[0:n, i:i + 1]

        with ExitStack() as setup:
            wf = [sb(f"wf{i}", [P, 2048], F32, setup) for i in range(3)]
            wt = sb("wt", [P, 2048], F32, setup)
            small = sb("setup_small", [P, 16], F32, setup)
            spx = sb("spx", [P, 4, H], F32, setup)
            block = setup.enter_context(nc.Block())
            loads = [(wf[0][:], io["w_gate"]), (wf[1][:], io["w_up"]), (wf[2][:], io["w_down"])]
            loads += [(w[n][:].rearrange("p a b -> p (a b)"), io[n]) for n in w]
            loads += [(col[n][:], io[n]) for n in col]
            loads += [(row[n][:], io[n][None, :].partition_broadcast(P).rearrange("p o d -> p (o d)"))
                      for n in row]
            loads += [(gate_w[:].rearrange("p a b -> p (a b)"), io["gate_w"]),
                      (gate_b[:], io["gate_b"][None, :].partition_broadcast(P).rearrange("p o d -> p (o d)")),
                      (temp_sp[:], io["temperature"][None, :].partition_broadcast(P).rearrange("p o d -> p (o d)")),
                      (qe_sp[:].rearrange("p h d -> p (h d)"),
                       io["query_embedding"][None, :].partition_broadcast(P).rearrange("p o d -> p (o d)")),
                      (ident[:], io["ident"]), (mask[:], io["mask"]),
                      (rope_cos[:].rearrange("p t d -> p (t d)"), io["rope_cos"]),
                      (rope_sin[:].rearrange("p t d -> p (t d)"), io["rope_sin"])]

            @block.sync
            def _(sp):
                for dst, src in loads:
                    sp.dma_start(dst, src).then_inc(consts_loaded, 16)

            @block.gpsimd
            def _(pool):
                pool.memset(neg_half[:], -0.5)
                pool.memset(ones[:], 1.0)
                pool.memset(power[:], -0.5).then_inc(setup_pool, 1)

            @block.tensor
            def _(pe):
                pe.wait_ge(setup_pool, 1)
                pe.wait_ge(setup_dve, 3)
                pe.matmul(pj[0][:, 0:3], ones[:], small[:, 0:3], start=True,
                          stop=True).then_inc(setup_pe, 1)

            @block.scalar
            def _(act):
                act.wait_ge(consts_loaded, 16 * len(loads))
                act.activation(spx[:, 0, :], temp_sp[:], ACT.Abs).then_inc(setup_act, 1)
                act.wait_ge(setup_act, 1)
                act.activation(spx[:, 1, :], spx[:, 0, :], ACT.Exp, scale=-1.0).then_inc(setup_act, 1)
                act.wait_ge(setup_act, 2)
                act.activation(spx[:, 2, :], spx[:, 1, :], ACT.Ln, bias=1.0).then_inc(setup_act, 1)

            @block.vector
            def _(dve):
                done = [0]

                def link(ins):
                    done[0] += 1
                    ins.then_inc(setup_dve, 1)
                    dve.wait_ge(setup_dve, done[0])

                dve.wait_ge(consts_loaded, 16 * len(loads))
                for i in range(3):
                    link(dve.tensor_reduce(small[:, i:i + 1], wf[i][:], AX.X, ALU.add,
                                           apply_absolute_value=True))
                dve.wait_ge(setup_pe, 1)
                link(dve.tensor_scalar(small[:, 3:6], pj[0][:, 0:3], 1.0 / (HID * D), EPS, ALU.mult, ALU.max))
                link(dve.reciprocal(small[:, 6:9], small[:, 3:6]))
                link(dve.reciprocal(wq_inv[:], small[:, 6:9]))
                for i, q in enumerate((wg, wu, wd)):
                    flat = q[:].rearrange("p a b -> p (a b)")
                    link(dve.tensor_scalar(wt[:], wf[i][:], small[:, 6 + i:7 + i], MAGIC, ALU.mult, ALU.add))
                    link(dve.tensor_scalar(wt[:], wt[:], MAGIC, 1.0, ALU.subtract, ALU.min))
                    link(dve.tensor_scalar(flat, wt[:], -1.0, None, ALU.max))
                link(dve.tensor_copy(ident_b[:], ident[:]))
                for a in ("A2", "A4"):
                    for e in range(2):
                        link(dve.tensor_scalar(kbias[a][:, e, :], col[a + "_bk"][:], mask_col(e),
                                               mask_col(2 + e), ALU.mult, ALU.add))
                dve.wait_ge(setup_act, 3)
                link(dve.tensor_scalar(spx[:, 3, :], temp_sp[:], 0.0, None, ALU.max))
                link(dve.tensor_tensor(temp_sp[:], spx[:, 3, :], spx[:, 2, :], ALU.add))
                link(dve.tensor_tensor(qe_sp[:], qe_sp[:], temp_sp[:].unsqueeze(2).to_broadcast([P, H, HD]),
                                       ALU.mult))

        def run(phase, where, counts, base):
            order = ORDER_A if phase == "A" else ORDER_C
            inputs_loaded = x_loaded if phase == "A" else path_loaded
            x0 = [sb(f"{phase}x0_{s}", [P, QT, D], F32, where) for s in range(2)]
            x = [sb(f"{phase}x_{s}", [P, QT, D], F32, where) for s in range(2)]
            if phase == "A":
                x0T = [sb(f"x0T_{s}", [P, FC, S], F32, where) for s in range(2)]
                ctxT = [sb(f"ctxT_{s}", [P, FC, C], F32, where) for s in range(2)]
                csq = sb("csq", [P, FC, C], F32, where)
                xsq = sb("xsq", [P, FC, S], F32, where)
                dist = sb("dist", [C, S], F32, where)
                xq_f, xq = sb("xq_f", [P, QT, D], F32, where), sb("xq", [P, QT, D], BF16, where)
                xqT = sb("xqT", [P, FC, S], BF16, where)
                th = sb("th", [P, 2, HALF], F32, where)
                hid = sb("hid", [P, 2, HALF], F32, where)
                hq = sb("hq", [P, HID], BF16, where)
                hqT = [sb(f"hqT{t}", [P, HC, P], BF16, where) for t in range(QT)]
                qsc = sb("qsc", [P, QT, 16], F32, where)
            else:
                path = [sb(f"path_{s}", [C, S], F32, where) for s in range(2)]
                ctx = [sb(f"ctx_{s}", [C, D], F32, where) for s in range(2)]
                sq = sb("sq", [P, QT * H, HD], F32, where)
                nrm = sb("nrm", [P, 2, QT, H], F32, where)
                lg = sb("lg", [P, QT, H + 1], F32, where)
                ex = sb("ex", [P, QT, H + 1], F32, where)
                top = sb("top", [P, QT, 8], F32, where)
                gs = sb("gs", [P, 16, QT], F32, where)
            ke = [[sb(f"{phase}k{e}_{s}", [P, FC, S], F32, where) for e in range(2)] for s in range(2)]
            qe = [[sb(f"{phase}q{e}_{s}", [P, FC, S], F32, where) for e in range(2)] for s in range(2)]
            vv = [sb(f"{phase}v_{s}", [P, QT, H, VW], F32, where) for s in range(2)]
            qf = sb(phase + "qf", [P, FC, S], F32, where)
            qb = [sb(f"{phase}qb{e}", [P, FC, S], BF16, where) for e in range(2)]
            kb = sb(phase + "kb", [P, FC, S], BF16, where)
            qk = sb(phase + "qk", [P, 2, QT, D], F32, where)
            qr = sb(phase + "qr", [P, 2, QT, D], F32, where)
            r2 = sb(phase + "r2", [P, QT, D], F32, where)
            mp = sb(phase + "mp", [P, QT, 2, FC, P], F32, where)
            xT = sb(phase + "xT", [P, FC, S], F32, where)
            pr = [sb(f"{phase}pr{i}", [P, QT, S], F32, where) for i in range(2)]
            rc = sb(phase + "rc", [P, QT, H], F32, where)
            at = sb(phase + "at", [P, QT, D], F32, where)
            atT = sb(phase + "atT", [P, FC, S], F32, where)
            res = sb(phase + "res", [P, QT, D], F32, where)
            stats = sb(phase + "stats", [P, QT, 6], F32, where)
            mv = sb(phase + "mv", [P, QT, 2], F32, where)
            ve = sb(phase + "ve", [P, QT, 2], F32, where)
            rstd = sb(phase + "rstd", [P, QT, 2], F32, where)
            block = where.enter_context(nc.Block())

            class Clock:

                def __init__(self, eng, it):
                    self.eng, self.it, self.seen = eng, it, {}
                    self.chain = 0

                def wait(self, name, step, behind=0, last=False):
                    k = counts.at[name, step] - behind + (0 if last else counts.per[name])
                    self.eng.wait_ge(sems[name], self.it * counts.per[name] + (base[name] + k))

                def tell(self, ins, name, step):
                    self.seen[name] = self.seen.get(name, 0) + 1
                    assert self.seen[name] == counts.at[name, step], (name, step)
                    ins.then_inc(sems[name], 1)

                def bank(self, use):
                    return pj[counts.bank[use][0]]

                def wait_bank_full(self, use):
                    self.eng.wait_ge(bank_full[counts.bank[use][0]],
                                     self.it * counts.bank_per + (base["bank"] + counts.bank[use][1]))

                def wait_bank_free(self, use):
                    before, last = counts.before[use]
                    self.wait(emptied_by(before), before[:-1] if before[0] == "gu" else before, last=last)

                def filled(self, ins, use):
                    ins.then_inc(bank_full[counts.bank[use][0]], 1)

                def iteration(self, semaphore, k=1, first=0):
                    self.eng.wait_ge(semaphore, self.it * (16 * k) + first)

            def alone(eng):
                eng.sem_inc(passed, 1)

            @block.sync
            def _(sp):
                def one(dram, b):
                    if isinstance(b, int):
                        return dram[b:b + 1].rearrange("o p n -> p o n")
                    return dram[bass.ds(b, 1)].rearrange("o p n -> p o n")

                def loads(it, s):
                    b = it * 2 + s
                    if phase == "A":
                        moves = [(x0T[s][:].rearrange("p a b -> p (a b)"), io["xT"]),
                                 (ctxT[s][:].rearrange("p a b -> p (a b)"), io["ctxT"]),
                                 (x0[s][:].rearrange("p a b -> p (a b)"), io["x"])]
                    else:
                        moves = [(path[s][:], path_dram), (ctx[s][:], io["ctx"]),
                                 (x0[s][:].rearrange("p a b -> p (a b)"), x4_dram)]
                    for dst, src in moves:
                        sp.dma_start(dst.unsqueeze(1), one(src, b)).then_inc(inputs_loaded[s], 16)

                def stores(it, s):
                    ck, b = Clock(sp, it), it * 2 + s
                    flat = x[s][:].rearrange("p a b -> p (a b)").unsqueeze(1)
                    if phase == "A":
                        ck.wait("x_ready", ("ln", "A3", s))
                        sp.dma_start(one(x4_dram, b), flat).then_inc(x4_stored[s], 16)
                        ck.wait("dist_ready", ("dist", "A3", s))
                        sp.dma_start(one(dist_dram, b), dist[:].unsqueeze(1)).then_inc(dist_stored, 16)
                    else:
                        ck.wait("x_ready", ("ln", "A4", s))
                        sp.dma_start(one(out, b), flat).then_inc(out_stored[s], 16)

                def next_loads(it, s):
                    if phase == "C":
                        Clock(sp, it).wait("x4_used", ("expand", "E", s))
                    loads(it + 1, s)

                for s in range(2):
                    loads(0, s)
                if iters > 1:
                    with sp.Fori(0, iters - 1) as it:
                        for s in range(2):
                            if phase == "C":
                                next_loads(it, s)
                            stores(it, s)
                            if phase == "A":
                                next_loads(it, s)
                for s in range(2):
                    stores(iters - 1, s)
                for s in range(2):
                    if phase == "A":
                        sp.wait_ge(x4_stored[s], 16 * (iters + 1))
                    else:
                        sp.wait_ge(out_stored[s], 16 * (iters + 1))
                if phase == "A":
                    sp.wait_ge(dist_stored, 16 * (nb + 1))

            @block.tensor
            def _(pe):
                def features(ck, step, weight, src, n):
                    bank = ck.bank(step)
                    ck.wait_bank_free(step)
                    for c in range(FC):
                        for f in range(FC):
                            ins = pe.matmul(bank[:, c * S:c * S + n], weight[:, f, c * P:(c + 1) * P],
                                            src[:, f, 0:n], start=(f == 0), stop=(f == FC - 1))
                    ck.filled(ins, step)

                def tokens(ck, step, weight, src, tiles):
                    bank = ck.bank(step)
                    ck.wait_bank_free(step)
                    for t, (k, n) in enumerate(tiles):
                        for f in range(FC):
                            ins = pe.matmul(bank[0:n, t * D:(t + 1) * D], src[:, f, k:k + n],
                                            weight[:, f, :], start=(f == 0), stop=(f == FC - 1))
                    ck.filled(ins, step)

                def turn(ck, step, src, ident_, dt=F32):
                    bank = ck.bank(step)[:] if dt == F32 else ck.bank(step)[:].bitcast(BF16)
                    ck.wait_bank_free(step)
                    for f in range(FC):
                        for t in range(QT):
                            ins = pe.transpose(bank[:, f * S + t * P:f * S + (t + 1) * P],
                                               src[:, t, f * P:(f + 1) * P], ident_)
                    ck.filled(ins, step)

                def weighted_values(ck, att, s, h):
                    ck.wait("probs_ready", ("core", att, s, h))
                    if h == 0:
                        ck.wait("out_taken", ("norm", att, s), behind=1)
                        ck.wait("v_ready", ("v", att, s))
                    tiles = key_tiles(att)
                    for t in range(QT):
                        for i, (k, n) in enumerate(tiles):
                            ins = pe.matmul(po[t][:, h * VW:(h + 1) * VW], pr[h % 2][0:n, i, t * P:(t + 1) * P],
                                            vv[s][0:n, i, h, :], start=(i == 0), stop=(i == len(tiles) - 1))
                    if h == H - 1:
                        ck.tell(ins, "out_ready", ("core", att, s, H))

                def do(ck, step):
                    kind, att, s = step[:3]
                    if kind in ("q", "k", "v"):
                        if att == "A1":
                            src = x0T[s]
                            if kind == "q":
                                ck.iteration(inputs_loaded[s], 3, 48)
                        elif att == "A2" and kind != "q":
                            src = ctxT[s]
                        else:
                            src = xT
                            before = {"A2": ("xT", "A1", s), "A3": ("xT", "F", s), "A4": ("xT", "E", s)}[att]
                            if kind == "q":
                                ck.wait("xT_ready", before)
                        weight = w[f"{att}_w{kind}"]
                        if kind == "v" or att == "A3" or (att == "A4" and kind == "q"):
                            tiles = key_tiles(att) if kind != "q" else [(0, P), (P, P)]
                            tokens(ck, step, weight, src, tiles)
                        else:
                            features(ck, step, weight, src, S if kind == "q" else KEYS[att])
                    elif kind == "qT":
                        ck.wait("rotated", ("rot", att, s))
                        turn(ck, step, qr[:, 0], ident[:])
                    elif kind == "kT":
                        turn(ck, step, qr[:, 1], ident[:])
                    elif kind == "max":
                        h = step[3]
                        c, p0, e = place(h)
                        n = KEYS[att]
                        if h == 0:
                            q_step = ("q", att, s) if att in ("A1", "A2") else ("qT", att, s)
                            k_step = ("kT", att, s) if att == "A3" else ("k", att, s)
                            ck.wait("qb_ready", q_step)
                            ck.wait("k_ready", k_step)
                        ck.wait("max_done", step, behind=2)
                        bank = sm[counts.at["max_scores", step] % 2]
                        for t in range(QT):
                            ins = pe.matmul(bank[:, t * S:t * S + n], qb[e][p0:p0 + 32, c, t * P:(t + 1) * P],
                                            kb[p0:p0 + 32, c, 0:n], start=True, stop=True)
                        ck.tell(ins, "max_scores", step)
                    elif kind == "shift":
                        e = step[3]
                        if e == 0:
                            ck.wait("max_done", ("max", att, s, H - 1))
                        ck.wait_bank_free(step)
                        for c in range(FC):
                            for t in range(QT):
                                ins = pe.transpose(ck.bank(step)[:, c * S + t * P:c * S + (t + 1) * P],
                                                   mp[:, t, e, c, :], ident[:])
                        ck.filled(ins, step)
                    elif kind == "core":
                        h = step[3]
                        if h < H:
                            c, p0, e = place(h)
                            if h == 0:
                                ck.wait("q_shifted", ("shift", att, s, 1))
                            bank = st[h % 2]
                            for i, (k, n) in enumerate(key_tiles(att)):
                                ins = pe.matmul(bank[0:n, i * S:(i + 1) * S], ke[s][e][p0:p0 + 32, c, k:k + n],
                                                qe[s][e][p0:p0 + 32, c, :], start=True, stop=True)
                            ck.tell(ins, "scores_ready", step)
                        if h > 0:
                            weighted_values(ck, att, s, h - 1)
                    elif kind == "oT":
                        ck.wait("out_taken", ("norm", att, s))
                        turn(ck, step, at[:], ident[:])
                    elif kind == "oproj":
                        if att != "A4":
                            ck.wait("attnT_ready", ("oT", att, s))
                        tokens(ck, step, w[f"{att}_wo"], atT, [(0, P), (P, P)])
                    elif kind == "xT":
                        ck.wait("x_ready", ("ln", att, s))
                        turn(ck, step, x[s][:], ident[:])
                    elif kind == "xqT":
                        ck.wait("xq_ready", ("fq", att, s))
                        turn(ck, step, xq[:], ident_b[:], BF16)
                    elif kind == "gu":
                        t, half = step[3:]
                        if (t, half) == (0, 0):
                            ck.wait("xqT_ready", ("xqT", att, s))
                        for name, wt_ in (("gate", wg), ("up", wu)):
                            use = step + (name,)
                            ck.wait_bank_free(use)
                            for f in range(FC):
                                ins = pe.matmul(ck.bank(use)[:], xqT[:, f, t * P:(t + 1) * P],
                                                wt_[:, f, half * HALF:(half + 1) * HALF],
                                                start=(f == 0), stop=(f == FC - 1))
                            ck.filled(ins, use)
                    elif kind == "hT":
                        t = step[3]
                        ck.wait("hq_ready", ("hq", att, s, t))
                        bank = ck.bank(step)[:].bitcast(BF16)
                        ck.wait_bank_free(step)
                        for j in range(HC):
                            ins = pe.transpose(bank[:, j * P:(j + 1) * P], hq[:, j * P:(j + 1) * P], ident_b[:])
                        ck.filled(ins, step)
                    elif kind == "down":
                        ck.wait("hqT_ready", ("hT", att, s, QT - 1))
                        ck.wait_bank_free(step)
                        for t in range(QT):
                            for j in range(HC):
                                ins = pe.matmul(ck.bank(step)[:, t * D:(t + 1) * D], hqT[t][:, j, :], wd[:, j, :],
                                                start=(j == 0), stop=(j == HC - 1))
                        ck.filled(ins, step)
                    elif kind == "dist":
                        ck.wait("xT_ready", ("xT", att, s))
                        ck.wait("squares_ready", step)
                        ck.wait_bank_free(step)
                        for i in range(3):
                            for f in range(FC):
                                lhs = (ctxT[s][:, f, :], neg_half[:, 0:C], csq[:, f, :])[i]
                                rhs = (xT[:, f, :], xsq[:, f, :], neg_half[:])[i]
                                ins = pe.matmul(ck.bank(step)[0:C, 0:S], lhs, rhs,
                                                start=(i == 0 and f == 0), stop=(i == 2 and f == FC - 1))
                        ck.filled(ins, step)
                    elif kind == "expand":
                        ck.iteration(inputs_loaded[s], 3, 48)
                        ck.wait_bank_free(step)
                        for t in range(QT):
                            ins = pe.matmul(ck.bank(step)[:, t * D:(t + 1) * D], path[s][:, t * P:(t + 1) * P],
                                            ctx[s][:], start=True, stop=True)
                        ck.filled(ins, step)
                    elif kind == "gate":
                        ck.wait("attnT_ready", ("oT", att, s))
                        ck.wait_bank_free(step)
                        for t in range(QT):
                            for f in range(FC):
                                ins = pe.matmul(ck.bank(step)[:, t * (H + 1):(t + 1) * (H + 1)],
                                                atT[:, f, t * P:(t + 1) * P], gate_w[:, f, :],
                                                start=(f == 0), stop=(f == FC - 1))
                        ck.filled(ins, step)

                with pe.Fori(0, iters) as it:
                    ck = Clock(pe, it)
                    for step in order:
                        do(ck, step)

            @block.scalar
            def _(act):
                def put_queries(ck, step, att):
                    use = step
                    ck.wait_bank_full(use)
                    bank = ck.bank(use)[:].rearrange("p (c n) -> p c n", c=FC)
                    if att == "A2":
                        for c in range(FC):
                            ins = act.activation(qf[:, c, :], bank[:, c, :], ACT.Identity, bias=col["A2_bq"][:, c:c + 1])
                    else:
                        ins = act.activation(qf[:], bank, ACT.Copy)
                    ck.tell(ins, "q_ready", step)

                def put_keys(ck, step, att):
                    ck.wait_bank_full(step)
                    n = KEYS[att]
                    bank = ck.bank(step)[:].rearrange("p (c n) -> p c n", c=FC)
                    if att in ("A1", "A3"):
                        act.activation(kb[:], bank, ACT.Copy)
                        for e in range(2):
                            ins = act.activation(ke[step[2]][e][:], bank, ACT.Identity, scale=mask_col(e),
                                                 bias=mask_col(2 + e))
                    else:
                        for c in range(FC):
                            act.activation(kb[:, c, 0:n], bank[:, c, 0:n], ACT.Identity,
                                           bias=col[att + "_bk"][:, c:c + 1])
                            for e in range(2):
                                ins = act.activation(ke[step[2]][e][:, c, 0:n], bank[:, c, 0:n], ACT.Identity,
                                                     scale=mask_col(e), bias=kbias[att][:, e, c:c + 1])
                    ck.tell(ins, "k_ready", step)

                def do(ck, step):
                    kind, att, s = step[:3]
                    if kind == "q" and att in ("A1", "A2") or kind == "qT":
                        put_queries(ck, step, att)
                    elif kind == "k" and att != "A3" or kind == "kT":
                        put_keys(ck, step, att)
                    elif kind == "core" and step[3] < H:
                        h = step[3]
                        ck.wait("scores_ready", step)
                        tiles = key_tiles(att)
                        n = tiles[0][1]
                        width = len(tiles) * S
                        ins = act.activation(pr[h % 2][0:n].rearrange("p a b -> p (a b)")[:, 0:width],
                                             st[h % 2][0:n, 0:width], ACT.Exp, scale=HD ** -0.5)
                        ck.tell(ins, "probs_ready", step)
                    elif kind in ("xT", "oT"):
                        dst, name = (xT, "xT_ready") if kind == "xT" else (atT, "attnT_ready")
                        ck.wait_bank_full(step)
                        ins = act.activation(dst[:].rearrange("p a b -> p (a b)"), ck.bank(step)[:], ACT.Copy)
                        ck.tell(ins, name, step)
                    elif kind == "xqT":
                        ck.wait_bank_full(step)
                        ins = act.activation(xqT[:].rearrange("p a b -> p (a b)"),
                                             ck.bank(step)[:].bitcast(BF16)[:, 0:FC * S], ACT.Copy)
                        ck.tell(ins, "xqT_ready", step)
                    elif kind == "gu":
                        t, half = step[3:]
                        use = step + ("gate",)
                        ck.wait_bank_full(use)
                        ins = act.activation(th[:, half, :], ck.bank(use)[:], ACT.Tanh, scale=qsc[:, t, 4:5])
                        ck.tell(ins, "tanh_ready", step)
                    elif kind == "hT":
                        t = step[3]
                        ck.wait_bank_full(step)
                        ins = act.activation(hqT[t][:].rearrange("p a b -> p (a b)"),
                                             ck.bank(step)[:].bitcast(BF16), ACT.Copy)
                        ck.tell(ins, "hqT_ready", step)
                    elif kind == "gate":
                        ck.wait("logits_ready", step)
                        ins = act.activation(ex[:], lg[:], ACT.Exp)
                        ck.tell(ins, "exps_ready", step)
                    else:
                        return

                with act.Fori(0, iters) as it:
                    ck = Clock(act, it)
                    for step in order:
                        do(ck, step)

            @block.gpsimd
            def _(pool):
                def link(ck, ins):
                    ck.chain += 1
                    ins.then_inc(pool_step, 1)
                    pool.wait_ge(pool_step, ck.it * CHAIN[phase]["pool"] + (base["pool"] + ck.chain))

                def do(ck, step):
                    kind, att, s = step[:3]
                    if kind == "q" and att in ("A1", "A2") or kind == "qT":
                        ck.wait("q_ready", step)
                        alone(pool)
                        for e in range(2):
                            ins = pool.tensor_scalar(qb[e][:], qf[:], mask_col(e), None, ALU.mult)
                        ck.tell(ins, "qb_ready", step)
                    elif kind == "rot" and att == "A3":
                        for i, name in enumerate("qk"):
                            ck.wait("q_tokens", (name, att, s))
                            src = qk[:, i].rearrange("p t (h d) -> p t h d", h=H)
                            dst = qr[:, i].rearrange("p t (h d) -> p t h d", h=H)
                            tmp = r2[:].rearrange("p t (h d) -> p t h d", h=H)
                            cos = rope_cos[:].unsqueeze(2).to_broadcast([P, QT, H, HD])
                            sin = rope_sin[:].unsqueeze(2).to_broadcast([P, QT, H, HD])
                            pool.tensor_tensor(dst, src, cos, ALU.mult)
                            pool.tensor_tensor(tmp[:, :, :, 0::2], src[:, :, :, 1::2], sin[:, :, :, 0::2], ALU.mult)
                            link(ck, pool.tensor_tensor(tmp[:, :, :, 1::2], src[:, :, :, 0::2], sin[:, :, :, 1::2],
                                                        ALU.mult))
                            ins = pool.tensor_tensor(dst, dst, tmp, ALU.add)
                            if i == 0:
                                link(ck, ins)
                        ck.tell(ins, "rotated", step)
                    elif kind == "rot" and att == "A4":
                        ck.wait("q_tokens", ("q", att, s))
                        src = qk[:, 0].rearrange("p t (h d) -> p (t h) d", h=H)
                        dst = qr[:, 0].rearrange("p t (h d) -> p (t h) d", h=H)
                        ck.tell(pool.tensor_tensor(sq[:], src, src, ALU.mult), "squared", step)
                        ck.wait("norms2", step)
                        link(ck, pool.tensor_tensor(nrm[:, 1].rearrange("p t h -> p (t h)"),
                                                    nrm[:, 0].rearrange("p t h -> p (t h)"), power[:], ALU.pow))
                        link(ck, pool.tensor_tensor(nrm[:, 0], nrm[:, 1],
                                                    temp_sp[:].unsqueeze(1).to_broadcast([P, QT, H]), ALU.mult))
                        link(ck, pool.tensor_tensor(
                            dst, src, nrm[:, 0].rearrange("p t h -> p (t h)").unsqueeze(2)
                            .to_broadcast([P, QT * H, HD]), ALU.mult))
                        qr4 = qr[:, 0].rearrange("p t (h d) -> p t (h d)", h=H)
                        emb = qe_sp[:].rearrange("p h d -> p (h d)").unsqueeze(1).to_broadcast([P, QT, D])
                        ck.tell(pool.tensor_tensor(qr4, qr4, emb, ALU.add), "rotated", step)
                    elif kind == "ln":
                        ck.wait("var_ready", step)
                        alone(pool)
                        link(ck, pool.tensor_scalar(ve[:, :, 0:1], mv[:, :, 1:2], EPS, None, ALU.add))
                        ck.tell(pool.tensor_tensor(rstd[:, :, 0:1], ve[:, :, 0:1],
                                                     power[:, 0:QT].unsqueeze(2), ALU.pow), "rstd_ready", step)
                    elif kind == "dist":
                        ck.wait("xT_ready", ("xT", att, s))
                        pool.tensor_tensor(xsq[:], xT[:], xT[:], ALU.mult)
                        ck.tell(pool.tensor_tensor(csq[:], ctxT[s][:], ctxT[s][:], ALU.mult),
                                  "squares_ready", step)

                with pool.Fori(0, iters) as it:
                    ck = Clock(pool, it)
                    for step in order:
                        do(ck, step)
                    assert ck.chain == CHAIN[phase]["pool"], ("pool", phase, ck.chain)

            @block.vector
            def _(dve):
                def link(ck, ins):
                    ck.chain += 1
                    ins.then_inc(dve_step, 1)
                    dve.wait_ge(dve_step, ck.it * CHAIN[phase]["dve"] + (base["dve"] + ck.chain))

                def do(ck, step):
                    kind, att, s = step[:3]
                    if kind in ("q", "k") and att == "A3" or kind == "q" and att == "A4":
                        i = "qk".index(kind)
                        ck.wait_bank_full(step)
                        bias = row[f"{att}_b{kind}"][:].unsqueeze(1).to_broadcast([P, QT, D])
                        ins = dve.tensor_tensor(qk[:, i], ck.bank(step)[:].rearrange("p (t d) -> p t d", t=QT),
                                                bias, ALU.add)
                        ck.tell(ins, "q_tokens", step)
                    elif kind == "rot" and att == "A4":
                        ck.wait("squared", step)
                        ck.tell(dve.tensor_reduce(nrm[:, 0].rearrange("p t h -> p (t h)"), sq[:], AX.X, ALU.add),
                                  "norms2", step)
                    elif kind == "v":
                        ck.wait_bank_full(step)
                        tiles = key_tiles(att)
                        n, nt = tiles[0][1], len(tiles)
                        src = ck.bank(step)[0:n, 0:nt * D].rearrange("p (t h d) -> p t h d", t=nt, h=H)
                        for t in range(nt):
                            dst = vv[s][0:n, t, :, 0:HD]
                            if att == "A1":
                                ins = dve.tensor_copy(dst, src[:, t])
                            else:
                                bias = row[att + "_bv"][0:n].rearrange("p (h d) -> p h d", h=H)
                                ins = dve.tensor_tensor(dst, src[:, t], bias, ALU.add)
                        ck.tell(ins, "v_ready", step)
                    elif kind == "max":
                        h = step[3]
                        c, p0, e = place(h)
                        ck.wait("max_scores", step)
                        bank = sm[counts.at["max_scores", step] % 2]
                        at_row = p0 + 16 * (1 - e)
                        ins = dve.tensor_reduce(mp[:, :, e, c, at_row:at_row + 1],
                                                bank[:].rearrange("p (t n) -> p t n", t=QT)[:, :, 0:KEYS[att]],
                                                AX.X, ALU.max, negate=True)
                        ck.tell(ins, "max_done", step)
                    elif kind == "shift":
                        e = step[3]
                        ck.wait_bank_full(step)
                        ins = dve.scalar_tensor_tensor(
                            out=qe[s][e][:].rearrange("p c n -> p (c n)"), in0=qf[:].rearrange("p c n -> p (c n)"),
                            scalar=mask_col(e), in1=ck.bank(step)[:], op0=ALU.mult, op1=ALU.add)
                        ck.tell(ins, "q_shifted", step)
                    elif kind == "norm":
                        ck.wait("out_ready", ("core", att, s, H))
                        for t in range(QT):
                            o = po[t][:, 0:H * VW].rearrange("p (h w) -> p h w", h=H)
                            ins = dve.reciprocal(rc[:, t, :].unsqueeze(2), o[:, :, HD:VW])
                        link(ck, ins)
                        for t in range(QT):
                            o = po[t][:, 0:H * VW].rearrange("p (h w) -> p h w", h=H)
                            ins = dve.tensor_tensor(at[:, t].rearrange("p (h d) -> p h d", h=H), o[:, :, 0:HD],
                                                    rc[:, t, :].unsqueeze(2).to_broadcast([P, H, HD]), ALU.mult)
                        ck.tell(ins, "out_taken", step)
                        if att == "A1":
                            ck.wait("out_taken", step)
                            ck.tell(dve.tensor_tensor(res[:], x0[s][:], at[:], ALU.add), "x_used", step)
                    elif kind == "oproj":
                        ck.wait_bank_full(step)
                        bank = ck.bank(step)[:].rearrange("p (t d) -> p t d", t=QT)
                        bias = row[att + "_bo"][:].unsqueeze(1).to_broadcast([P, QT, D])
                        if att == "A4":
                            for t in range(QT):
                                ins = dve.scalar_tensor_tensor(out=at[:, t], in0=bank[:, t], scalar=gs[:, 15, t:t + 1],
                                                               in1=row["A4_bo"][:], op0=ALU.mult, op1=ALU.add)
                        else:
                            ins = dve.tensor_tensor(at[:], bank, bias, ALU.add)
                        ck.tell(ins, "proj_taken", step)
                        ck.wait("proj_taken", step)
                        link(ck, dve.tensor_tensor(res[:], at[:], x[s][:], ALU.add))
                    elif kind == "expand":
                        ck.wait_bank_full(step)
                        ck.wait("x_ready", ("ln", "E", s), behind=1)
                        ins = dve.tensor_tensor(res[:], ck.bank(step)[:].rearrange("p (t d) -> p t d", t=QT),
                                                x0[s][:], ALU.add)
                        ck.tell(ins, "x4_used", step)
                    elif kind == "down":
                        ck.wait_bank_full(step)
                        bank = ck.bank(step)[:].rearrange("p (t d) -> p t d", t=QT)
                        for t in range(QT):
                            ins = dve.scalar_tensor_tensor(out=res[:, t], in0=bank[:, t], scalar=qsc[:, t, 10:11],
                                                           in1=x[s][:, t], op0=ALU.mult, op1=ALU.add)
                        ck.tell(ins, "down_taken", step)
                        ck.wait("down_taken", step)
                    elif kind == "ln":
                        if att == "A1":
                            ck.wait("x_used", ("norm", att, s))
                        if att == "E":
                            ck.wait("x4_used", ("expand", att, s))
                        for t in range(QT):
                            ins = dve.bn_stats(stats[:, t, :], res[:, t, :])
                        link(ck, ins)
                        alone(dve)
                        for t in range(QT):
                            ins = dve.bn_aggr(mv[:, t, :], stats[:, t, :])
                        ck.tell(ins, "var_ready", step)
                        ck.wait("rstd_ready", step)
                        if att == "A1":
                            ck.iteration(x4_stored[s], 1, 16)
                        if att == "E":
                            ck.iteration(out_stored[s], 1, 16)
                        for t in range(QT):
                            ins = dve.tensor_scalar(x[s][:, t], res[:, t], mv[:, t, 0:1], rstd[:, t, 0:1],
                                                    ALU.subtract, ALU.mult)
                        ck.tell(ins, "x_ready", step)
                    elif kind == "fq":
                        ck.wait("x_ready", ("ln", "A2", s))
                        link(ck, dve.tensor_reduce(qsc[:, :, 0:1], x[s][:], AX.X, ALU.max, apply_absolute_value=True))
                        link(ck, dve.tensor_scalar(qsc[:, :, 1:2], qsc[:, :, 0:1], EPS, None, ALU.max))
                        link(ck, dve.reciprocal(qsc[:, :, 2:3], qsc[:, :, 1:2]))
                        link(ck, dve.tensor_scalar(qsc[:, :, 3:4], qsc[:, :, 2:3], QMAX, None, ALU.mult))
                        for t in range(QT):
                            ins = dve.tensor_scalar(xq_f[:, t], x[s][:, t], qsc[:, t, 3:4], MAGIC, ALU.mult, ALU.add)
                        link(ck, ins)
                        link(ck, dve.tensor_scalar(xq[:], xq_f[:], MAGIC, QMAX, ALU.subtract, ALU.min))
                        link(ck, dve.tensor_scalar(qsc[:, :, 4:5], qsc[:, :, 1:2], wq_inv[:, 0:1], 0.5 / QMAX,
                                                   ALU.mult, ALU.mult))
                        link(ck, dve.tensor_scalar(qsc[:, :, 5:6], qsc[:, :, 1:2], wq_inv[:, 1:2], 1.0 / QMAX,
                                                   ALU.mult, ALU.mult))
                        ck.tell(dve.tensor_tensor(qsc[:, :, 6:7], qsc[:, :, 4:5], qsc[:, :, 5:6], ALU.mult),
                                  "xq_ready", step)
                    elif kind == "gu":
                        t, half = step[3:]
                        g, u = step + ("gate",), step + ("up",)
                        ck.wait("tanh_ready", step)
                        ins = dve.scalar_tensor_tensor(out=hid[:, half], in0=th[:, half], scalar=1.0,
                                                       in1=ck.bank(g)[:], op0=ALU.add, op1=ALU.mult)
                        ck.tell(ins, "gated", step)
                        ck.wait("gated", step)
                        ck.wait_bank_full(u)
                        ins = dve.tensor_tensor(hid[:, half], hid[:, half], ck.bank(u)[:], ALU.mult)
                        ck.tell(ins, "hid_ready", step)
                    elif kind == "hq":
                        t = step[3]
                        q = qsc[:, t]
                        ck.wait("hid_ready", ("gu", att, s, t, 1))
                        flat = hid[:].rearrange("p a b -> p (a b)")
                        link(ck, dve.tensor_reduce(q[:, 7:8], flat, AX.X, ALU.max, apply_absolute_value=True))
                        link(ck, dve.tensor_scalar(q[:, 8:9], q[:, 7:8], q[:, 6:7], EPS, ALU.mult, ALU.max))
                        link(ck, dve.reciprocal(q[:, 9:10], q[:, 8:9]))
                        link(ck, dve.tensor_scalar(q[:, 11:12], q[:, 9:10], q[:, 6:7], QMAX, ALU.mult, ALU.mult))
                        link(ck, dve.tensor_scalar(q[:, 10:11], q[:, 8:9], wq_inv[:, 2:3], 1.0 / QMAX,
                                                   ALU.mult, ALU.mult))
                        link(ck, dve.tensor_scalar(flat, flat, q[:, 11:12], MAGIC, ALU.mult, ALU.add))
                        if t > 0:
                            ck.wait("hqT_ready", ("hT", att, s, t - 1))
                        ck.tell(dve.tensor_scalar(hq[:], flat, MAGIC, QMAX, ALU.subtract, ALU.min), "hq_ready", step)
                        ck.wait("hq_ready", step)
                    elif kind == "dist":
                        ck.wait_bank_full(step)
                        dve.wait_ge(dist_stored, it_dist(ck, s))
                        ins = dve.tensor_scalar(dist[:], ck.bank(step)[0:C, 0:S], -2.0, 0.0, ALU.mult, ALU.max)
                        ck.tell(ins, "dist_ready", step)
                    elif kind == "gate":
                        ck.wait_bank_full(step)
                        src = ck.bank(step)[:, 0:QT * (H + 1)].rearrange("p (t n) -> p t n", t=QT)
                        ins = (dve.tensor_tensor(lg[:], src, gate_b[:].unsqueeze(1).to_broadcast([P, QT, H + 1]),
                                                 ALU.add))
                        ck.tell(ins, "logits_taken", step)
                        ck.wait("logits_taken", step)
                        nr = H - 1
                        dve.tensor_reduce(gs[:, 0, :].unsqueeze(2), lg[:, :, 0:nr], AX.X, ALU.max)
                        link(ck, dve.tensor_reduce(gs[:, 1, :].unsqueeze(2), lg[:, :, nr:H + 1], AX.X, ALU.max))
                        dve.tensor_tensor(lg[:, :, 0:nr], lg[:, :, 0:nr],
                                          gs[:, 0, :].unsqueeze(2).to_broadcast([P, QT, nr]), ALU.subtract)
                        ck.tell(dve.tensor_tensor(lg[:, :, nr:H + 1], lg[:, :, nr:H + 1],
                                                    gs[:, 1, :].unsqueeze(2).to_broadcast([P, QT, 2]), ALU.subtract),
                                  "logits_ready", step)
                        ck.wait("exps_ready", step)
                        alone(dve)
                        for t in range(QT):
                            dve.max(top[:, t, :], ex[:, t, 0:nr])
                        dve.tensor_reduce(gs[:, 2, :].unsqueeze(2), ex[:, :, 0:nr], AX.X, ALU.add)
                        link(ck, dve.tensor_reduce(gs[:, 3, :].unsqueeze(2), ex[:, :, nr:H + 1], AX.X, ALU.add))
                        dve.tensor_reduce(gs[:, 4, :].unsqueeze(2), top[:, :, 0:ROUTED], AX.X, ALU.add)
                        dve.reciprocal(gs[:, 5, :], gs[:, 2, :])
                        link(ck, dve.reciprocal(gs[:, 6, :], gs[:, 3, :]))
                        e0, e1 = (ex[:, :, nr + i:nr + i + 1].rearrange("p t o -> p (t o)") for i in range(2))
                        dve.tensor_tensor(gs[:, 7, :], e0, gs[:, 6, :], ALU.mult)
                        dve.tensor_tensor(gs[:, 8, :], e1, gs[:, 6, :], ALU.mult)
                        link(ck, dve.tensor_tensor(gs[:, 9, :], gs[:, 4, :], gs[:, 5, :], ALU.mult))
                        dve.tensor_tensor(gs[:, 10, :], gs[:, 7, :], gs[:, 8, :], ALU.add)
                        link(ck, dve.tensor_tensor(gs[:, 11, :], gs[:, 8, :], gs[:, 9, :], ALU.mult))
                        dve.tensor_scalar(gs[:, 12, :], gs[:, 11, :], 2.0 * ROUTED, None, ALU.mult)
                        link(ck, dve.tensor_tensor(gs[:, 13, :], gs[:, 7, :], gs[:, 10, :], ALU.mult))
                        link(ck, dve.tensor_scalar(gs[:, 14, :], gs[:, 13, :], 2.0, None, ALU.mult))
                        link(ck, dve.tensor_tensor(gs[:, 15, :], gs[:, 14, :], gs[:, 12, :], ALU.add))

                def it_dist(ck, s):
                    return ck.it * 32 + (16 + 16 * s)

                dve.memset(mp[:], 0.0).then_inc(setup_dve, 1)
                for s in range(2):
                    dve.memset(vv[s][:, :, :, HD:VW], 1.0).then_inc(setup_dve, 1)
                dve.wait_ge(setup_dve, base["setup"] + 3)
                with dve.Fori(0, iters) as it:
                    ck = Clock(dve, it)
                    for step in order:
                        do(ck, step)
                    assert ck.chain == CHAIN[phase]["dve"], ("dve", phase, ck.chain)

        base = {x: 0 for x in SIGNALS}
        base.update(bank=0, dve=0, pool=0, setup=SETUP_STEPS)

        def prime(counts, stored):
            with nc.Block() as start:
                @start.sync
                def _(sp):
                    for x in SIGNALS:
                        if counts.per[x]:
                            sp.sem_inc(sems[x], counts.per[x])
                    for x in stored:
                        sp.sem_inc(x, 16)

        prime(COUNTS_A, x4_stored + [dist_stored])
        with ExitStack() as where:
            run("A", where, COUNTS_A, base)
        for x in SIGNALS:
            base[x] += COUNTS_A.per[x] * (iters + 1)
        base["bank"] += COUNTS_A.bank_per * iters
        base["dve"] += CHAIN["A"]["dve"] * iters
        base["pool"] += CHAIN["A"]["pool"] * iters
        base["setup"] += 3

        with ExitStack() as where:
            cost = sb("cost", [nb, C + 1, S + 1], F32, where)
            low = sb("low", [nb, S], F32, where)
            left = sb("left", [nb, S + 1], F32, where)
            diag = sb("diag", [nb, S], F32, where)
            on = sb("on", [nb, S], F32, where)
            enter = sb("enter", [nb, S], F32, where)
            leave = sb("leave", [nb, S], F32, where)
            leave_diag = sb("leave_diag", [nb, S + 1], F32, where)
            leave_up = sb("leave_up", [nb, S], F32, where)
            block = where.enter_context(nc.Block())
            ROWS = 7
            CHUNKS = C // ROWS

            def rows(first, n=1):
                return cost[:, bass.ds(first, n), :]

            @block.sync
            def _(sp):
                for c in range(CHUNKS):
                    if c >= 2:
                        sp.wait_ge(roots_ready, c - 1)
                    sp.dma_start(cost[:, 1 + c * ROWS:1 + (c + 1) * ROWS, 1:S + 1],
                                 dist_dram[:, c * ROWS:(c + 1) * ROWS, :]).then_inc(dist_loaded[c % 2], 16)
                for c in reversed(range(CHUNKS)):
                    sp.wait_ge(path_ready, ROWS * (CHUNKS - c) + 1)
                    sp.dma_start(path_dram[:, c * ROWS:(c + 1) * ROWS, :],
                                 cost[:, 1 + c * ROWS:1 + (c + 1) * ROWS, 1:S + 1]).then_inc(path_stored, 16)
                sp.wait_ge(path_stored, 16 * CHUNKS)

            @block.scalar
            def _(act):
                for c in range(CHUNKS):
                    act.wait_ge(dist_loaded[c % 2], 16 * (c // 2 + 1))
                    part = cost[:, 1 + c * ROWS:1 + (c + 1) * ROWS, 1:S + 1]
                    act.activation(part, part, ACT.Sqrt).then_inc(roots_ready, 1)
                act.sem_inc(path_ready, 1)
                with act.Fori(0, CHUNKS) as c:
                    for u in range(ROWS):
                        here = rows(c * (-ROWS) + (C - u))
                        act.wait_ge(on_ready, c * ROWS + (u + 1))
                        act.activation(flat(here[:, :, 1:S + 1]), on[:], ACT.Copy).then_inc(path_ready, 1)

            @block.vector
            def _(dve):
                dve.memset(cost[:, 0, :], BIG).then_inc(dtw_step, 1)
                dve.memset(cost[:, 1:C + 1, 0:1], BIG).then_inc(dtw_step, 1)
                dve.memset(left[:, S:S + 1], 0.0).then_inc(dtw_step, 1)
                dve.memset(leave_diag[:, S:S + 1], 0.0).then_inc(dtw_step, 1)
                dve.memset(enter[:], 0.0).then_inc(dtw_step, 1)
                dve.wait_ge(dtw_step, 5)
                dve.memset(enter[:, S - 1:S], 1.0).then_inc(dtw_step, 1)
                dve.memset(cost[:, 0, 0:1], 0.0).then_inc(dtw_step, 1)
                dve.wait_ge(dtw_step, 7)
                with dve.Fori(0, CHUNKS) as c:
                    dve.wait_ge(roots_ready, c + 1)
                    for u in range(ROWS):
                        above, here = rows(c * ROWS + u), rows(c * ROWS + (u + 1))
                        n = c * (2 * ROWS) + (7 + 2 * u)
                        dve.tensor_tensor(low[:], flat(above[:, :, 0:S]), flat(above[:, :, 1:S + 1]),
                                          ALU.min).then_inc(dtw_step, 1)
                        dve.wait_ge(dtw_step, n + 1)
                        dve.tensor_tensor_scan(flat(here[:, :, 1:S + 1]), low[:], flat(here[:, :, 1:S + 1]), BIG,
                                               ALU.min, ALU.add).then_inc(dtw_step, 1)
                        dve.wait_ge(dtw_step, n + 2)
                first = 7 + 2 * C
                with dve.Fori(0, CHUNKS) as c:
                    for u in range(ROWS):
                        i = c * (-ROWS) + (C - 1 - u)
                        above, here = rows(i), rows(i + 1)
                        n = c * (6 * ROWS) + (first + 6 * u)
                        up, dg = flat(above[:, :, 1:S + 1]), flat(above[:, :, 0:S])
                        dve.tensor_tensor(diag[:], dg, up, ALU.is_le)
                        dve.tensor_tensor(low[:], dg, up, ALU.min).then_inc(dtw_step, 1)
                        dve.wait_ge(dtw_step, n + 1)
                        dve.tensor_tensor(left[:, 0:S], flat(here[:, :, 0:S]), low[:], ALU.is_lt).then_inc(dtw_step, 1)
                        dve.wait_ge(dtw_step, n + 2)
                        dve.wait_ge(path_ready, c * ROWS + (u + 1))
                        dve.tensor_tensor_scan(on[:, ::-1], left[:, S:0:-1], enter[:, ::-1], 0.0,
                                               ALU.mult, ALU.add).then_inc(on_ready, 1)
                        dve.wait_ge(on_ready, c * ROWS + (u + 1))
                        dve.tensor_tensor(leave[:], on[:], left[:, 0:S], ALU.is_gt).then_inc(dtw_step, 1)
                        dve.wait_ge(dtw_step, n + 3)
                        dve.tensor_tensor(leave_diag[:, 0:S], leave[:], diag[:], ALU.mult).then_inc(dtw_step, 1)
                        dve.wait_ge(dtw_step, n + 4)
                        dve.tensor_tensor(leave_up[:], leave[:], leave_diag[:, 0:S], ALU.subtract).then_inc(dtw_step, 1)
                        dve.wait_ge(dtw_step, n + 5)
                        dve.tensor_tensor(enter[:], leave_up[:], leave_diag[:, 1:S + 1], ALU.add).then_inc(dtw_step, 1)
                        dve.wait_ge(dtw_step, n + 6)

        prime(COUNTS_C, out_stored)
        with ExitStack() as where:
            run("C", where, COUNTS_C, base)


def flat(ap):
    return ap.rearrange("p o n -> p (o n)")


SETUP_STEPS = 23



def chunked(wt):
    k, n = wt.shape
    return wt.reshape(k // P, P, n).transpose(1, 0, 2).reshape(P, k // P * n)


def layouts(a):
    nb = a["x"].shape[0]
    g = {}
    g["x"] = a["x"].reshape(nb, QT, P, D).transpose(0, 2, 1, 3).reshape(nb, P, QT * D)
    g["xT"] = a["x"].transpose(0, 2, 1).reshape(nb, FC, P, S).transpose(0, 2, 1, 3).reshape(nb, P, FC * S)
    g["ctxT"] = a["ctx_1024"].transpose(0, 2, 1).reshape(nb, FC, P, C).transpose(0, 2, 1, 3).reshape(nb, P, FC * C)
    g["ctx"] = a["ctx_1024"]
    qkv, qkv_b = a["L1_attn_qkv_w"], a["L1_attn_qkv_b"]
    square = {"A1_wq": a["L0_attn_Wq"], "A1_wk": a["L0_attn_Wk"], "A1_wv": a["L0_attn_Wv"],
              "A2_wq": a["L0_xattn_wq"], "A2_wk": a["L0_xattn_wk"], "A2_wv": a["L0_xattn_wv"],
              "A2_wo": a["L0_xattn_wo"],
              "A3_wq": qkv[0:D], "A3_wk": qkv[D:2 * D], "A3_wv": qkv[2 * D:3 * D], "A3_wo": a["L1_attn_proj_w"],
              "A4_wq": a["L1_ffn_Wq"], "A4_wk": a["L1_ffn_Wk"], "A4_wv": a["L1_ffn_Wv"], "A4_wo": a["L1_ffn_Wp"]}
    for n, m in square.items():
        g[n] = chunked(m.T)
    g.update(w_gate=chunked(a["L0_ffn_w_gate"].T), w_up=chunked(a["L0_ffn_w_up"].T),
             w_down=chunked(a["L0_ffn_w_down"].T))
    for n, b in (("A2_bq", a["L0_xattn_bq"]), ("A2_bk", a["L0_xattn_bk"]), ("A4_bk", a["L1_ffn_bk"])):
        g[n] = b.reshape(FC, P).T
    g.update(A2_bv=a["L0_xattn_bv"], A2_bo=a["L0_xattn_bo"], A3_bq=qkv_b[0:D], A3_bk=qkv_b[D:2 * D],
             A3_bv=qkv_b[2 * D:3 * D], A3_bo=a["L1_attn_proj_b"], A4_bq=a["L1_ffn_bq"], A4_bv=a["L1_ffn_bv"],
             A4_bo=a["L1_ffn_bp"])
    g["gate_w"] = chunked(np.concatenate([a["L1_ffn_Wr"], a["L1_ffn_Ws"]], axis=0).T)
    g["gate_b"] = np.concatenate([a["L1_ffn_br"], a["L1_ffn_bs"]])
    g["temperature"] = a["L1_ffn_temperature"].reshape(H)
    g["query_embedding"] = a["L1_ffn_query_embedding"].reshape(H * HD)
    g["ident"] = np.eye(P, dtype=np.float32)
    r = np.arange(P) % 32
    g["mask"] = np.stack([r < 16, r >= 16, r == 16, r == 0], axis=1).astype(np.float32)
    inv_freq = (1.0 / np.float32(10000.0) ** (np.arange(0, HD, 2, dtype=np.float32) / np.float32(HD))).astype(np.float32)
    freqs = np.arange(S, dtype=np.float32)[:, None] * inv_freq[None, :]
    emb = np.concatenate([freqs, freqs], axis=-1)
    sign = np.where(np.arange(HD) % 2 == 0, -1.0, 1.0).astype(np.float32)
    for n, t in (("rope_cos", np.cos(emb)), ("rope_sin", np.sin(emb) * sign)):
        g[n] = t.astype(np.float32).reshape(QT, P, HD).transpose(1, 0, 2).reshape(P, QT * HD)
    return {n: np.ascontiguousarray(v) for n, v in g.items()}, list(square)


def program(nc, arrays, square, nb):
    io = {n: nc.dram_tensor(f"in_{n}", v.shape, mybir.dt.from_np(v.dtype), kind="ExternalInput").ap()
          for n, v in arrays.items()}
    io["square_weights"] = square
    out = nc.dram_tensor("out_0", (nb, P, QT * D), F32, kind="ExternalOutput").ap()
    build(nc, nb, io, out)


def kernel(**inputs):
    import concourse.bacc as bacc
    from concourse.bass_utils import run_bass_kernel_spmd

    arrays, square = layouts({n: np.asarray(v) for n, v in inputs.items()})
    nb = arrays["x"].shape[0]
    nc = bacc.Bacc("TRN2", target_bir_lowering=False, num_devices=1)
    program(nc, arrays, square, nb)
    r = run_bass_kernel_spmd(nc, [{f"in_{n}": v for n, v in arrays.items()}], core_ids=[0])
    got = r.results[0]["out_0"]
    return got.reshape(nb, P, QT, D).transpose(0, 2, 1, 3).reshape(nb, S, D)
```

```python
from contextlib import ExitStack

import concourse.bass as bass
import numpy as np
from concourse import mybir

ALU = mybir.AluOpType
ACT = mybir.ActivationFunctionType
AX = mybir.AxisListType
F32 = mybir.dt.float32
BF16 = mybir.dt.bfloat16

P = 128
D = 256
S = 256
C = 77
H = 16
HD = D // H
FC = D // P
QT = S // P
HID = 1024
HC = HID // P
HALF = 512
VW = 32
EPS = 1e-5
MAGIC = 1.5 * 2.0 ** 23
QMAX = 127.0
BIG = 3.0e38
ROUTED = 3

KEYS = {"A1": S, "A2": C, "A3": S, "A4": S}
ALL_BIASES = ("A2_bo", "A2_bv", "A3_bq", "A3_bk", "A3_bv", "A3_bo", "A4_bq", "A4_bv", "A4_bo")


def key_tiles(att):
    return [(k, min(P, KEYS[att] - k)) for k in range(0, KEYS[att], P)]


def place(h):
    return h // 8, 32 * (h % 8 // 2), h % 2


HEADS = [8 * c + 2 * r + e for c in range(FC) for e in range(2) for r in range(4)]
PAIRS = H // 2



def before_core(att, s):
    steps = [("q", att, s), ("k", att, s), ("v", att, s)]
    if att == "A3":
        steps += [("rot", att, s), ("qT", att, s), ("kT", att, s)]
    if att == "A4":
        steps += [("rot", att, s), ("qT", att, s)]
    steps += [("max", att, s, i) for i in range(H)]
    return steps + [("shift", att, s, 0), ("shift", att, s, 1)]


def core(att, s):
    return [("core", att, s, p) for p in range(PAIRS + 1)] + [("take", att, s)]


def after_core(att, s):
    steps = [("norm", att, s, 0), ("norm", att, s, 1)]
    if att == "A4":
        steps += [("oT", att, s), ("gate", att, s), ("oproj", att, s)]
    elif att != "A1":
        steps += [("oT", att, s), ("oproj", att, s)]
    return steps + [("ln", att, s)]


def mlp(s):
    f = ("F", s)
    return [("fq",) + f, ("xqT",) + f, ("gu",) + f + (0, 0), ("gu",) + f + (0, 1), ("hq",) + f + (0,),
            ("gu",) + f + (1, 0), ("gu",) + f + (1, 1), ("hT",) + f + (0,), ("hq",) + f + (1,),
            ("hT",) + f + (1,), ("down",) + f, ("ln",) + f]


def entry(phase, s):
    if phase == "A":
        return (before_core("A1", s) + core("A1", s) + after_core("A1", s)
                + [("xT", "A1", s)] + before_core("A2", s) + core("A2", s) + after_core("A2", s) + mlp(s)
                + [("xT", "F", s)] + before_core("A3", s) + core("A3", s) + after_core("A3", s)
                + [("store", "A3", s), ("xT", "A3", s), ("dist", "A3", s), ("store", "D", s)])
    return ([("expand", "E", s), ("ln", "E", s), ("xT", "E", s)] + before_core("A4", s) + core("A4", s)
            + after_core("A4", s) + [("store", "A4", s)])


TIMES = {"q": (1.7, 0), "k": (1.7, 0), "v": (1.7, 0.5), "rot": (0, 5.0), "qT": (0.25, 0.5), "kT": (0.25, 1.5),
         "max": (0.22, 0.45), "shift": (0.25, 0.8), "core": (1.5, 0), "take": (0, 1.2), "norm": (0.25, 0.7),
         "oT": (0.25, 0.7), "oproj": (1.7, 1.6), "gate": (0.1, 0.5), "ln": (0, 3.8), "xT": (0.25, 0.9),
         "fq": (0, 3.0), "xqT": (0.15, 0.7), "gu": (0.85, 1.2), "hq": (0, 2.2), "hT": (0.3, 0.7),
         "down": (0.9, 0.8), "dist": (1.3, 1.0), "expand": (0.9, 0.8), "load": (0, 0), "store": (0, 0)}


def times(step):
    pe, wait = TIMES[step[0]]
    if step[1] == "A2" and step[0] in ("k", "v", "max", "core"):
        pe, wait = pe / 2, wait / 2
    return pe, wait


def merge(first, second):
    queues, ready, clock, owner, out = [list(first), list(second)], [0.0, 0.0], 0.0, None, []
    while queues[0] or queues[1]:
        free = [i for i in range(2) if queues[i] and not
                (queues[i][0][0] in ("core", "take") and owner is not None and owner != i)]
        i = min(free, key=lambda n: (max(ready[n], clock), n))
        step = queues[i].pop(0)
        pe, wait = times(step)
        clock = max(clock, ready[i] if pe else clock) + pe
        ready[i] = max(ready[i], clock if pe else ready[i]) + wait
        out.append(step)
        if step[0] == "core":
            owner = i
        elif step[0] == "take":
            owner = None
    return out, max(clock, max(ready))


def orders(phase):
    even, odd = entry(phase, 0), entry(phase, 1)
    cuts = [n for n in range(1, len(odd)) if odd[n][0] not in ("core", "take", "max", "shift", "store")]
    cut = min(cuts, key=lambda n: merge(even, odd[n:] + odd[:n])[1])
    load_next = [("load", phase, s) for s in range(2)]
    if phase == "A":
        even = even + [load_next[0]]
        late = odd[cut:] + [load_next[1]]
    else:
        even.insert(1, load_next[0])
        late = odd[cut:] + [load_next[1]]
    body, _ = merge(even, late + odd[:cut])
    before = load_next + odd[:cut]
    after, _ = merge([x for x in even if x[0] != "load"], odd[cut:])
    return before, body, after, set(odd[:cut])


def bank_uses(step):
    kind = step[0]
    if kind in ("q", "k", "v", "qT", "kT", "shift", "xT", "oT", "oproj", "xqT", "hT", "down",
                "norm", "dist", "expand", "gate"):
        return [step]
    if kind == "gu":
        return [step + ("gate",), step + ("up",)]
    return []


def signals(step):
    kind, att = step[0], step[1]
    token_q = att in ("A3", "A4")
    queries = ["q_ready"]
    return {
        "q": ["q_tokens"] if token_q else queries,
        "k": ["q_tokens"] if att == "A3" else ["k_ready"],
        "v": ["v_ready"],
        "rot": ["pool_step"] * 3 + ["rotated"] if att == "A3" else ["squared", "norms2"] + ["pool_step"] * 3
        + ["rotated"],
        "qT": queries,
        "kT": ["k_ready"],
        "max": ["max_scores", "max_done"],
        "shift": ["q_shifted"],
        "core": (["scores_ready", "probs_ready"] * 2 if step[-1] < PAIRS else []) + ["weighted"] * (step[-1] != 0),
        "take": ["out_taken"],
        "norm": ["dve_step", "normed"] + ["x_used"] * (att == "A1" and step[-1] == 1),
        "oT": ["attnT_ready"],
        "gate": ["logits_taken", "dve_step", "logits_ready", "exps_ready"] + ["dve_step"] * 7,
        "oproj": ["proj_taken", "dve_step"],
        "ln": ["dve_step", "var_ready", "pool_step", "rstd_ready", "x_ready"],
        "xT": ["xT_ready"],
        "fq": ["dve_step"] * 8 + ["xq_ready"],
        "xqT": ["xqT_ready"],
        "gu": ["tanh_ready", "gated", "hid_ready"],
        "hq": ["dve_step"] * 6 + ["hq_ready"],
        "hT": ["hqT_ready"],
        "down": ["down_taken"],
        "dist": ["squares_ready", "dist_ready"],
        "expand": ["x4_used"],
        "load": [],
        "store": [],
    }[kind]


def emptied_by(use):
    kind, att = use[0], use[1]
    if kind == "gu":
        return "gated" if use[-1] == "gate" else "hid_ready"
    if kind == "q":
        return "q_tokens" if att in ("A3", "A4") else "q_ready"
    if kind == "k":
        return "q_tokens" if att == "A3" else "k_ready"
    return {"v": "v_ready", "qT": "q_ready", "kT": "k_ready", "shift": "q_shifted", "xT": "xT_ready",
            "norm": "normed", "oT": "attnT_ready", "oproj": "proj_taken", "xqT": "xqT_ready",
            "hT": "hqT_ready", "down": "down_taken", "dist": "dist_ready", "expand": "x4_used",
            "gate": "logits_taken"}[kind]


SIGNALS = sorted({x for p in "AC" for step in entry(p, 0) for x in signals(step)})


class Counts:

    def __init__(self, order):
        self.index = {step: n for n, step in enumerate(order)}
        self.at, self.per, self.bank, self.banks = {}, {x: 0 for x in SIGNALS}, {}, [0, 0]
        for step in order:
            seen = {}
            for x in signals(step):
                self.per[x] += 1
                self.at[x, step, seen.get(x, 0)] = self.at[x, step, -1] = self.per[x]
                seen[x] = seen.get(x, 0) + 1
        uses = [(use, step) for step in order for use in bank_uses(step)]
        for n, (use, step) in enumerate(uses):
            self.banks[n % 2] += 1
            self.bank[use] = (n % 2, self.banks[n % 2])
        self.before = {use: (uses[n - 2] if n >= 2 or len(uses) % 2 == 0 else None)
                       for n, (use, _) in enumerate(uses)}


def build(nc, nb, io, out):
    stack = ExitStack()
    with stack:
        def sem(name):
            return stack.enter_context(nc.semaphore(name))

        def sb(name, shape, dt=F32, where=stack):
            return where.enter_context(nc.sbuf_tensor(name, shape, dt))

        sems = {x: sem(x) for x in SIGNALS}
        bank_full = [sem("bank_full0"), sem("bank_full1")]
        consts_loaded, consts_ready = sem("consts_loaded"), sem("consts_ready")
        setup_dve, setup_act, setup_pe, setup_pool = (
            sem("setup_dve"), sem("setup_act"), sem("setup_pe"), sem("setup_pool"))
        inputs_loaded = {p: [sem(f"inputs_loaded_{p}{s}") for s in range(2)] for p in "AC"}
        tokens_stored = {p: [sem(f"tokens_stored_{p}{s}") for s in range(2)] for p in "AC"}
        dist_stored = [sem("dist_stored0"), sem("dist_stored1")]
        dist_loaded = [sem(f"dist_loaded{i}") for i in range(2)]
        roots_ready = sem("roots_ready")
        passed = sem("passed")
        on_ready = sem("on_ready")
        dtw_step, path_ready, path_stored = sem("dtw_step"), sem("path_ready"), sem("path_stored")

        pj = [stack.enter_context(nc.psum_tensor(f"pj{i}", [P, HALF], F32)) for i in range(2)]
        sm = [stack.enter_context(nc.psum_tensor(f"sm{i}", [P, HALF], F32)) for i in range(2)]
        st = [stack.enter_context(nc.psum_tensor(f"st{i}", [P, HALF], F32)) for i in range(2)]
        po = [stack.enter_context(nc.psum_tensor(f"po{i}", [P, HALF], F32)) for i in range(2)]

        x4_dram = nc.dram_tensor("x4_scratch", [nb, P, QT * D], F32, kind="Internal").ap()
        dist_dram = nc.dram_tensor("dist_scratch", [nb, C, S], F32, kind="Internal").ap()
        path_dram = nc.dram_tensor("path_scratch", [nb, C, S], F32, kind="Internal").ap()

        w = {n: sb(n, [P, FC, D]) for n in io["square_weights"]}
        col = {n: sb(n, [P, FC]) for n in ("A2_bq", "A2_bk", "A4_bk")}
        row = {n: sb(n, [P, D]) for n in ALL_BIASES}
        gate_w = sb("gate_w", [P, FC, H + 1])
        gate_b = sb("gate_b", [P, H + 1])
        temp_sp = sb("temp_sp", [P, H])
        qe_sp = sb("qe_sp", [P, H, HD])
        wg, wu = sb("wg", [P, FC, HID], BF16), sb("wu", [P, FC, HID], BF16)
        wd = sb("wd", [P, HC, D], BF16)
        wq_inv = sb("wq_inv", [P, 3])
        ident, ident_b = sb("ident", [P, P]), sb("ident_b", [P, P], BF16)
        mask = sb("mask", [P, 4])
        kbias = {a: sb(f"kbias_{a}", [P, 2, FC]) for a in ("A2", "A4")}
        qbias = sb("qbias", [P, 2, FC])
        rope_cos, rope_sin = sb("rope_cos", [P, QT, HD]), sb("rope_sin", [P, QT, HD])
        neg_half = sb("neg_half", [P, S])
        ones = sb("ones", [P, P])
        power = sb("power", [P, QT * H])

        def mask_col(i, n=P):
            return mask[0:n, i:i + 1]

        with ExitStack() as setup:
            wf = [sb(f"wf{i}", [P, 2048], F32, setup) for i in range(3)]
            wt = sb("wt", [P, 2048], F32, setup)
            small = sb("setup_small", [P, 16], F32, setup)
            spx = sb("spx", [P, 4, H], F32, setup)
            block = setup.enter_context(nc.Block())
            loads = [(wf[0][:], io["w_gate"]), (wf[1][:], io["w_up"]), (wf[2][:], io["w_down"])]
            loads += [(w[n][:].rearrange("p a b -> p (a b)"), io[n]) for n in w]
            loads += [(col[n][:], io[n]) for n in col]
            loads += [(row[n][:], io[n][None, :].partition_broadcast(P).rearrange("p o d -> p (o d)"))
                      for n in row]
            loads += [(gate_w[:].rearrange("p a b -> p (a b)"), io["gate_w"]),
                      (gate_b[:], io["gate_b"][None, :].partition_broadcast(P).rearrange("p o d -> p (o d)")),
                      (temp_sp[:], io["temperature"][None, :].partition_broadcast(P).rearrange("p o d -> p (o d)")),
                      (qe_sp[:].rearrange("p h d -> p (h d)"),
                       io["query_embedding"][None, :].partition_broadcast(P).rearrange("p o d -> p (o d)")),
                      (ident[:], io["ident"]), (mask[:], io["mask"]),
                      (rope_cos[:].rearrange("p t d -> p (t d)"), io["rope_cos"]),
                      (rope_sin[:].rearrange("p t d -> p (t d)"), io["rope_sin"])]

            @block.sync
            def _(sp):
                for dst, src in loads:
                    sp.dma_start(dst, src).then_inc(consts_loaded, 16)

            @block.gpsimd
            def _(pool):
                pool.memset(neg_half[:], -0.5)
                pool.memset(ones[:], 1.0)
                pool.memset(power[:], -0.5).then_inc(setup_pool, 1)

            @block.tensor
            def _(pe):
                pe.wait_ge(setup_pool, 1)
                pe.wait_ge(setup_dve, 3)
                pe.matmul(pj[0][:, 0:3], ones[:], small[:, 0:3], start=True,
                          stop=True).then_inc(setup_pe, 1)

            @block.scalar
            def _(act):
                act.wait_ge(consts_loaded, 16 * len(loads))
                act.activation(spx[:, 0, :], temp_sp[:], ACT.Abs).then_inc(setup_act, 1)
                act.wait_ge(setup_act, 1)
                act.activation(spx[:, 1, :], spx[:, 0, :], ACT.Exp, scale=-1.0).then_inc(setup_act, 1)
                act.wait_ge(setup_act, 2)
                act.activation(spx[:, 2, :], spx[:, 1, :], ACT.Ln, bias=1.0).then_inc(setup_act, 1)

            @block.vector
            def _(dve):
                done = [0]

                def link(ins):
                    done[0] += 1
                    ins.then_inc(setup_dve, 1)
                    dve.wait_ge(setup_dve, done[0])

                dve.wait_ge(consts_loaded, 16 * len(loads))
                for i in range(3):
                    link(dve.tensor_reduce(small[:, i:i + 1], wf[i][:], AX.X, ALU.add,
                                           apply_absolute_value=True))
                dve.wait_ge(setup_pe, 1)
                link(dve.tensor_scalar(small[:, 3:6], pj[0][:, 0:3], 1.0 / (HID * D), EPS, ALU.mult, ALU.max))
                link(dve.reciprocal(small[:, 6:9], small[:, 3:6]))
                link(dve.reciprocal(wq_inv[:], small[:, 6:9]))
                for i, q in enumerate((wg, wu, wd)):
                    flat = q[:].rearrange("p a b -> p (a b)")
                    link(dve.tensor_scalar(wt[:], wf[i][:], small[:, 6 + i:7 + i], MAGIC, ALU.mult, ALU.add))
                    link(dve.tensor_scalar(wt[:], wt[:], MAGIC, 1.0, ALU.subtract, ALU.min))
                    link(dve.tensor_scalar(flat, wt[:], -1.0, None, ALU.max))
                link(dve.tensor_copy(ident_b[:], ident[:]))
                for a in ("A2", "A4"):
                    for e in range(2):
                        link(dve.tensor_scalar(kbias[a][:, e, :], col[a + "_bk"][:], mask_col(e),
                                               mask_col(2 + e), ALU.mult, ALU.add))
                for e in range(2):
                    link(dve.tensor_scalar(qbias[:, e, :], col["A2_bq"][:], mask_col(e), None, ALU.mult))
                dve.wait_ge(setup_act, 3)
                link(dve.tensor_scalar(spx[:, 3, :], temp_sp[:], 0.0, None, ALU.max))
                link(dve.tensor_tensor(temp_sp[:], spx[:, 3, :], spx[:, 2, :], ALU.add))
                link(dve.tensor_tensor(qe_sp[:], qe_sp[:], temp_sp[:].unsqueeze(2).to_broadcast([P, H, HD]),
                                       ALU.mult))

        def both(phase, name, shape, dt, where):
            return [sb(f"{phase}{name}_{s}", shape, dt, where) for s in range(2)]

        class Tiles:

            def __init__(self, phase, where):
                def two(name, shape, dt=F32):
                    return both(phase, name, shape, dt, where)

                self.x0, self.x = two("x0", [P, QT, D]), two("x", [P, QT, D])
                self.kz = [[two(f"k{e}{g}", [P, FC, S]) for g in range(4)] for e in range(2)]
                self.qe = [two(f"q{e}", [P, FC, S]) for e in range(2)]
                self.kb = two("kb", [P, FC, S], BF16)
                self.qb = [two(f"qb{e}", [P, FC, S], BF16) for e in range(2)]
                self.vv = two("v", [P, QT, H, VW])
                self.qk, self.qr = two("qk", [P, 2, QT, D]), two("qr", [P, 2, QT, D])
                self.r2 = two("r2", [P, QT, D])
                self.mp = two("mp", [P, QT, 2, FC, P])
                self.xT = two("xT", [P, FC, S])
                self.outT = two("outT", [P, H // 4, S])
                self.rc = two("rc", [P, QT, H])
                self.at, self.atT, self.res = two("at", [P, QT, D]), two("atT", [P, FC, S]), two("res", [P, QT, D])
                self.stats, self.mv = two("stats", [P, QT, 6]), two("mv", [P, QT, 2])
                self.ve, self.rstd = two("ve", [P, QT, 2]), two("rstd", [P, QT, 2])
                self.pr = [sb(f"{phase}pr{i}", [P, QT, S], F32, where) for i in range(4)]
                if phase == "A":
                    self.x0T, self.ctxT = two("x0T", [P, FC, S]), two("ctxT", [P, FC, C])
                    self.csq, self.xsq = two("csq", [P, FC, C]), two("xsq", [P, FC, S])
                    self.dist = two("dist", [C, S])
                    self.xq, self.xqT = two("xq", [P, QT, D], BF16), two("xqT", [P, FC, S], BF16)
                    self.hq = two("hq", [P, HID], BF16)
                    self.qsc = two("qsc", [P, QT, 16])
                    self.th = [t[:].rearrange("p i t d -> p i (t d)") for t in self.qk]
                    self.hid = [t[:].rearrange("p i t d -> p i (t d)") for t in self.qr]
                    self.xq_f = self.r2
                    self.hqT = [t[:].rearrange("p g n -> p (g n)").bitcast(BF16).rearrange(
                        "p (t j n) -> p t j n", t=QT, j=HC) for t in self.outT]
                else:
                    self.path, self.ctx = two("path", [C, S]), two("ctx", [C, D])
                    self.sq, self.nrm = two("sq", [P, QT * H, HD]), two("nrm", [P, 2, QT, H])
                    self.lg, self.ex = two("lg", [P, QT, H + 1]), two("ex", [P, QT, H + 1])
                    self.top, self.gs = two("top", [P, QT, 8]), two("gs", [P, 16, QT])

        def segment(phase, tiles, order, passes, ordinal, base, where, last):
            counts = Counts(order)
            assert passes == 1 or counts.banks[0] == counts.banks[1]
            x0, x, vv, kb, qb = tiles.x0, tiles.x, tiles.vv, tiles.kb, tiles.qb
            qk, qr, r2, mp, xT, outT = tiles.qk, tiles.qr, tiles.r2, tiles.mp, tiles.xT, tiles.outT
            rc, at, atT, res, stats, mv = tiles.rc, tiles.at, tiles.atT, tiles.res, tiles.stats, tiles.mv
            ve, rstd, pr, kz, qe = tiles.ve, tiles.rstd, tiles.pr, tiles.kz, tiles.qe
            if phase == "A":
                x0T, ctxT, csq, xsq, dist = tiles.x0T, tiles.ctxT, tiles.csq, tiles.xsq, tiles.dist
                xq, xqT, hq, qsc, th, hid = tiles.xq, tiles.xqT, tiles.hq, tiles.qsc, tiles.th, tiles.hid
                xq_f, hqT = tiles.xq_f, tiles.hqT
            else:
                path, ctx, sq, nrm = tiles.path, tiles.ctx, tiles.sq, tiles.nrm
                lg, ex, top, gs = tiles.lg, tiles.ex, tiles.top, tiles.gs
            block = where.enter_context(nc.Block())

            class Clock:

                def __init__(self, eng, it):
                    self.eng, self.it, self.step, self.seen = eng, it, None, {}

                def wait(self, name, step, nth=-1, behind=0):
                    if step not in counts.index:
                        return
                    k = counts.at[name, step, nth] - behind
                    if counts.index[step] <= counts.index[self.step]:
                        k += counts.per[name]
                    elif passes == 1:
                        return
                    self.eng.wait_ge(sems[name], self.it * counts.per[name] + (base[name] + k))

                def tell(self, ins, name, step):
                    n = self.seen.get((name, step), 0)
                    assert (name, step, n) in counts.at, (name, step, n)
                    self.seen[name, step] = n + 1
                    self.seen[name] = self.seen.get(name, 0) + 1
                    assert self.seen[name] == counts.at[name, step, n], (name, step)
                    ins.then_inc(sems[name], 1)

                def link(self, ins, name):
                    step = self.step
                    n = self.seen.get((name, step), 0)
                    self.tell(ins, name, step)
                    self.wait(name, step, nth=n)

                def bank(self, use):
                    return pj[counts.bank[use][0]]

                def wait_bank_full(self, use):
                    b, k = counts.bank[use]
                    self.eng.wait_ge(bank_full[b], self.it * counts.banks[b] + (base["bank"][b] + k))

                def wait_bank_free(self, use):
                    if counts.before[use] is not None:
                        before, step = counts.before[use]
                        self.wait(emptied_by(before), step)

                def filled(self, ins, use):
                    ins.then_inc(bank_full[counts.bank[use][0]], 1)

                def stored(self, semaphore, step):
                    self.eng.wait_ge(semaphore, ordinal(step, self.it) * 16 + 16)

            def walk(eng, do):
                if passes > 1:
                    with eng.Fori(0, passes) as it:
                        ck = Clock(eng, it)
                        for step in order:
                            ck.step = step
                            do(ck, step)
                else:
                    ck = Clock(eng, 0)
                    for step in order:
                        ck.step = step
                        do(ck, step)

            def alone(eng):
                eng.sem_inc(passed, 1)

            @block.sync
            def _(sp):
                def one(dram, b):
                    part = dram[b:b + 1] if isinstance(b, int) else dram[bass.ds(b, 1)]
                    return part.rearrange("o p n -> p o n")

                def do(ck, step):
                    kind, what, s = step
                    b = ordinal(step, ck.it) * 2 + s
                    if kind == "load":
                        if phase == "A":
                            ck.wait("dist_ready", ("dist", "A3", s))
                            moves = [(x0T[s][:].rearrange("p a b -> p (a b)"), io["xT"]),
                                     (ctxT[s][:].rearrange("p a b -> p (a b)"), io["ctxT"]),
                                     (x0[s][:].rearrange("p a b -> p (a b)"), io["x"])]
                        else:
                            ck.wait("x4_used", ("expand", "E", s))
                            moves = [(path[s][:], path_dram), (ctx[s][:], io["ctx"]),
                                     (x0[s][:].rearrange("p a b -> p (a b)"), x4_dram)]
                        for dst, src in moves:
                            sp.dma_start(dst.unsqueeze(1), one(src, b)).then_inc(inputs_loaded[phase][s], 16)
                    elif what == "D":
                        ck.wait("dist_ready", ("dist", "A3", s))
                        sp.dma_start(one(dist_dram, b), dist[s][:].unsqueeze(1)).then_inc(dist_stored[s], 16)
                    else:
                        ck.wait("x_ready", ("ln", what, s))
                        sp.dma_start(one(x4_dram if phase == "A" else out, b),
                                     x[s][:].rearrange("p a b -> p (a b)").unsqueeze(1)).then_inc(
                                         tokens_stored[phase][s], 16)

                walk(sp, lambda ck, step: do(ck, step) if step[0] in ("load", "store") else None)
                if last:
                    for s in range(2):
                        sp.wait_ge(tokens_stored[phase][s], 16 * (nb // 2 + 1))
                        if phase == "A":
                            sp.wait_ge(dist_stored[s], 16 * (nb // 2 + 1))

            @block.tensor
            def _(pe):
                def features(ck, step, weight, src, n):
                    bank = ck.bank(step)
                    ck.wait_bank_free(step)
                    for c in range(FC):
                        for f in range(FC):
                            ins = pe.matmul(bank[:, c * S:c * S + n], weight[:, f, c * P:(c + 1) * P],
                                            src[:, f, 0:n], start=(f == 0), stop=(f == FC - 1))
                    ck.filled(ins, step)

                def tokens(ck, step, weight, src, tiles):
                    bank = ck.bank(step)
                    ck.wait_bank_free(step)
                    for t, (k, n) in enumerate(tiles):
                        for f in range(FC):
                            ins = pe.matmul(bank[0:n, t * D:(t + 1) * D], src[:, f, k:k + n],
                                            weight[:, f, :], start=(f == 0), stop=(f == FC - 1))
                    ck.filled(ins, step)

                def turn(ck, step, src, ident_, dt=F32):
                    bank = ck.bank(step)[:] if dt == F32 else ck.bank(step)[:].bitcast(BF16)
                    ck.wait_bank_free(step)
                    for f in range(FC):
                        for t in range(QT):
                            ins = pe.transpose(bank[:, f * S + t * P:f * S + (t + 1) * P],
                                               src[:, t, f * P:(f + 1) * P], ident_)
                    ck.filled(ins, step)

                def loaded(ck, step):
                    pe.wait_ge(inputs_loaded[phase][step[2]], ordinal(step, ck.it) * 48 + 48)

                def scores(ck, att, s, p):
                    for i, (k, n) in enumerate(key_tiles(att)):
                        for j in range(2):
                            c, p0, e = place(HEADS[2 * p + j])
                            ins = pe.matmul(st[j][0:n, i * S:(i + 1) * S], kz[e][p0 // 32][s][:, c, k:k + n],
                                            qe[e][s][:, c, :], start=True, stop=True)
                            if i == len(key_tiles(att)) - 1:
                                ck.tell(ins, "scores_ready", ("core", att, s, p))

                def weighted_values(ck, att, s, p):
                    ck.wait("probs_ready", ("core", att, s, p))
                    if p == 0:
                        ck.wait("out_taken", ("take", att, s), behind=1)
                        ck.wait("v_ready", ("v", att, s))
                    tiles_ = key_tiles(att)
                    for i, (k, n) in enumerate(tiles_):
                        for j in range(2):
                            h = HEADS[2 * p + j]
                            g, r = h // 4, 32 * (h % 4)
                            ins = pe.matmul(po[g // 2][r:r + VW, g % 2 * S:(g % 2 + 1) * S], vv[s][0:n, i, h, :],
                                            pr[2 * (p % 2) + j][0:n, i, :], start=(i == 0),
                                            stop=(i == len(tiles_) - 1), skip_group_check=True)
                    ck.tell(ins, "weighted", ("core", att, s, p + 1))

                def do(ck, step):
                    kind, att, s = step[:3]
                    if kind in ("q", "k", "v"):
                        if att == "A1":
                            src = x0T[s]
                            if kind == "q":
                                loaded(ck, step)
                        elif att == "A2" and kind != "q":
                            src = ctxT[s]
                        else:
                            src = xT[s]
                            before = {"A2": ("xT", "A1", s), "A3": ("xT", "F", s), "A4": ("xT", "E", s)}[att]
                            if kind == "q":
                                ck.wait("xT_ready", before)
                        weight = w[f"{att}_w{kind}"]
                        if kind == "v" or att == "A3" or (att == "A4" and kind == "q"):
                            tiles = key_tiles(att) if kind != "q" else [(0, P), (P, P)]
                            tokens(ck, step, weight, src, tiles)
                        else:
                            features(ck, step, weight, src, S if kind == "q" else KEYS[att])
                    elif kind == "qT":
                        ck.wait("rotated", ("rot", att, s))
                        turn(ck, step, qr[s][:, 0], ident[:])
                    elif kind == "kT":
                        turn(ck, step, qr[s][:, 1], ident[:])
                    elif kind == "max":
                        i = step[3]
                        c, p0, e = place(HEADS[i])
                        n = KEYS[att]
                        if i == 0:
                            q_step = ("q", att, s) if att in ("A1", "A2") else ("qT", att, s)
                            k_step = ("kT", att, s) if att == "A3" else ("k", att, s)
                            ck.wait("q_ready", q_step)
                            ck.wait("k_ready", k_step)
                        ck.wait("max_done", step, behind=2)
                        bank = sm[counts.at["max_scores", step, -1] % 2]
                        for t in range(QT):
                            ins = pe.matmul(bank[:, t * S:t * S + n], qb[e][s][p0:p0 + 32, c, t * P:(t + 1) * P],
                                            kb[s][p0:p0 + 32, c, 0:n], start=True, stop=True)
                        ck.tell(ins, "max_scores", step)
                    elif kind == "shift":
                        e = step[3]
                        if e == 0:
                            ck.wait("max_done", ("max", att, s, H - 1))
                        ck.wait_bank_free(step)
                        for c in range(FC):
                            for t in range(QT):
                                ins = pe.transpose(ck.bank(step)[:, c * S + t * P:c * S + (t + 1) * P],
                                                   mp[s][:, t, e, c, :], ident[:])
                        ck.filled(ins, step)
                    elif kind == "core":
                        p = step[3]
                        if p == 0:
                            ck.wait("q_shifted", ("shift", att, s, 1))
                        elif p < PAIRS:
                            ck.wait("probs_ready", ("core", att, s, p - 1))
                        if p < PAIRS:
                            scores(ck, att, s, p)
                        if p > 0:
                            weighted_values(ck, att, s, p - 1)
                    elif kind == "norm":
                        t = step[3]
                        if t == 0:
                            ck.wait("out_taken", ("take", att, s))
                        ck.wait_bank_free(step)
                        for g in range(H // 4):
                            ins = pe.transpose(ck.bank(step)[:, g * P:(g + 1) * P], outT[s][:, g, t * P:(t + 1) * P],
                                               ident[:])
                        ck.filled(ins, step)
                    elif kind == "oT":
                        ck.wait("normed", ("norm", att, s, 1))
                        turn(ck, step, at[s][:], ident[:])
                    elif kind == "oproj":
                        if att != "A4":
                            ck.wait("attnT_ready", ("oT", att, s))
                        tokens(ck, step, w[f"{att}_wo"], atT[s], [(0, P), (P, P)])
                    elif kind == "xT":
                        ck.wait("x_ready", ("ln", att, s))
                        turn(ck, step, x[s][:], ident[:])
                    elif kind == "xqT":
                        ck.wait("xq_ready", ("fq", att, s))
                        turn(ck, step, xq[s][:], ident_b[:], BF16)
                    elif kind == "gu":
                        t, half = step[3:]
                        if (t, half) == (0, 0):
                            ck.wait("xqT_ready", ("xqT", att, s))
                        for name, wt_ in (("gate", wg), ("up", wu)):
                            use = step + (name,)
                            ck.wait_bank_free(use)
                            for f in range(FC):
                                ins = pe.matmul(ck.bank(use)[:], xqT[s][:, f, t * P:(t + 1) * P],
                                                wt_[:, f, half * HALF:(half + 1) * HALF],
                                                start=(f == 0), stop=(f == FC - 1))
                            ck.filled(ins, use)
                    elif kind == "hT":
                        t = step[3]
                        ck.wait("hq_ready", ("hq", att, s, t))
                        bank = ck.bank(step)[:].bitcast(BF16)
                        ck.wait_bank_free(step)
                        for j in range(HC):
                            ins = pe.transpose(bank[:, j * P:(j + 1) * P], hq[s][:, j * P:(j + 1) * P], ident_b[:])
                        ck.filled(ins, step)
                    elif kind == "down":
                        ck.wait("hqT_ready", ("hT", att, s, QT - 1))
                        ck.wait_bank_free(step)
                        for t in range(QT):
                            for j in range(HC):
                                ins = pe.matmul(ck.bank(step)[:, t * D:(t + 1) * D], hqT[s][:, t, j, :], wd[:, j, :],
                                                start=(j == 0), stop=(j == HC - 1))
                        ck.filled(ins, step)
                    elif kind == "dist":
                        ck.wait("xT_ready", ("xT", att, s))
                        ck.wait("squares_ready", step)
                        ck.wait_bank_free(step)
                        for i in range(3):
                            for f in range(FC):
                                lhs = (ctxT[s][:, f, :], neg_half[:, 0:C], csq[s][:, f, :])[i]
                                rhs = (xT[s][:, f, :], xsq[s][:, f, :], neg_half[:])[i]
                                ins = pe.matmul(ck.bank(step)[0:C, 0:S], lhs, rhs,
                                                start=(i == 0 and f == 0), stop=(i == 2 and f == FC - 1))
                        ck.filled(ins, step)
                    elif kind == "expand":
                        loaded(ck, step)
                        ck.wait_bank_free(step)
                        for t in range(QT):
                            ins = pe.matmul(ck.bank(step)[:, t * D:(t + 1) * D], path[s][:, t * P:(t + 1) * P],
                                            ctx[s][:], start=True, stop=True)
                        ck.filled(ins, step)
                    elif kind == "gate":
                        ck.wait("attnT_ready", ("oT", att, s))
                        ck.wait_bank_free(step)
                        for t in range(QT):
                            for f in range(FC):
                                ins = pe.matmul(ck.bank(step)[:, t * (H + 1):(t + 1) * (H + 1)],
                                                atT[s][:, f, t * P:(t + 1) * P], gate_w[:, f, :],
                                                start=(f == 0), stop=(f == FC - 1))
                        ck.filled(ins, step)

                walk(pe, do)

            @block.scalar
            def _(act):
                def put_queries(ck, step, att):
                    s = step[2]
                    use = step
                    ck.wait_bank_full(use)
                    bank = ck.bank(use)[:].rearrange("p (c n) -> p c n", c=FC)
                    for e in range(2):
                        if att == "A2":
                            for c in range(FC):
                                for dst in (qb[e][s], qe[e][s]):
                                    ins = act.activation(dst[:, c, :], bank[:, c, :], ACT.Identity,
                                                         scale=mask_col(e), bias=qbias[:, e, c:c + 1])
                        else:
                            for dst in (qb[e][s], qe[e][s]):
                                ins = act.activation(dst[:], bank, ACT.Copy, scale=mask_col(e))
                    ck.tell(ins, "q_ready", step)

                def put_keys(ck, step, att):
                    s = step[2]
                    ck.wait_bank_full(step)
                    n = KEYS[att]
                    bank = ck.bank(step)[:].rearrange("p (c n) -> p c n", c=FC)
                    if att in ("A1", "A3"):
                        act.activation(kb[s][:], bank, ACT.Copy)
                    else:
                        for c in range(FC):
                            act.activation(kb[s][:, c, 0:n], bank[:, c, 0:n], ACT.Identity,
                                           bias=col[att + "_bk"][:, c:c + 1])
                    for g in range(4):
                        r = slice(32 * g, 32 * g + 32)
                        for e in range(2):
                            if att in ("A1", "A3"):
                                ins = act.activation(kz[e][g][s][r], bank[r], ACT.Identity, scale=mask[r, e:e + 1],
                                                     bias=mask[r, 2 + e:3 + e])
                            else:
                                for c in range(FC):
                                    ins = act.activation(kz[e][g][s][r, c, 0:n], bank[r, c, 0:n], ACT.Identity,
                                                         scale=mask[r, e:e + 1], bias=kbias[att][r, e, c:c + 1])
                    ck.tell(ins, "k_ready", step)

                def do(ck, step):
                    kind, att, s = step[:3]
                    if kind == "q" and att in ("A1", "A2") or kind == "qT":
                        put_queries(ck, step, att)
                    elif kind == "k" and att != "A3" or kind == "kT":
                        put_keys(ck, step, att)
                    elif kind == "core" and step[3] < PAIRS:
                        tiles_ = key_tiles(att)
                        n, width = tiles_[0][1], len(tiles_) * S
                        for j in range(2):
                            ck.wait("scores_ready", step, nth=j)
                            dst = pr[2 * (step[3] % 2) + j][0:n].rearrange("p a b -> p (a b)")
                            ck.tell(act.activation(dst[:, 0:width], st[j][0:n, 0:width], ACT.Exp, scale=HD ** -0.5),
                                    "probs_ready", step)
                    elif kind == "take":
                        ck.wait("weighted", ("core", att, s, PAIRS))
                        for i in range(2):
                            ins = act.activation(outT[s][:, 2 * i:2 * i + 2].rearrange("p a b -> p (a b)"), po[i][:],
                                                 ACT.Copy)
                        ck.tell(ins, "out_taken", step)
                    elif kind in ("xT", "oT"):
                        dst, name = (xT[s], "xT_ready") if kind == "xT" else (atT[s], "attnT_ready")
                        ck.wait_bank_full(step)
                        ins = act.activation(dst[:].rearrange("p a b -> p (a b)"), ck.bank(step)[:], ACT.Copy)
                        ck.tell(ins, name, step)
                    elif kind == "xqT":
                        ck.wait_bank_full(step)
                        ins = act.activation(xqT[s][:].rearrange("p a b -> p (a b)"),
                                             ck.bank(step)[:].bitcast(BF16)[:, 0:FC * S], ACT.Copy)
                        ck.tell(ins, "xqT_ready", step)
                    elif kind == "gu":
                        t, half = step[3:]
                        use = step + ("gate",)
                        ck.wait_bank_full(use)
                        ins = act.activation(th[s][:, half, :], ck.bank(use)[:], ACT.Tanh, scale=qsc[s][:, t, 4:5])
                        ck.tell(ins, "tanh_ready", step)
                    elif kind == "hT":
                        t = step[3]
                        ck.wait_bank_full(step)
                        ins = act.activation(hqT[s][:, t].rearrange("p a b -> p (a b)"),
                                             ck.bank(step)[:].bitcast(BF16), ACT.Copy)
                        ck.tell(ins, "hqT_ready", step)
                    elif kind == "gate":
                        ck.wait("logits_ready", step)
                        ins = act.activation(ex[s][:], lg[s][:], ACT.Exp)
                        ck.tell(ins, "exps_ready", step)
                    else:
                        return

                walk(act, do)

            @block.gpsimd
            def _(pool):
                def link(ck, ins):
                    ck.link(ins, "pool_step")

                def do(ck, step):
                    kind, att, s = step[:3]
                    if kind == "rot" and att == "A3":
                        for i, name in enumerate("qk"):
                            ck.wait("q_tokens", (name, att, s))
                            src = qk[s][:, i].rearrange("p t (h d) -> p t h d", h=H)
                            dst = qr[s][:, i].rearrange("p t (h d) -> p t h d", h=H)
                            tmp = r2[s][:].rearrange("p t (h d) -> p t h d", h=H)
                            cos = rope_cos[:].unsqueeze(2).to_broadcast([P, QT, H, HD])
                            sin = rope_sin[:].unsqueeze(2).to_broadcast([P, QT, H, HD])
                            pool.tensor_tensor(dst, src, cos, ALU.mult)
                            pool.tensor_tensor(tmp[:, :, :, 0::2], src[:, :, :, 1::2], sin[:, :, :, 0::2], ALU.mult)
                            link(ck, pool.tensor_tensor(tmp[:, :, :, 1::2], src[:, :, :, 0::2], sin[:, :, :, 1::2],
                                                        ALU.mult))
                            ins = pool.tensor_tensor(dst, dst, tmp, ALU.add)
                            if i == 0:
                                link(ck, ins)
                        ck.tell(ins, "rotated", step)
                    elif kind == "rot" and att == "A4":
                        ck.wait("q_tokens", ("q", att, s))
                        src = qk[s][:, 0].rearrange("p t (h d) -> p (t h) d", h=H)
                        dst = qr[s][:, 0].rearrange("p t (h d) -> p (t h) d", h=H)
                        ck.tell(pool.tensor_tensor(sq[s][:], src, src, ALU.mult), "squared", step)
                        ck.wait("norms2", step)
                        link(ck, pool.tensor_tensor(nrm[s][:, 1].rearrange("p t h -> p (t h)"),
                                                    nrm[s][:, 0].rearrange("p t h -> p (t h)"), power[:], ALU.pow))
                        link(ck, pool.tensor_tensor(nrm[s][:, 0], nrm[s][:, 1],
                                                    temp_sp[:].unsqueeze(1).to_broadcast([P, QT, H]), ALU.mult))
                        link(ck, pool.tensor_tensor(
                            dst, src, nrm[s][:, 0].rearrange("p t h -> p (t h)").unsqueeze(2)
                            .to_broadcast([P, QT * H, HD]), ALU.mult))
                        qr4 = qr[s][:, 0].rearrange("p t (h d) -> p t (h d)", h=H)
                        emb = qe_sp[:].rearrange("p h d -> p (h d)").unsqueeze(1).to_broadcast([P, QT, D])
                        ck.tell(pool.tensor_tensor(qr4, qr4, emb, ALU.add), "rotated", step)
                    elif kind == "ln":
                        ck.wait("var_ready", step)
                        alone(pool)
                        link(ck, pool.tensor_scalar(ve[s][:, :, 0:1], mv[s][:, :, 1:2], EPS, None, ALU.add))
                        ck.tell(pool.tensor_tensor(rstd[s][:, :, 0:1], ve[s][:, :, 0:1],
                                                     power[:, 0:QT].unsqueeze(2), ALU.pow), "rstd_ready", step)
                    elif kind == "dist":
                        ck.wait("xT_ready", ("xT", att, s))
                        pool.tensor_tensor(xsq[s][:], xT[s][:], xT[s][:], ALU.mult)
                        ck.tell(pool.tensor_tensor(csq[s][:], ctxT[s][:], ctxT[s][:], ALU.mult),
                                  "squares_ready", step)

                walk(pool, do)

            @block.vector
            def _(dve):
                def link(ck, ins):
                    ck.link(ins, "dve_step")

                def do(ck, step):
                    kind, att, s = step[:3]
                    if kind in ("q", "k") and att == "A3" or kind == "q" and att == "A4":
                        i = "qk".index(kind)
                        ck.wait_bank_full(step)
                        bias = row[f"{att}_b{kind}"][:].unsqueeze(1).to_broadcast([P, QT, D])
                        ins = dve.tensor_tensor(qk[s][:, i], ck.bank(step)[:].rearrange("p (t d) -> p t d", t=QT),
                                                bias, ALU.add)
                        ck.tell(ins, "q_tokens", step)
                    elif kind == "rot" and att == "A4":
                        ck.wait("squared", step)
                        ck.tell(dve.tensor_reduce(nrm[s][:, 0].rearrange("p t h -> p (t h)"), sq[s][:], AX.X, ALU.add),
                                  "norms2", step)
                    elif kind == "v":
                        ck.wait_bank_full(step)
                        tiles = key_tiles(att)
                        n, nt = tiles[0][1], len(tiles)
                        src = ck.bank(step)[0:n, 0:nt * D].rearrange("p (t h d) -> p t h d", t=nt, h=H)
                        for t in range(nt):
                            dst = vv[s][0:n, t, :, 0:HD]
                            if att == "A1":
                                ins = dve.tensor_copy(dst, src[:, t])
                            else:
                                bias = row[att + "_bv"][0:n].rearrange("p (h d) -> p h d", h=H)
                                ins = dve.tensor_tensor(dst, src[:, t], bias, ALU.add)
                        ck.tell(ins, "v_ready", step)
                    elif kind == "max":
                        c, p0, e = place(HEADS[step[3]])
                        ck.wait("max_scores", step)
                        bank = sm[counts.at["max_scores", step, -1] % 2]
                        at_row = p0 + 16 * (1 - e)
                        ins = dve.tensor_reduce(mp[s][:, :, e, c, at_row:at_row + 1],
                                                bank[:].rearrange("p (t n) -> p t n", t=QT)[:, :, 0:KEYS[att]],
                                                AX.X, ALU.max, negate=True)
                        ck.tell(ins, "max_done", step)
                    elif kind == "shift":
                        e = step[3]
                        ck.wait_bank_full(step)
                        queries = qe[e][s][:].rearrange("p c n -> p (c n)")
                        ins = dve.tensor_tensor(queries, queries, ck.bank(step)[:], ALU.add)
                        ck.tell(ins, "q_shifted", step)
                    elif kind == "norm":
                        t = step[3]
                        ck.wait_bank_full(step)
                        o = ck.bank(step)[:].rearrange("p (h w) -> p h w", h=H)
                        link(ck, dve.reciprocal(rc[s][:, t, :].unsqueeze(2), o[:, :, HD:HD + 1]))
                        ins = dve.tensor_tensor(at[s][:, t].rearrange("p (h d) -> p h d", h=H), o[:, :, 0:HD],
                                                rc[s][:, t, :].unsqueeze(2).to_broadcast([P, H, HD]), ALU.mult)
                        ck.tell(ins, "normed", step)
                        if att == "A1" and t == 1:
                            ck.wait("normed", step)
                            ck.tell(dve.tensor_tensor(res[s][:], x0[s][:], at[s][:], ALU.add), "x_used", step)
                    elif kind == "oproj":
                        ck.wait_bank_full(step)
                        bank = ck.bank(step)[:].rearrange("p (t d) -> p t d", t=QT)
                        bias = row[att + "_bo"][:].unsqueeze(1).to_broadcast([P, QT, D])
                        if att == "A4":
                            for t in range(QT):
                                ins = dve.scalar_tensor_tensor(out=at[s][:, t], in0=bank[:, t], scalar=gs[s][:, 15, t:t + 1],
                                                               in1=row["A4_bo"][:], op0=ALU.mult, op1=ALU.add)
                        else:
                            ins = dve.tensor_tensor(at[s][:], bank, bias, ALU.add)
                        ck.tell(ins, "proj_taken", step)
                        ck.wait("proj_taken", step)
                        link(ck, dve.tensor_tensor(res[s][:], at[s][:], x[s][:], ALU.add))
                    elif kind == "expand":
                        ck.wait_bank_full(step)
                        ck.wait("x_ready", ("ln", "A4", s))
                        ins = dve.tensor_tensor(res[s][:], ck.bank(step)[:].rearrange("p (t d) -> p t d", t=QT),
                                                x0[s][:], ALU.add)
                        ck.tell(ins, "x4_used", step)
                    elif kind == "down":
                        ck.wait_bank_full(step)
                        bank = ck.bank(step)[:].rearrange("p (t d) -> p t d", t=QT)
                        for t in range(QT):
                            ins = dve.scalar_tensor_tensor(out=res[s][:, t], in0=bank[:, t], scalar=qsc[s][:, t, 10:11],
                                                           in1=x[s][:, t], op0=ALU.mult, op1=ALU.add)
                        ck.tell(ins, "down_taken", step)
                        ck.wait("down_taken", step)
                    elif kind == "ln":
                        if att == "A1":
                            ck.wait("x_used", ("norm", att, s, 1))
                        if att == "E":
                            ck.wait("x4_used", ("expand", att, s))
                        for t in range(QT):
                            ins = dve.bn_stats(stats[s][:, t, :], res[s][:, t, :])
                        link(ck, ins)
                        alone(dve)
                        for t in range(QT):
                            ins = dve.bn_aggr(mv[s][:, t, :], stats[s][:, t, :])
                        ck.tell(ins, "var_ready", step)
                        ck.wait("rstd_ready", step)
                        if att == "A1":
                            ck.stored(tokens_stored[phase][s], step)
                        if att == "E":
                            ck.stored(tokens_stored[phase][s], step)
                        for t in range(QT):
                            ins = dve.tensor_scalar(x[s][:, t], res[s][:, t], mv[s][:, t, 0:1], rstd[s][:, t, 0:1],
                                                    ALU.subtract, ALU.mult)
                        ck.tell(ins, "x_ready", step)
                    elif kind == "fq":
                        ck.wait("x_ready", ("ln", "A2", s))
                        link(ck, dve.tensor_reduce(qsc[s][:, :, 0:1], x[s][:], AX.X, ALU.max, apply_absolute_value=True))
                        link(ck, dve.tensor_scalar(qsc[s][:, :, 1:2], qsc[s][:, :, 0:1], EPS, None, ALU.max))
                        link(ck, dve.reciprocal(qsc[s][:, :, 2:3], qsc[s][:, :, 1:2]))
                        link(ck, dve.tensor_scalar(qsc[s][:, :, 3:4], qsc[s][:, :, 2:3], QMAX, None, ALU.mult))
                        for t in range(QT):
                            ins = dve.tensor_scalar(xq_f[s][:, t], x[s][:, t], qsc[s][:, t, 3:4], MAGIC, ALU.mult, ALU.add)
                        link(ck, ins)
                        link(ck, dve.tensor_scalar(xq[s][:], xq_f[s][:], MAGIC, QMAX, ALU.subtract, ALU.min))
                        link(ck, dve.tensor_scalar(qsc[s][:, :, 4:5], qsc[s][:, :, 1:2], wq_inv[:, 0:1], 0.5 / QMAX,
                                                   ALU.mult, ALU.mult))
                        link(ck, dve.tensor_scalar(qsc[s][:, :, 5:6], qsc[s][:, :, 1:2], wq_inv[:, 1:2], 1.0 / QMAX,
                                                   ALU.mult, ALU.mult))
                        ck.tell(dve.tensor_tensor(qsc[s][:, :, 6:7], qsc[s][:, :, 4:5], qsc[s][:, :, 5:6], ALU.mult),
                                  "xq_ready", step)
                    elif kind == "gu":
                        t, half = step[3:]
                        g, u = step + ("gate",), step + ("up",)
                        ck.wait("tanh_ready", step)
                        if (t, half) == (1, 0):
                            ck.wait("hq_ready", ("hq", att, s, 0))
                        ins = dve.scalar_tensor_tensor(out=hid[s][:, half], in0=th[s][:, half], scalar=1.0,
                                                       in1=ck.bank(g)[:], op0=ALU.add, op1=ALU.mult)
                        ck.tell(ins, "gated", step)
                        ck.wait("gated", step)
                        ck.wait_bank_full(u)
                        ins = dve.tensor_tensor(hid[s][:, half], hid[s][:, half], ck.bank(u)[:], ALU.mult)
                        ck.tell(ins, "hid_ready", step)
                    elif kind == "hq":
                        t = step[3]
                        q = qsc[s][:, t]
                        ck.wait("hid_ready", ("gu", att, s, t, 1))
                        flat = hid[s][:].rearrange("p a b -> p (a b)")
                        link(ck, dve.tensor_reduce(q[:, 7:8], flat, AX.X, ALU.max, apply_absolute_value=True))
                        link(ck, dve.tensor_scalar(q[:, 8:9], q[:, 7:8], q[:, 6:7], EPS, ALU.mult, ALU.max))
                        link(ck, dve.reciprocal(q[:, 9:10], q[:, 8:9]))
                        link(ck, dve.tensor_scalar(q[:, 11:12], q[:, 9:10], q[:, 6:7], QMAX, ALU.mult, ALU.mult))
                        link(ck, dve.tensor_scalar(q[:, 10:11], q[:, 8:9], wq_inv[:, 2:3], 1.0 / QMAX,
                                                   ALU.mult, ALU.mult))
                        link(ck, dve.tensor_scalar(flat, flat, q[:, 11:12], MAGIC, ALU.mult, ALU.add))
                        if t > 0:
                            ck.wait("hqT_ready", ("hT", att, s, t - 1))
                        ck.tell(dve.tensor_scalar(hq[s][:], flat, MAGIC, QMAX, ALU.subtract, ALU.min), "hq_ready", step)
                        ck.wait("hq_ready", step)
                    elif kind == "dist":
                        ck.wait_bank_full(step)
                        ck.stored(dist_stored[s], step)
                        ins = dve.tensor_scalar(dist[s][:], ck.bank(step)[0:C, 0:S], -2.0, 0.0, ALU.mult, ALU.max)
                        ck.tell(ins, "dist_ready", step)
                    elif kind == "gate":
                        ck.wait_bank_full(step)
                        src = ck.bank(step)[:, 0:QT * (H + 1)].rearrange("p (t n) -> p t n", t=QT)
                        ins = (dve.tensor_tensor(lg[s][:], src, gate_b[:].unsqueeze(1).to_broadcast([P, QT, H + 1]),
                                                 ALU.add))
                        ck.tell(ins, "logits_taken", step)
                        ck.wait("logits_taken", step)
                        nr = H - 1
                        dve.tensor_reduce(gs[s][:, 0, :].unsqueeze(2), lg[s][:, :, 0:nr], AX.X, ALU.max)
                        link(ck, dve.tensor_reduce(gs[s][:, 1, :].unsqueeze(2), lg[s][:, :, nr:H + 1], AX.X, ALU.max))
                        dve.tensor_tensor(lg[s][:, :, 0:nr], lg[s][:, :, 0:nr],
                                          gs[s][:, 0, :].unsqueeze(2).to_broadcast([P, QT, nr]), ALU.subtract)
                        ck.tell(dve.tensor_tensor(lg[s][:, :, nr:H + 1], lg[s][:, :, nr:H + 1],
                                                    gs[s][:, 1, :].unsqueeze(2).to_broadcast([P, QT, 2]), ALU.subtract),
                                  "logits_ready", step)
                        ck.wait("exps_ready", step)
                        alone(dve)
                        for t in range(QT):
                            dve.max(top[s][:, t, :], ex[s][:, t, 0:nr])
                        dve.tensor_reduce(gs[s][:, 2, :].unsqueeze(2), ex[s][:, :, 0:nr], AX.X, ALU.add)
                        link(ck, dve.tensor_reduce(gs[s][:, 3, :].unsqueeze(2), ex[s][:, :, nr:H + 1], AX.X, ALU.add))
                        dve.tensor_reduce(gs[s][:, 4, :].unsqueeze(2), top[s][:, :, 0:ROUTED], AX.X, ALU.add)
                        dve.reciprocal(gs[s][:, 5, :], gs[s][:, 2, :])
                        link(ck, dve.reciprocal(gs[s][:, 6, :], gs[s][:, 3, :]))
                        e0, e1 = (ex[s][:, :, nr + i:nr + i + 1].rearrange("p t o -> p (t o)") for i in range(2))
                        dve.tensor_tensor(gs[s][:, 7, :], e0, gs[s][:, 6, :], ALU.mult)
                        dve.tensor_tensor(gs[s][:, 8, :], e1, gs[s][:, 6, :], ALU.mult)
                        link(ck, dve.tensor_tensor(gs[s][:, 9, :], gs[s][:, 4, :], gs[s][:, 5, :], ALU.mult))
                        dve.tensor_tensor(gs[s][:, 10, :], gs[s][:, 7, :], gs[s][:, 8, :], ALU.add)
                        link(ck, dve.tensor_tensor(gs[s][:, 11, :], gs[s][:, 8, :], gs[s][:, 9, :], ALU.mult))
                        dve.tensor_scalar(gs[s][:, 12, :], gs[s][:, 11, :], 2.0 * ROUTED, None, ALU.mult)
                        link(ck, dve.tensor_tensor(gs[s][:, 13, :], gs[s][:, 7, :], gs[s][:, 10, :], ALU.mult))
                        link(ck, dve.tensor_scalar(gs[s][:, 14, :], gs[s][:, 13, :], 2.0, None, ALU.mult))
                        link(ck, dve.tensor_tensor(gs[s][:, 15, :], gs[s][:, 14, :], gs[s][:, 12, :], ALU.add))

                walk(dve, do)

        pairs = nb // 2
        base = {x: 0 for x in SIGNALS}
        base["bank"] = [0, 0]

        def prime(start_counts, stored):
            with nc.Block() as start:
                @start.sync
                def _(sp):
                    for x in SIGNALS:
                        if start_counts.per[x]:
                            sp.sem_inc(sems[x], start_counts.per[x])
                    for x in stored:
                        sp.sem_inc(x, 16)

        def run(phase, stored):
            before, body, after, ahead = orders(phase)

            def in_body(step, it):
                return it + 1 if step in ahead or step[0] == "load" else it

            with ExitStack() as where:
                tiles = Tiles(phase, where)
                with nc.Block() as fixed:
                    @fixed.vector
                    def _(dve):
                        for s in range(2):
                            dve.memset(tiles.mp[s][:], 0.0)
                            for e in range(2):
                                for g in range(4):
                                    dve.memset(tiles.kz[e][g][s][:], 0.0)
                            dve.memset(tiles.vv[s][:, :, :, HD:HD + 1], 1.0)
                            dve.memset(tiles.vv[s][:, :, :, HD + 1:VW], 0.0)
                segments = [(before, 1, lambda step, it: 0)]
                if pairs > 1:
                    segments.append((body, pairs - 1, in_body))
                segments.append((after, 1, lambda step, it: pairs - 1))
                for n, (order, passes, ordinal) in enumerate(segments):
                    counts = Counts(order)
                    prime(counts, stored if n == 0 else [])
                    with ExitStack() as blocks:
                        segment(phase, tiles, order, passes, ordinal, base, blocks, n == len(segments) - 1)
                    for x in SIGNALS:
                        base[x] += counts.per[x] * (passes + 1)
                    base["bank"] = [base["bank"][i] + counts.banks[i] * passes for i in range(2)]

        run("A", tokens_stored["A"] + dist_stored)

        with ExitStack() as where:
            cost = sb("cost", [nb, C + 1, S + 1], F32, where)
            low = sb("low", [nb, S], F32, where)
            left = sb("left", [nb, S + 1], F32, where)
            diag = sb("diag", [nb, S], F32, where)
            on = sb("on", [nb, S], F32, where)
            enter = sb("enter", [nb, S], F32, where)
            leave = sb("leave", [nb, S], F32, where)
            leave_diag = sb("leave_diag", [nb, S + 1], F32, where)
            leave_up = sb("leave_up", [nb, S], F32, where)
            block = where.enter_context(nc.Block())
            ROWS = 7
            CHUNKS = C // ROWS

            def rows(first, n=1):
                return cost[:, bass.ds(first, n), :]

            @block.sync
            def _(sp):
                for c in range(CHUNKS):
                    if c >= 2:
                        sp.wait_ge(roots_ready, c - 1)
                    sp.dma_start(cost[:, 1 + c * ROWS:1 + (c + 1) * ROWS, 1:S + 1],
                                 dist_dram[:, c * ROWS:(c + 1) * ROWS, :]).then_inc(dist_loaded[c % 2], 16)
                for c in reversed(range(CHUNKS)):
                    sp.wait_ge(path_ready, ROWS * (CHUNKS - c) + 1)
                    sp.dma_start(path_dram[:, c * ROWS:(c + 1) * ROWS, :],
                                 cost[:, 1 + c * ROWS:1 + (c + 1) * ROWS, 1:S + 1]).then_inc(path_stored, 16)
                sp.wait_ge(path_stored, 16 * CHUNKS)

            @block.scalar
            def _(act):
                for c in range(CHUNKS):
                    act.wait_ge(dist_loaded[c % 2], 16 * (c // 2 + 1))
                    part = cost[:, 1 + c * ROWS:1 + (c + 1) * ROWS, 1:S + 1]
                    act.activation(part, part, ACT.Sqrt).then_inc(roots_ready, 1)
                act.sem_inc(path_ready, 1)
                with act.Fori(0, CHUNKS) as c:
                    for u in range(ROWS):
                        here = rows(c * (-ROWS) + (C - u))
                        act.wait_ge(on_ready, c * ROWS + (u + 1))
                        act.activation(flat(here[:, :, 1:S + 1]), on[:], ACT.Copy).then_inc(path_ready, 1)

            @block.vector
            def _(dve):
                dve.memset(cost[:, 0, :], BIG).then_inc(dtw_step, 1)
                dve.memset(cost[:, 1:C + 1, 0:1], BIG).then_inc(dtw_step, 1)
                dve.memset(left[:, S:S + 1], 0.0).then_inc(dtw_step, 1)
                dve.memset(leave_diag[:, S:S + 1], 0.0).then_inc(dtw_step, 1)
                dve.memset(enter[:], 0.0).then_inc(dtw_step, 1)
                dve.wait_ge(dtw_step, 5)
                dve.memset(enter[:, S - 1:S], 1.0).then_inc(dtw_step, 1)
                dve.memset(cost[:, 0, 0:1], 0.0).then_inc(dtw_step, 1)
                dve.wait_ge(dtw_step, 7)
                with dve.Fori(0, CHUNKS) as c:
                    dve.wait_ge(roots_ready, c + 1)
                    for u in range(ROWS):
                        above, here = rows(c * ROWS + u), rows(c * ROWS + (u + 1))
                        n = c * (2 * ROWS) + (7 + 2 * u)
                        dve.tensor_tensor(low[:], flat(above[:, :, 0:S]), flat(above[:, :, 1:S + 1]),
                                          ALU.min).then_inc(dtw_step, 1)
                        dve.wait_ge(dtw_step, n + 1)
                        dve.tensor_tensor_scan(flat(here[:, :, 1:S + 1]), low[:], flat(here[:, :, 1:S + 1]), BIG,
                                               ALU.min, ALU.add).then_inc(dtw_step, 1)
                        dve.wait_ge(dtw_step, n + 2)
                first = 7 + 2 * C
                with dve.Fori(0, CHUNKS) as c:
                    for u in range(ROWS):
                        i = c * (-ROWS) + (C - 1 - u)
                        above, here = rows(i), rows(i + 1)
                        n = c * (6 * ROWS) + (first + 6 * u)
                        up, dg = flat(above[:, :, 1:S + 1]), flat(above[:, :, 0:S])
                        dve.tensor_tensor(diag[:], dg, up, ALU.is_le)
                        dve.tensor_tensor(low[:], dg, up, ALU.min).then_inc(dtw_step, 1)
                        dve.wait_ge(dtw_step, n + 1)
                        dve.tensor_tensor(left[:, 0:S], flat(here[:, :, 0:S]), low[:], ALU.is_lt).then_inc(dtw_step, 1)
                        dve.wait_ge(dtw_step, n + 2)
                        dve.wait_ge(path_ready, c * ROWS + (u + 1))
                        dve.tensor_tensor_scan(on[:, ::-1], left[:, S:0:-1], enter[:, ::-1], 0.0,
                                               ALU.mult, ALU.add).then_inc(on_ready, 1)
                        dve.wait_ge(on_ready, c * ROWS + (u + 1))
                        dve.tensor_tensor(leave[:], on[:], left[:, 0:S], ALU.is_gt).then_inc(dtw_step, 1)
                        dve.wait_ge(dtw_step, n + 3)
                        dve.tensor_tensor(leave_diag[:, 0:S], leave[:], diag[:], ALU.mult).then_inc(dtw_step, 1)
                        dve.wait_ge(dtw_step, n + 4)
                        dve.tensor_tensor(leave_up[:], leave[:], leave_diag[:, 0:S], ALU.subtract).then_inc(dtw_step, 1)
                        dve.wait_ge(dtw_step, n + 5)
                        dve.tensor_tensor(enter[:], leave_up[:], leave_diag[:, 1:S + 1], ALU.add).then_inc(dtw_step, 1)
                        dve.wait_ge(dtw_step, n + 6)

        run("C", tokens_stored["C"])


def flat(ap):
    return ap.rearrange("p o n -> p (o n)")


SETUP_STEPS = 23



def chunked(wt):
    k, n = wt.shape
    return wt.reshape(k // P, P, n).transpose(1, 0, 2).reshape(P, k // P * n)


def layouts(a):
    nb = a["x"].shape[0]
    g = {}
    g["x"] = a["x"].reshape(nb, QT, P, D).transpose(0, 2, 1, 3).reshape(nb, P, QT * D)
    g["xT"] = a["x"].transpose(0, 2, 1).reshape(nb, FC, P, S).transpose(0, 2, 1, 3).reshape(nb, P, FC * S)
    g["ctxT"] = a["ctx_1024"].transpose(0, 2, 1).reshape(nb, FC, P, C).transpose(0, 2, 1, 3).reshape(nb, P, FC * C)
    g["ctx"] = a["ctx_1024"]
    qkv, qkv_b = a["L1_attn_qkv_w"], a["L1_attn_qkv_b"]
    square = {"A1_wq": a["L0_attn_Wq"], "A1_wk": a["L0_attn_Wk"], "A1_wv": a["L0_attn_Wv"],
              "A2_wq": a["L0_xattn_wq"], "A2_wk": a["L0_xattn_wk"], "A2_wv": a["L0_xattn_wv"],
              "A2_wo": a["L0_xattn_wo"],
              "A3_wq": qkv[0:D], "A3_wk": qkv[D:2 * D], "A3_wv": qkv[2 * D:3 * D], "A3_wo": a["L1_attn_proj_w"],
              "A4_wq": a["L1_ffn_Wq"], "A4_wk": a["L1_ffn_Wk"], "A4_wv": a["L1_ffn_Wv"], "A4_wo": a["L1_ffn_Wp"]}
    for n, m in square.items():
        g[n] = chunked(m.T)
    g.update(w_gate=chunked(a["L0_ffn_w_gate"].T), w_up=chunked(a["L0_ffn_w_up"].T),
             w_down=chunked(a["L0_ffn_w_down"].T))
    for n, b in (("A2_bq", a["L0_xattn_bq"]), ("A2_bk", a["L0_xattn_bk"]), ("A4_bk", a["L1_ffn_bk"])):
        g[n] = b.reshape(FC, P).T
    g.update(A2_bv=a["L0_xattn_bv"], A2_bo=a["L0_xattn_bo"], A3_bq=qkv_b[0:D], A3_bk=qkv_b[D:2 * D],
             A3_bv=qkv_b[2 * D:3 * D], A3_bo=a["L1_attn_proj_b"], A4_bq=a["L1_ffn_bq"], A4_bv=a["L1_ffn_bv"],
             A4_bo=a["L1_ffn_bp"])
    g["gate_w"] = chunked(np.concatenate([a["L1_ffn_Wr"], a["L1_ffn_Ws"]], axis=0).T)
    g["gate_b"] = np.concatenate([a["L1_ffn_br"], a["L1_ffn_bs"]])
    g["temperature"] = a["L1_ffn_temperature"].reshape(H)
    g["query_embedding"] = a["L1_ffn_query_embedding"].reshape(H * HD)
    g["ident"] = np.eye(P, dtype=np.float32)
    r = np.arange(P) % 32
    g["mask"] = np.stack([r < 16, r >= 16, r == 16, r == 0], axis=1).astype(np.float32)
    inv_freq = (1.0 / np.float32(10000.0) ** (np.arange(0, HD, 2, dtype=np.float32) / np.float32(HD))).astype(np.float32)
    freqs = np.arange(S, dtype=np.float32)[:, None] * inv_freq[None, :]
    emb = np.concatenate([freqs, freqs], axis=-1)
    sign = np.where(np.arange(HD) % 2 == 0, -1.0, 1.0).astype(np.float32)
    for n, t in (("rope_cos", np.cos(emb)), ("rope_sin", np.sin(emb) * sign)):
        g[n] = t.astype(np.float32).reshape(QT, P, HD).transpose(1, 0, 2).reshape(P, QT * HD)
    return {n: np.ascontiguousarray(v) for n, v in g.items()}, list(square)


def program(nc, arrays, square, nb):
    io = {n: nc.dram_tensor(f"in_{n}", v.shape, mybir.dt.from_np(v.dtype), kind="ExternalInput").ap()
          for n, v in arrays.items()}
    io["square_weights"] = square
    out = nc.dram_tensor("out_0", (nb, P, QT * D), F32, kind="ExternalOutput").ap()
    build(nc, nb, io, out)


def kernel(**inputs):
    import concourse.bacc as bacc
    from concourse.bass_utils import run_bass_kernel_spmd

    arrays, square = layouts({n: np.asarray(v) for n, v in inputs.items()})
    nb = arrays["x"].shape[0]
    nc = bacc.Bacc("TRN2", target_bir_lowering=False, num_devices=1)
    program(nc, arrays, square, nb)
    r = run_bass_kernel_spmd(nc, [{f"in_{n}": v for n, v in arrays.items()}], core_ids=[0])
    got = r.results[0]["out_0"]
    return got.reshape(nb, P, QT, D).transpose(0, 2, 1, 3).reshape(nb, S, D)
```

```python
from contextlib import ExitStack

import concourse.bass as bass
import numpy as np
from concourse import mybir

ALU = mybir.AluOpType
ACT = mybir.ActivationFunctionType
AX = mybir.AxisListType
F32 = mybir.dt.float32
BF16 = mybir.dt.bfloat16

P = 128
D = 256
S = 256
C = 77
H = 16
HD = D // H
FC = D // P
QT = S // P
HID = 1024
HC = HID // P
HALF = 512
VW = 32
EPS = 1e-5
MAGIC = 1.5 * 2.0 ** 23
QMAX = 127.0
BIG = 3.0e38
ROUTED = 3
RING = 6

KEYS = {"A1": S, "A2": C, "A3": S, "A4": S}
ALL_BIASES = ("A2_bq", "A2_bk", "A4_bk", "A2_bo", "A2_bv", "A3_bq", "A3_bk", "A3_bv", "A3_bo", "A4_bq", "A4_bv", "A4_bo")


def key_tiles(att):
    return [(k, min(P, KEYS[att] - k)) for k in range(0, KEYS[att], P)]


def place(h):
    return h // 8, 32 * (h % 8 // 2), h % 2




def slot_heads(att):
    return 2 // len(key_tiles(att))


def core_steps(att):
    return H // (2 * slot_heads(att))


def max_steps(att):
    return H // slot_heads(att)


def quads_before(att, p):
    return p * 2 * slot_heads(att) // 4




def before_core(att, s):
    steps = [("q", att, s), ("k", att, s), ("v", att, s)]
    if att == "A3":
        steps += [("rot", att, s), ("qT", att, s), ("kT", att, s)]
    if att == "A4":
        steps += [("rot", att, s), ("qT", att, s)]
    maxima = [("max", att, s, i) for i in range(max_steps(att))]
    if att == "A1":
        steps, maxima = steps[:2], maxima[:4] + steps[2:] + maxima[4:]
    steps += maxima
    return steps + [("shift", att, s, 0), ("shift", att, s, 1)]


def core(att, s):
    return [("core", att, s, p) for p in range(core_steps(att) + 1)] + [("take", att, s)]


def after_core(att, s):
    steps = [("norm", att, s, 0), ("norm", att, s, 1)]
    if att == "A4":
        steps += [("oT", att, s), ("gate", att, s), ("oproj", att, s)]
    elif att != "A1":
        steps += [("oT", att, s), ("oproj", att, s)]
    return steps + [("ln", att, s)]


def mlp(s):
    f = ("F", s)
    return [("fq",) + f, ("xqT",) + f, ("gu",) + f + (0, 0), ("gu",) + f + (0, 1), ("hq",) + f + (0,),
            ("gu",) + f + (1, 0), ("gu",) + f + (1, 1), ("hT",) + f + (0,), ("hq",) + f + (1,),
            ("hT",) + f + (1,), ("down",) + f, ("ln",) + f]


def entry(phase, s):
    if phase == "A":
        q2, k2, v2, *rest2 = before_core("A2", s)
        return (before_core("A1", s) + core("A1", s) + [k2, v2] + after_core("A1", s)
                + [("xT", "A1", s), q2] + rest2 + core("A2", s) + after_core("A2", s) + mlp(s)
                + [("xT", "F", s)] + before_core("A3", s) + core("A3", s) + after_core("A3", s)
                + [("store", "A3", s), ("xT", "A3", s), ("dist", "A3", s), ("store", "D", s)])
    return ([("expand", "E", s), ("ln", "E", s), ("xT", "E", s)] + before_core("A4", s) + core("A4", s)
            + after_core("A4", s) + [("store", "A4", s)])


ORDER = {
    "A": ("000000011001000001000100110011010101101001110011010101001010100010100110010010101010110000"
          "101000111010111011110111111111111101011001011101001010111101000011101110110101001001001100"
          "010011001011010111000101101011100110000110001110010001"),
    "C": ("1100110110110101001111111111010010010000001100100100100110110101100101100100001010111000"),
}
AHEAD = {"A": 76, "C": 7}


def orders(phase):
    cut = AHEAD[phase]
    even, odd = entry(phase, 0), entry(phase, 1)
    if phase == "A":
        even.insert(even.index(("norm", "A1", 0, 1)) + 1, ("load", "A", 0, "x"))
        even.append(("load", "A", 0, "ctx"))
        late = [("load", "A", 1, "x")] + odd[cut:] + [("load", "A", 1, "ctx")]
    else:
        even.insert(1, ("load", "C", 0, "x"))
        late = [("load", "C", 1, "x")] + odd[cut:]
    load_next = [step for step in even + late if step[0] == "load"]
    streams = [iter(even), iter(late + odd[:cut])]
    body = [next(streams[int(digit)]) for digit in ORDER[phase]]
    assert len(body) == len(even) + len(late) + cut
    ahead = set(odd[:cut])
    before = load_next + odd[:cut]
    after = [step for step in body if step not in ahead and step[0] != "load"]
    return before, body, after, ahead


def weighs(step):
    _, att, _, p = step
    return p > 0 and quads_before(att, p) > quads_before(att, p - 1)


def bank_uses(step):
    kind = step[0]
    if kind in ("q", "k", "v", "qT", "kT", "shift", "xT", "oT", "oproj", "xqT", "hT", "down",
                "norm", "dist", "expand", "gate"):
        return [step]
    if kind == "gu":
        return [step + ("gate",), step + ("up",)]
    return []


def signals(step):
    kind, att = step[0], step[1]
    if kind in ("load", "store"):
        return []
    token_q = att in ("A3", "A4")
    queries, keys = ["q_rounded", "q_ready"], ["k_rounded", "k_ready"]
    return {
        "q": ["q_tokens"] if token_q else queries,
        "k": ["q_tokens"] if att == "A3" else keys,
        "v": ["v_ready"],
        "rot": ["pool_step", "rotated", "dve_step", "k_rotated"] if att == "A3" else ["squared", "norms2"] + ["pool_step"] * 3
        + ["rotated"],
        "qT": queries,
        "kT": keys,
        "max": ["max_scores", "max_done"],
        "shift": ["q_shifted"],
        "core": ((["scores_ready", "probs_ready"] * 2 if step[-1] < core_steps(att) else [])
                 + ["weighted"] * weighs(step)) if kind == "core" else [],
        "take": ["out_taken"],
        "norm": ["dve_step", "normed"] + ["x_used"] * (att == "A1" and step[-1] == 1)
        + ["base_ready"] * (att != "A1" and step[-1] == 0),
        "oT": ["attnT_ready"],
        "gate": ["logits_taken", "dve_step", "logits_ready", "exps_ready"] + ["dve_step"] * 7,
        "oproj": ["proj_taken"],
        "ln": ["dve_step", "var_ready", "pool_step", "rstd_ready", "x_ready"],
        "xT": ["xT_ready"],
        "fq": ["dve_step"] * 8 + ["xq_ready"],
        "xqT": ["xqT_ready"],
        "gu": ["tanh_ready", "gated", "hid_ready"],
        "hq": ["dve_step"] * 6 + ["hq_ready"],
        "hT": ["hqT_ready"],
        "down": ["down_taken"],
        "dist": ["squares_ready", "dist_ready"],
        "expand": ["x4_used"],
    }[kind]


def emptied_by(use):
    kind, att = use[0], use[1]
    if kind == "gu":
        return "gated" if use[-1] == "gate" else "hid_ready"
    if kind == "q":
        return "q_tokens" if att in ("A3", "A4") else "q_ready"
    if kind == "k":
        return "q_tokens" if att == "A3" else "k_ready"
    return {"v": "v_ready", "qT": "q_ready", "kT": "k_ready", "shift": "q_shifted", "xT": "xT_ready",
            "norm": "normed", "oT": "attnT_ready", "oproj": "proj_taken", "xqT": "xqT_ready",
            "hT": "hqT_ready", "down": "down_taken", "dist": "dist_ready", "expand": "x4_used",
            "gate": "logits_taken"}[kind]


SIGNALS = sorted({x for p in "AC" for step in entry(p, 0) for x in signals(step)})


class Counts:

    def __init__(self, order):
        self.index = {step: n for n, step in enumerate(order)}
        self.at, self.per, self.bank, self.banks = {}, {x: 0 for x in SIGNALS}, {}, [0, 0]
        for step in order:
            seen = {}
            for x in signals(step):
                self.per[x] += 1
                self.at[x, step, seen.get(x, 0)] = self.at[x, step, -1] = self.per[x]
                seen[x] = seen.get(x, 0) + 1
        uses = [(use, step) for step in order for use in bank_uses(step)]
        for n, (use, step) in enumerate(uses):
            self.banks[n % 2] += 1
            self.bank[use] = (n % 2, self.banks[n % 2])
        self.before = {use: (uses[n - 2] if n >= 2 or len(uses) % 2 == 0 else None)
                       for n, (use, _) in enumerate(uses)}


def build(nc, nb, io, out):
    stack = ExitStack()
    with stack:
        def sem(name):
            return stack.enter_context(nc.semaphore(name))

        def sb(name, shape, dt=F32, where=stack):
            return where.enter_context(nc.sbuf_tensor(name, shape, dt))

        sems = {x: sem(x) for x in SIGNALS}
        bank_full = [sem("bank_full0"), sem("bank_full1")]
        consts_loaded, consts_ready = sem("consts_loaded"), sem("consts_ready")
        setup_dve, setup_act, setup_pe, setup_pool = (
            sem("setup_dve"), sem("setup_act"), sem("setup_pe"), sem("setup_pool"))
        inputs_loaded = {(p, n): [sem(f"inputs_loaded_{p}_{n}{s}") for s in range(2)]
                         for p, n in (("A", "x"), ("A", "ctx"), ("C", "x"))}
        tokens_stored = {p: [sem(f"tokens_stored_{p}{s}") for s in range(2)] for p in "AC"}
        dist_stored = [sem("dist_stored0"), sem("dist_stored1")]
        dist_loaded = [sem(f"dist_loaded{i}") for i in range(2)]
        roots_ready = sem("roots_ready")
        passed = sem("passed")
        on_ready = sem("on_ready")
        dtw_step, path_ready, path_stored = sem("dtw_step"), sem("path_ready"), sem("path_stored")

        pj = [stack.enter_context(nc.psum_tensor(f"pj{i}", [P, HALF], F32)) for i in range(2)]
        sm = [stack.enter_context(nc.psum_tensor(f"sm{i}", [P, HALF], F32)) for i in range(2)]
        st = [stack.enter_context(nc.psum_tensor(f"st{i}", [P, HALF], F32)) for i in range(2)]
        po = [stack.enter_context(nc.psum_tensor(f"po{i}", [P, HALF], F32)) for i in range(2)]

        x4_dram = nc.dram_tensor("x4_scratch", [nb, P, QT * D], F32, kind="Internal").ap()
        dist_dram = nc.dram_tensor("dist_scratch", [nb, C, S], F32, kind="Internal").ap()
        path_dram = nc.dram_tensor("path_scratch", [nb, C, S], F32, kind="Internal").ap()

        w = {n: sb(n, [P, FC, D]) for n in io["square_weights"]}
        row = {n: sb(n, [P, D]) for n in ALL_BIASES}
        gate_w = sb("gate_w", [P, FC, H + 1])
        gate_b = sb("gate_b", [P, H + 1])
        temp_sp = sb("temp_sp", [P, H])
        qe_sp = sb("qe_sp", [P, H, HD])
        wg, wu = sb("wg", [P, FC, HID], BF16), sb("wu", [P, FC, HID], BF16)
        wd = sb("wd", [P, HC, D], BF16)
        wq_inv = sb("wq_inv", [P, 3])
        ident, ident_b = sb("ident", [P, P]), sb("ident_b", [P, P], BF16)
        mask = sb("mask", [P, 4])
        rope_cos, rope_sin = sb("rope_cos", [P, QT, HD]), sb("rope_sin", [P, QT, HD])
        neg_half = sb("neg_half", [P, S])
        ones = sb("ones", [P, S])
        power = sb("power", [P, QT * H])

        def mask_col(i, n=P):
            return mask[0:n, i:i + 1]

        with ExitStack() as setup:
            wf = [sb(f"wf{i}", [P, 2048], F32, setup) for i in range(3)]
            wt = sb("wt", [P, 2048], F32, setup)
            small = sb("setup_small", [P, 16], F32, setup)
            spx = sb("spx", [P, 4, H], F32, setup)
            block = setup.enter_context(nc.Block())
            loads = [(wf[0][:], io["w_gate"]), (wf[1][:], io["w_up"]), (wf[2][:], io["w_down"])]
            loads += [(w[n][:].rearrange("p a b -> p (a b)"), io[n]) for n in w]
            loads += [(row[n][:], io[n][None, :].partition_broadcast(P).rearrange("p o d -> p (o d)"))
                      for n in row]
            loads += [(gate_w[:].rearrange("p a b -> p (a b)"), io["gate_w"]),
                      (gate_b[:], io["gate_b"][None, :].partition_broadcast(P).rearrange("p o d -> p (o d)")),
                      (temp_sp[:], io["temperature"][None, :].partition_broadcast(P).rearrange("p o d -> p (o d)")),
                      (qe_sp[:].rearrange("p h d -> p (h d)"),
                       io["query_embedding"][None, :].partition_broadcast(P).rearrange("p o d -> p (o d)")),
                      (ident[:], io["ident"]), (mask[:], io["mask"]),
                      (rope_cos[:].rearrange("p t d -> p (t d)"), io["rope_cos"]),
                      (rope_sin[:].rearrange("p t d -> p (t d)"), io["rope_sin"])]

            @block.sync
            def _(sp):
                for dst, src in loads:
                    sp.dma_start(dst, src).then_inc(consts_loaded, 16)

            @block.gpsimd
            def _(pool):
                pool.memset(neg_half[:], -0.5)
                pool.memset(ones[:], 1.0)
                pool.memset(power[:], -0.5).then_inc(setup_pool, 1)

            @block.tensor
            def _(pe):
                pe.wait_ge(setup_pool, 1)
                pe.wait_ge(setup_dve, 3)
                pe.matmul(pj[0][:, 0:3], ones[:, 0:P], small[:, 0:3], start=True,
                          stop=True).then_inc(setup_pe, 1)

            @block.scalar
            def _(act):
                act.wait_ge(consts_loaded, 16 * len(loads))
                act.activation(spx[:, 0, :], temp_sp[:], ACT.Abs).then_inc(setup_act, 1)
                act.wait_ge(setup_act, 1)
                act.activation(spx[:, 1, :], spx[:, 0, :], ACT.Exp, scale=-1.0).then_inc(setup_act, 1)
                act.wait_ge(setup_act, 2)
                act.activation(spx[:, 2, :], spx[:, 1, :], ACT.Ln, bias=1.0).then_inc(setup_act, 1)

            @block.vector
            def _(dve):
                done = [0]

                def link(ins):
                    done[0] += 1
                    ins.then_inc(setup_dve, 1)
                    dve.wait_ge(setup_dve, done[0])

                dve.wait_ge(consts_loaded, 16 * len(loads))
                for i in range(3):
                    link(dve.tensor_reduce(small[:, i:i + 1], wf[i][:], AX.X, ALU.add,
                                           apply_absolute_value=True))
                dve.wait_ge(setup_pe, 1)
                link(dve.tensor_scalar(small[:, 3:6], pj[0][:, 0:3], 1.0 / (HID * D), EPS, ALU.mult, ALU.max))
                link(dve.reciprocal(small[:, 6:9], small[:, 3:6]))
                link(dve.reciprocal(wq_inv[:], small[:, 6:9]))
                for i, q in enumerate((wg, wu, wd)):
                    flat = q[:].rearrange("p a b -> p (a b)")
                    link(dve.tensor_scalar(wt[:], wf[i][:], small[:, 6 + i:7 + i], MAGIC, ALU.mult, ALU.add))
                    link(dve.tensor_scalar(wt[:], wt[:], MAGIC, 1.0, ALU.subtract, ALU.min))
                    link(dve.tensor_scalar(flat, wt[:], -1.0, None, ALU.max))
                link(dve.tensor_copy(ident_b[:], ident[:]))
                dve.wait_ge(setup_act, 3)
                link(dve.tensor_scalar(spx[:, 3, :], temp_sp[:], 0.0, None, ALU.max))
                link(dve.tensor_tensor(temp_sp[:], spx[:, 3, :], spx[:, 2, :], ALU.add))
                link(dve.tensor_tensor(qe_sp[:], qe_sp[:], temp_sp[:].unsqueeze(2).to_broadcast([P, H, HD]),
                                       ALU.mult))

        def both(phase, name, shape, dt, where):
            return [sb(f"{phase}{name}_{s}", shape, dt, where) for s in range(2)]

        class Tiles:

            def __init__(self, phase, where):
                def two(name, shape, dt=F32):
                    return both(phase, name, shape, dt, where)

                self.x0, self.x = two("x0", [P, QT, D]), two("x", [P, QT, D])
                self.kz = [[two(f"k{e}{g}", [P, FC, S]) for g in range(4)] for e in range(2)]
                self.qe = [two(f"q{e}", [P, FC, S]) for e in range(2)]
                self.kb = two("kb", [P, FC, S], BF16)
                self.qb = [two(f"qb{e}", [P, FC, S], BF16) for e in range(2)]
                self.vv = two("v", [P, QT, H, VW])
                self.qk, self.qr = two("qk", [P, 2, QT, D]), two("qr", [P, 2, QT, D])
                self.r2 = two("r2", [P, QT, D])
                self.mp = two("mp", [P, QT, 2, FC, P])
                self.xT = two("xT", [P, FC, S])
                self.outT = two("outT", [P, H // 4, S])
                self.rc = two("rc", [P, QT, H])
                self.at, self.atT, self.res = two("at", [P, QT, D]), two("atT", [P, FC, S]), two("res", [P, QT, D])
                self.stats, self.mv = two("stats", [P, QT, 6]), two("mv", [P, QT, 2])
                self.ve, self.rstd = two("ve", [P, QT, 2]), two("rstd", [P, QT, 2])
                self.pr = [sb(f"{phase}pr{i}", [P, QT, S], F32, where) for i in range(RING)]
                if phase == "A":
                    self.x0T, self.ctxT = two("x0T", [P, FC, S]), two("ctxT", [P, FC, C])
                    self.csq, self.xsq = two("csq", [P, FC, C]), two("xsq", [P, FC, S])
                    self.dist = two("dist", [C, S])
                    self.xq, self.xqT = two("xq", [P, QT, D], BF16), two("xqT", [P, FC, S], BF16)
                    self.hq = two("hq", [P, HID], BF16)
                    self.qsc = two("qsc", [P, QT, 16])
                    self.th = [t[:].rearrange("p i t d -> p i (t d)") for t in self.qk]
                    self.hid = [t[:].rearrange("p i t d -> p i (t d)") for t in self.qr]
                    self.xq_f = self.r2
                    self.hqT = [t[:].rearrange("p g n -> p (g n)").bitcast(BF16).rearrange(
                        "p (t j n) -> p t j n", t=QT, j=HC) for t in self.outT]
                else:
                    self.path, self.ctx = two("path", [C, S]), two("ctx", [C, D])
                    self.sq, self.nrm = two("sq", [P, QT * H, HD]), two("nrm", [P, 2, QT, H])
                    self.lg, self.ex = two("lg", [P, QT, H + 1]), two("ex", [P, QT, H + 1])
                    self.top, self.gs = two("top", [P, QT, 8]), two("gs", [P, 16, QT])

        def segment(phase, tiles, order, passes, ordinal, base, where, last):
            counts = Counts(order)
            assert passes == 1 or counts.banks[0] == counts.banks[1]
            x0, x, vv, kb, qb = tiles.x0, tiles.x, tiles.vv, tiles.kb, tiles.qb
            qk, qr, r2, mp, xT, outT = tiles.qk, tiles.qr, tiles.r2, tiles.mp, tiles.xT, tiles.outT
            rc, at, atT, res, stats, mv = tiles.rc, tiles.at, tiles.atT, tiles.res, tiles.stats, tiles.mv
            ve, rstd, pr, kz, qe = tiles.ve, tiles.rstd, tiles.pr, tiles.kz, tiles.qe
            if phase == "A":
                x0T, ctxT, csq, xsq, dist = tiles.x0T, tiles.ctxT, tiles.csq, tiles.xsq, tiles.dist
                xq, xqT, hq, qsc, th, hid = tiles.xq, tiles.xqT, tiles.hq, tiles.qsc, tiles.th, tiles.hid
                xq_f, hqT = tiles.xq_f, tiles.hqT
            else:
                path, ctx, sq, nrm = tiles.path, tiles.ctx, tiles.sq, tiles.nrm
                lg, ex, top, gs = tiles.lg, tiles.ex, tiles.top, tiles.gs
            block = where.enter_context(nc.Block())

            class Clock:

                def __init__(self, eng, it):
                    self.eng, self.it, self.step, self.seen = eng, it, None, {}

                def wait(self, name, step, nth=-1, behind=0):
                    if step not in counts.index:
                        return
                    k = counts.at[name, step, nth] - behind
                    if counts.index[step] <= counts.index[self.step]:
                        k += counts.per[name]
                    elif passes == 1:
                        return
                    self.eng.wait_ge(sems[name], self.it * counts.per[name] + (base[name] + k))

                def tell(self, ins, name, step):
                    n = self.seen.get((name, step), 0)
                    assert (name, step, n) in counts.at, (name, step, n)
                    self.seen[name, step] = n + 1
                    self.seen[name] = self.seen.get(name, 0) + 1
                    assert self.seen[name] == counts.at[name, step, n], (name, step)
                    ins.then_inc(sems[name], 1)

                def link(self, ins, name):
                    step = self.step
                    n = self.seen.get((name, step), 0)
                    self.tell(ins, name, step)
                    self.wait(name, step, nth=n)

                def bank(self, use):
                    return pj[counts.bank[use][0]]

                def wait_bank_full(self, use):
                    b, k = counts.bank[use]
                    self.eng.wait_ge(bank_full[b], self.it * counts.banks[b] + (base["bank"][b] + k))

                def wait_bank_free(self, use):
                    if counts.before[use] is not None:
                        before, step = counts.before[use]
                        self.wait(emptied_by(before), step)

                def filled(self, ins, use):
                    ins.then_inc(bank_full[counts.bank[use][0]], 1)

                def stored(self, semaphore, step):
                    self.eng.wait_ge(semaphore, ordinal(step, self.it) * 16 + 16)

            def walk(eng, do):
                if passes > 1:
                    with eng.Fori(0, passes) as it:
                        ck = Clock(eng, it)
                        for step in order:
                            ck.step = step
                            do(ck, step)
                else:
                    ck = Clock(eng, 0)
                    for step in order:
                        ck.step = step
                        do(ck, step)

            def alone(eng):
                eng.sem_inc(passed, 1)

            def rotate(eng, dst, src, tmp, link, tell):
                dst, src, tmp = (t.rearrange("p t (h d) -> p t h d", h=H) for t in (dst, src, tmp))
                cos = rope_cos[:].unsqueeze(2).to_broadcast([P, QT, H, HD])
                sin = rope_sin[:].unsqueeze(2).to_broadcast([P, QT, H, HD])
                eng.tensor_tensor(dst, src, cos, ALU.mult)
                eng.tensor_tensor(tmp[:, :, :, 0::2], src[:, :, :, 1::2], sin[:, :, :, 0::2], ALU.mult)
                link(eng.tensor_tensor(tmp[:, :, :, 1::2], src[:, :, :, 0::2], sin[:, :, :, 1::2], ALU.mult))
                tell(eng.tensor_tensor(dst, dst, tmp, ALU.add))

            @block.sync
            def _(sp):
                def one(dram, b):
                    part = dram[b:b + 1] if isinstance(b, int) else dram[bass.ds(b, 1)]
                    return part.rearrange("o p n -> p o n")

                def do(ck, step):
                    kind, what, s = step[:3]
                    b = ordinal(step, ck.it) * 2 + s
                    if kind == "load":
                        if phase == "C":
                            ck.wait("x4_used", ("expand", "E", s))
                            moves = [(path[s][:], path_dram), (ctx[s][:], io["ctx"]),
                                     (x0[s][:].rearrange("p a b -> p (a b)"), x4_dram)]
                        elif step[3] == "x":
                            ck.wait("x_used", ("norm", "A1", s, 1))
                            moves = [(x0T[s][:].rearrange("p a b -> p (a b)"), io["xT"]),
                                     (x0[s][:].rearrange("p a b -> p (a b)"), io["x"])]
                        else:
                            ck.wait("dist_ready", ("dist", "A3", s))
                            moves = [(ctxT[s][:].rearrange("p a b -> p (a b)"), io["ctxT"])]
                        for dst, src in moves:
                            sp.dma_start(dst.unsqueeze(1), one(src, b)).then_inc(inputs_loaded[phase, step[3]][s], 16)
                    elif what == "D":
                        ck.wait("dist_ready", ("dist", "A3", s))
                        sp.dma_start(one(dist_dram, b), dist[s][:].unsqueeze(1)).then_inc(dist_stored[s], 16)
                    else:
                        ck.wait("x_ready", ("ln", what, s))
                        sp.dma_start(one(x4_dram if phase == "A" else out, b),
                                     x[s][:].rearrange("p a b -> p (a b)").unsqueeze(1)).then_inc(
                                         tokens_stored[phase][s], 16)

                walk(sp, lambda ck, step: do(ck, step) if step[0] in ("load", "store") else None)
                if last:
                    for s in range(2):
                        sp.wait_ge(tokens_stored[phase][s], 16 * (nb // 2 + 1))
                        if phase == "A":
                            sp.wait_ge(dist_stored[s], 16 * (nb // 2 + 1))

            @block.tensor
            def _(pe):
                def features(ck, step, weight, src, n, bias):
                    bank = ck.bank(step)
                    ck.wait_bank_free(step)
                    for c in range(FC):
                        if bias is not None:
                            pe.matmul(bank[:, c * S:c * S + n], bias[0:1, c * P:(c + 1) * P], ones[0:1, 0:n],
                                      start=True, stop=False)
                        for f in range(FC):
                            ins = pe.matmul(bank[:, c * S:c * S + n], weight[:, f, c * P:(c + 1) * P],
                                            src[:, f, 0:n], start=(f == 0 and bias is None), stop=(f == FC - 1))
                    ck.filled(ins, step)

                def tokens(ck, step, weight, src, tiles):
                    bank = ck.bank(step)
                    ck.wait_bank_free(step)
                    for t, (k, n) in enumerate(tiles):
                        for f in range(FC):
                            ins = pe.matmul(bank[0:n, t * D:(t + 1) * D], src[:, f, k:k + n],
                                            weight[:, f, :], start=(f == 0), stop=(f == FC - 1))
                    ck.filled(ins, step)

                def turn(ck, step, src, ident_, dt=F32):
                    bank = ck.bank(step)[:] if dt == F32 else ck.bank(step)[:].bitcast(BF16)
                    ck.wait_bank_free(step)
                    for f in range(FC):
                        for t in range(QT):
                            ins = pe.transpose(bank[:, f * S + t * P:f * S + (t + 1) * P],
                                               src[:, t, f * P:(f + 1) * P], ident_)
                    ck.filled(ins, step)

                def loaded(ck, step, what, dmas):
                    pe.wait_ge(inputs_loaded[phase, what][step[2]], ordinal(step, ck.it) * (16 * dmas) + 16 * dmas)

                def scores(ck, att, s, p):
                    parts = [(hh, k, n) for hh in range(slot_heads(att)) for k, n in key_tiles(att)]
                    for j in range(2):
                        if p > 0:
                            ck.wait("probs_ready", ("core", att, s, p - 1), nth=j)
                        for i, (hh, k, n) in enumerate(parts):
                            c, p0, e = place((2 * p + j) * slot_heads(att) + hh)
                            ins = pe.matmul(st[j][0:n, i * S:(i + 1) * S], kz[e][p0 // 32][s][:, c, k:k + n],
                                            qe[e][s][:, c, :], start=True, stop=True)
                        ck.tell(ins, "scores_ready", ("core", att, s, p))

                def weighted_values(ck, att, s, p):
                    quad, tiles_ = quads_before(att, p) - 1, key_tiles(att)
                    ck.wait("probs_ready", ("core", att, s, p - 1))
                    if quad == 0:
                        ck.wait("out_taken", ("take", att, s), behind=1)
                        ck.wait("v_ready", ("v", att, s))
                    for i, (k, n) in enumerate(tiles_):
                        for h in range(4 * quad, 4 * quad + 4):
                            slot, hh = divmod(h, slot_heads(att))
                            r = 32 * (h % 4)
                            ins = pe.matmul(po[quad // 2][r:r + VW, quad % 2 * S:(quad % 2 + 1) * S],
                                            vv[s][0:n, i, h, :], pr[slot % RING][0:n, max(i, hh), :], start=(i == 0),
                                            stop=(i == len(tiles_) - 1), skip_group_check=True)
                    ck.tell(ins, "weighted", ("core", att, s, p))

                def do(ck, step):
                    kind, att, s = step[:3]
                    if kind in ("q", "k", "v"):
                        if att == "A1":
                            src = x0T[s]
                            if kind == "q":
                                loaded(ck, step, "x", 2)
                        elif att == "A2" and kind != "q":
                            src = ctxT[s]
                            if kind == "k":
                                loaded(ck, step, "ctx", 1)
                        else:
                            src = xT[s]
                            before = {"A2": ("xT", "A1", s), "A3": ("xT", "F", s), "A4": ("xT", "E", s)}[att]
                            if kind == "q":
                                ck.wait("xT_ready", before)
                        weight = w[f"{att}_w{kind}"]
                        if kind == "v" or att == "A3" or (att == "A4" and kind == "q"):
                            tiles = key_tiles(att) if kind != "q" else [(0, P), (P, P)]
                            tokens(ck, step, weight, src, tiles)
                        else:
                            features(ck, step, weight, src, S if kind == "q" else KEYS[att], row.get(f"{att}_b{kind}"))
                    elif kind == "qT":
                        ck.wait("rotated", ("rot", att, s))
                        turn(ck, step, qr[s][:, 0], ident[:])
                    elif kind == "kT":
                        ck.wait("k_rotated", ("rot", att, s))
                        turn(ck, step, qr[s][:, 1], ident[:])
                    elif kind == "max":
                        i, m, n = step[3], slot_heads(att), KEYS[att]
                        if i == 0:
                            q_step = ("q", att, s) if att in ("A1", "A2") else ("qT", att, s)
                            k_step = ("kT", att, s) if att == "A3" else ("k", att, s)
                            ck.wait("q_rounded", q_step)
                            ck.wait("k_rounded", k_step)
                        ck.wait("max_done", step, behind=2)
                        bank = sm[counts.at["max_scores", step, -1] % 2]
                        for hh in range(m):
                            c, p0, e = place(m * i + hh)
                            for t in range(QT):
                                first = (QT * hh + t) * S // m
                                ins = pe.matmul(bank[:, first:first + n], qb[e][s][p0:p0 + 32, c, t * P:(t + 1) * P],
                                                kb[s][p0:p0 + 32, c, 0:n], start=True, stop=True)
                        ck.tell(ins, "max_scores", step)
                    elif kind == "shift":
                        e = step[3]
                        if e == 0:
                            ck.wait("max_done", ("max", att, s, max_steps(att) - 1))
                        ck.wait_bank_free(step)
                        for c in range(FC):
                            for t in range(QT):
                                ins = pe.transpose(ck.bank(step)[:, c * S + t * P:c * S + (t + 1) * P],
                                                   mp[s][:, t, e, c, :], ident[:])
                        ck.filled(ins, step)
                    elif kind == "core":
                        p = step[3]
                        if p == 0:
                            ck.wait("q_shifted", ("shift", att, s, 1))
                            ck.wait("k_ready", ("kT" if att == "A3" else "k", att, s))
                        if p < core_steps(att):
                            scores(ck, att, s, p)
                        if weighs(step):
                            weighted_values(ck, att, s, p)
                    elif kind == "norm":
                        t = step[3]
                        if t == 0:
                            ck.wait("out_taken", ("take", att, s))
                        ck.wait_bank_free(step)
                        for g in range(H // 4):
                            ins = pe.transpose(ck.bank(step)[:, g * P:(g + 1) * P], outT[s][:, g, t * P:(t + 1) * P],
                                               ident[:])
                        ck.filled(ins, step)
                    elif kind == "oT":
                        ck.wait("normed", ("norm", att, s, 1))
                        turn(ck, step, at[s][:], ident[:])
                    elif kind == "oproj":
                        if att != "A4":
                            ck.wait("attnT_ready", ("oT", att, s))
                        tokens(ck, step, w[f"{att}_wo"], atT[s], [(0, P), (P, P)])
                    elif kind == "xT":
                        ck.wait("x_ready", ("ln", att, s))
                        turn(ck, step, x[s][:], ident[:])
                    elif kind == "xqT":
                        ck.wait("xq_ready", ("fq", att, s))
                        turn(ck, step, xq[s][:], ident_b[:], BF16)
                    elif kind == "gu":
                        t, half = step[3:]
                        if (t, half) == (0, 0):
                            ck.wait("xqT_ready", ("xqT", att, s))
                        for name, wt_ in (("gate", wg), ("up", wu)):
                            use = step + (name,)
                            ck.wait_bank_free(use)
                            for f in range(FC):
                                ins = pe.matmul(ck.bank(use)[:], xqT[s][:, f, t * P:(t + 1) * P],
                                                wt_[:, f, half * HALF:(half + 1) * HALF],
                                                start=(f == 0), stop=(f == FC - 1))
                            ck.filled(ins, use)
                    elif kind == "hT":
                        t = step[3]
                        ck.wait("hq_ready", ("hq", att, s, t))
                        bank = ck.bank(step)[:].bitcast(BF16)
                        ck.wait_bank_free(step)
                        for j in range(HC):
                            ins = pe.transpose(bank[:, j * P:(j + 1) * P], hq[s][:, j * P:(j + 1) * P], ident_b[:])
                        ck.filled(ins, step)
                    elif kind == "down":
                        ck.wait("hqT_ready", ("hT", att, s, QT - 1))
                        ck.wait_bank_free(step)
                        for t in range(QT):
                            for j in range(HC):
                                ins = pe.matmul(ck.bank(step)[:, t * D:(t + 1) * D], hqT[s][:, t, j, :], wd[:, j, :],
                                                start=(j == 0), stop=(j == HC - 1))
                        ck.filled(ins, step)
                    elif kind == "dist":
                        ck.wait("xT_ready", ("xT", att, s))
                        ck.wait("squares_ready", step)
                        ck.wait_bank_free(step)
                        for i in range(3):
                            for f in range(FC):
                                lhs = (ctxT[s][:, f, :], neg_half[:, 0:C], csq[s][:, f, :])[i]
                                rhs = (xT[s][:, f, :], xsq[s][:, f, :], neg_half[:])[i]
                                ins = pe.matmul(ck.bank(step)[0:C, 0:S], lhs, rhs,
                                                start=(i == 0 and f == 0), stop=(i == 2 and f == FC - 1))
                        ck.filled(ins, step)
                    elif kind == "expand":
                        loaded(ck, step, "x", 3)
                        ck.wait_bank_free(step)
                        for t in range(QT):
                            ins = pe.matmul(ck.bank(step)[:, t * D:(t + 1) * D], path[s][:, t * P:(t + 1) * P],
                                            ctx[s][:], start=True, stop=True)
                        ck.filled(ins, step)
                    elif kind == "gate":
                        ck.wait("attnT_ready", ("oT", att, s))
                        ck.wait_bank_free(step)
                        for t in range(QT):
                            for f in range(FC):
                                ins = pe.matmul(ck.bank(step)[:, t * (H + 1):(t + 1) * (H + 1)],
                                                atT[s][:, f, t * P:(t + 1) * P], gate_w[:, f, :],
                                                start=(f == 0), stop=(f == FC - 1))
                        ck.filled(ins, step)

                walk(pe, do)

            @block.scalar
            def _(act):
                def put_queries(ck, step, att):
                    s = step[2]
                    ck.wait_bank_full(step)
                    bank = ck.bank(step)[:].rearrange("p (c n) -> p c n", c=FC)
                    for dst, signal in ((qb, "q_rounded"), (qe, "q_ready")):
                        for e in range(2):
                            ins = act.activation(dst[e][s][:], bank, ACT.Copy, scale=mask_col(e))
                        ck.tell(ins, signal, step)

                def put_keys(ck, step, att):
                    s = step[2]
                    ck.wait_bank_full(step)
                    n = KEYS[att]
                    bank = ck.bank(step)[:].rearrange("p (c n) -> p c n", c=FC)
                    ck.tell(act.activation(kb[s][:, :, 0:n], bank[:, :, 0:n], ACT.Copy), "k_rounded", step)
                    for g in range(4):
                        r = slice(32 * g, 32 * g + 32)
                        for e in range(2):
                            ins = act.activation(kz[e][g][s][r, :, 0:n], bank[r, :, 0:n], ACT.Identity,
                                                 scale=mask[r, e:e + 1], bias=mask[r, 2 + e:3 + e])
                    ck.tell(ins, "k_ready", step)

                def do(ck, step):
                    kind, att, s = step[:3]
                    if kind == "q" and att in ("A1", "A2") or kind == "qT":
                        put_queries(ck, step, att)
                    elif kind == "k" and att != "A3" or kind == "kT":
                        put_keys(ck, step, att)
                    elif kind == "core" and step[3] < core_steps(att):
                        n = key_tiles(att)[0][1]
                        for j in range(2):
                            ck.wait("scores_ready", step, nth=j)
                            dst = pr[(2 * step[3] + j) % RING][0:n].rearrange("p a b -> p (a b)")
                            ck.tell(act.activation(dst, st[j][0:n, :], ACT.Exp, scale=HD ** -0.5),
                                    "probs_ready", step)
                    elif kind == "take":
                        ck.wait("weighted", ("core", att, s, core_steps(att)))
                        for i in range(2):
                            ins = act.activation(outT[s][:, 2 * i:2 * i + 2].rearrange("p a b -> p (a b)"), po[i][:],
                                                 ACT.Copy)
                        ck.tell(ins, "out_taken", step)
                    elif kind in ("xT", "oT"):
                        dst, name = (xT[s], "xT_ready") if kind == "xT" else (atT[s], "attnT_ready")
                        ck.wait_bank_full(step)
                        ins = act.activation(dst[:].rearrange("p a b -> p (a b)"), ck.bank(step)[:], ACT.Copy)
                        ck.tell(ins, name, step)
                    elif kind == "xqT":
                        ck.wait_bank_full(step)
                        ins = act.activation(xqT[s][:].rearrange("p a b -> p (a b)"),
                                             ck.bank(step)[:].bitcast(BF16)[:, 0:FC * S], ACT.Copy)
                        ck.tell(ins, "xqT_ready", step)
                    elif kind == "gu":
                        t, half = step[3:]
                        use = step + ("gate",)
                        ck.wait_bank_full(use)
                        ins = act.activation(th[s][:, half, :], ck.bank(use)[:], ACT.Tanh, scale=qsc[s][:, t, 4:5])
                        ck.tell(ins, "tanh_ready", step)
                    elif kind == "hT":
                        t = step[3]
                        ck.wait_bank_full(step)
                        ins = act.activation(hqT[s][:, t].rearrange("p a b -> p (a b)"),
                                             ck.bank(step)[:].bitcast(BF16), ACT.Copy)
                        ck.tell(ins, "hqT_ready", step)
                    elif kind == "gate":
                        ck.wait("logits_ready", step)
                        ins = act.activation(ex[s][:], lg[s][:], ACT.Exp)
                        ck.tell(ins, "exps_ready", step)
                    else:
                        return

                walk(act, do)

            @block.gpsimd
            def _(pool):
                def link(ck, ins):
                    ck.link(ins, "pool_step")

                def do(ck, step):
                    kind, att, s = step[:3]
                    if kind == "rot" and att == "A3":
                        ck.wait("q_tokens", ("q", att, s))
                        rotate(pool, qr[s][:, 0], qk[s][:, 0], r2[s][:], lambda ins: link(ck, ins),
                               lambda ins: ck.tell(ins, "rotated", step))
                    elif kind == "rot" and att == "A4":
                        ck.wait("q_tokens", ("q", att, s))
                        src = qk[s][:, 0].rearrange("p t (h d) -> p (t h) d", h=H)
                        dst = qr[s][:, 0].rearrange("p t (h d) -> p (t h) d", h=H)
                        ck.tell(pool.tensor_tensor(sq[s][:], src, src, ALU.mult), "squared", step)
                        ck.wait("norms2", step)
                        link(ck, pool.tensor_tensor(nrm[s][:, 1].rearrange("p t h -> p (t h)"),
                                                    nrm[s][:, 0].rearrange("p t h -> p (t h)"), power[:], ALU.pow))
                        link(ck, pool.tensor_tensor(nrm[s][:, 0], nrm[s][:, 1],
                                                    temp_sp[:].unsqueeze(1).to_broadcast([P, QT, H]), ALU.mult))
                        link(ck, pool.tensor_tensor(
                            dst, src, nrm[s][:, 0].rearrange("p t h -> p (t h)").unsqueeze(2)
                            .to_broadcast([P, QT * H, HD]), ALU.mult))
                        qr4 = qr[s][:, 0].rearrange("p t (h d) -> p t (h d)", h=H)
                        emb = qe_sp[:].rearrange("p h d -> p (h d)").unsqueeze(1).to_broadcast([P, QT, D])
                        ck.tell(pool.tensor_tensor(qr4, qr4, emb, ALU.add), "rotated", step)
                    elif kind == "norm" and att != "A1" and step[3] == 0:
                        ck.wait("x_ready", ("ln", {"A2": "A1", "A3": "F", "A4": "E"}[att], s))
                        bias = row[att + "_bo"][:].unsqueeze(1).to_broadcast([P, QT, D])
                        ck.tell(pool.tensor_tensor(res[s][:], x[s][:], bias, ALU.add), "base_ready", step)
                    elif kind == "ln":
                        ck.wait("var_ready", step)
                        alone(pool)
                        link(ck, pool.tensor_scalar(ve[s][:, :, 0:1], mv[s][:, :, 1:2], EPS, None, ALU.add))
                        ck.tell(pool.tensor_tensor(rstd[s][:, :, 0:1], ve[s][:, :, 0:1],
                                                     power[:, 0:QT].unsqueeze(2), ALU.pow), "rstd_ready", step)
                    elif kind == "dist":
                        ck.wait("xT_ready", ("xT", att, s))
                        pool.tensor_tensor(xsq[s][:], xT[s][:], xT[s][:], ALU.mult)
                        ck.tell(pool.tensor_tensor(csq[s][:], ctxT[s][:], ctxT[s][:], ALU.mult),
                                  "squares_ready", step)

                walk(pool, do)

            @block.vector
            def _(dve):
                def link(ck, ins):
                    ck.link(ins, "dve_step")

                def do(ck, step):
                    kind, att, s = step[:3]
                    if kind in ("q", "k") and att == "A3" or kind == "q" and att == "A4":
                        i = "qk".index(kind)
                        ck.wait_bank_full(step)
                        bias = row[f"{att}_b{kind}"][:].unsqueeze(1).to_broadcast([P, QT, D])
                        ins = dve.tensor_tensor(qk[s][:, i], ck.bank(step)[:].rearrange("p (t d) -> p t d", t=QT),
                                                bias, ALU.add)
                        ck.tell(ins, "q_tokens", step)
                    elif kind == "rot" and att == "A3":
                        ck.wait("q_tokens", ("k", att, s))
                        rotate(dve, qr[s][:, 1], qk[s][:, 1], at[s][:], lambda ins: link(ck, ins),
                               lambda ins: ck.tell(ins, "k_rotated", step))
                    elif kind == "rot" and att == "A4":
                        ck.wait("squared", step)
                        ck.tell(dve.tensor_reduce(nrm[s][:, 0].rearrange("p t h -> p (t h)"), sq[s][:], AX.X, ALU.add),
                                  "norms2", step)
                    elif kind == "v":
                        ck.wait_bank_full(step)
                        tiles = key_tiles(att)
                        n, nt = tiles[0][1], len(tiles)
                        src = ck.bank(step)[0:n, 0:nt * D].rearrange("p (t h d) -> p t h d", t=nt, h=H)
                        for t in range(nt):
                            dst = vv[s][0:n, t, :, 0:HD]
                            if att == "A1":
                                ins = dve.tensor_copy(dst, src[:, t])
                            else:
                                bias = row[att + "_bv"][0:n].rearrange("p (h d) -> p h d", h=H)
                                ins = dve.tensor_tensor(dst, src[:, t], bias, ALU.add)
                        ck.tell(ins, "v_ready", step)
                    elif kind == "max":
                        m = slot_heads(att)
                        c, p0, e = place(m * step[3])
                        ck.wait("max_scores", step)
                        bank = sm[counts.at["max_scores", step, -1] % 2]
                        first, apart = e * D + c * P + p0 + 16 * (1 - e), D - 16
                        dst = mp[s][:].rearrange("p t e c n -> p t (e c n)")[:, :, first:first + apart * (m - 1) + 1:apart]
                        src = bank[:].rearrange("p (h t n) -> p t h n", h=m, t=QT)[:, :, :, 0:KEYS[att]]
                        ins = dve.tensor_reduce(dst, src, AX.X, ALU.max, negate=True)
                        ck.tell(ins, "max_done", step)
                    elif kind == "shift":
                        e = step[3]
                        ck.wait_bank_full(step)
                        if e == 0:
                            ck.wait("q_ready", ("q" if att in ("A1", "A2") else "qT", att, s))
                        queries = qe[e][s][:].rearrange("p c n -> p (c n)")
                        ins = dve.tensor_tensor(queries, queries, ck.bank(step)[:], ALU.add)
                        ck.tell(ins, "q_shifted", step)
                    elif kind == "norm":
                        t = step[3]
                        ck.wait_bank_full(step)
                        o = ck.bank(step)[:].rearrange("p (h w) -> p h w", h=H)
                        link(ck, dve.reciprocal(rc[s][:, t, :].unsqueeze(2), o[:, :, HD:HD + 1]))
                        ins = dve.tensor_tensor(at[s][:, t].rearrange("p (h d) -> p h d", h=H), o[:, :, 0:HD],
                                                rc[s][:, t, :].unsqueeze(2).to_broadcast([P, H, HD]), ALU.mult)
                        ck.tell(ins, "normed", step)
                        if att == "A1" and t == 1:
                            ck.wait("normed", step)
                            ck.tell(dve.tensor_tensor(res[s][:], x0[s][:], at[s][:], ALU.add), "x_used", step)
                    elif kind == "oproj":
                        ck.wait_bank_full(step)
                        bank = ck.bank(step)[:].rearrange("p (t d) -> p t d", t=QT)
                        ck.wait("base_ready", ("norm", att, s, 0))
                        if att == "A4":
                            for t in range(QT):
                                ins = dve.scalar_tensor_tensor(out=res[s][:, t], in0=bank[:, t], scalar=gs[s][:, 15, t:t + 1],
                                                               in1=res[s][:, t], op0=ALU.mult, op1=ALU.add)
                        else:
                            ins = dve.tensor_tensor(res[s][:], bank, res[s][:], ALU.add)
                        ck.tell(ins, "proj_taken", step)
                    elif kind == "expand":
                        ck.wait_bank_full(step)
                        ck.wait("x_ready", ("ln", "A4", s))
                        ins = dve.tensor_tensor(res[s][:], ck.bank(step)[:].rearrange("p (t d) -> p t d", t=QT),
                                                x0[s][:], ALU.add)
                        ck.tell(ins, "x4_used", step)
                    elif kind == "down":
                        ck.wait_bank_full(step)
                        bank = ck.bank(step)[:].rearrange("p (t d) -> p t d", t=QT)
                        for t in range(QT):
                            ins = dve.scalar_tensor_tensor(out=res[s][:, t], in0=bank[:, t], scalar=qsc[s][:, t, 10:11],
                                                           in1=x[s][:, t], op0=ALU.mult, op1=ALU.add)
                        ck.tell(ins, "down_taken", step)
                        ck.wait("down_taken", step)
                    elif kind == "ln":
                        if att == "A1":
                            ck.wait("x_used", ("norm", att, s, 1))
                        if att == "E":
                            ck.wait("x4_used", ("expand", att, s))
                        if att in ("A2", "A3", "A4"):
                            ck.wait("proj_taken", ("oproj", att, s))
                        for t in range(QT):
                            ins = dve.bn_stats(stats[s][:, t, :], res[s][:, t, :])
                        link(ck, ins)
                        alone(dve)
                        for t in range(QT):
                            ins = dve.bn_aggr(mv[s][:, t, :], stats[s][:, t, :])
                        ck.tell(ins, "var_ready", step)
                        ck.wait("rstd_ready", step)
                        if att == "A1":
                            ck.stored(tokens_stored[phase][s], step)
                        if att == "E":
                            ck.stored(tokens_stored[phase][s], step)
                        for t in range(QT):
                            ins = dve.tensor_scalar(x[s][:, t], res[s][:, t], mv[s][:, t, 0:1], rstd[s][:, t, 0:1],
                                                    ALU.subtract, ALU.mult)
                        ck.tell(ins, "x_ready", step)
                    elif kind == "fq":
                        ck.wait("x_ready", ("ln", "A2", s))
                        link(ck, dve.tensor_reduce(qsc[s][:, :, 0:1], x[s][:], AX.X, ALU.max, apply_absolute_value=True))
                        link(ck, dve.tensor_scalar(qsc[s][:, :, 1:2], qsc[s][:, :, 0:1], EPS, None, ALU.max))
                        link(ck, dve.reciprocal(qsc[s][:, :, 2:3], qsc[s][:, :, 1:2]))
                        link(ck, dve.tensor_scalar(qsc[s][:, :, 3:4], qsc[s][:, :, 2:3], QMAX, None, ALU.mult))
                        for t in range(QT):
                            ins = dve.tensor_scalar(xq_f[s][:, t], x[s][:, t], qsc[s][:, t, 3:4], MAGIC, ALU.mult, ALU.add)
                        link(ck, ins)
                        link(ck, dve.tensor_scalar(xq[s][:], xq_f[s][:], MAGIC, QMAX, ALU.subtract, ALU.min))
                        link(ck, dve.tensor_scalar(qsc[s][:, :, 4:5], qsc[s][:, :, 1:2], wq_inv[:, 0:1], 0.5 / QMAX,
                                                   ALU.mult, ALU.mult))
                        link(ck, dve.tensor_scalar(qsc[s][:, :, 5:6], qsc[s][:, :, 1:2], wq_inv[:, 1:2], 1.0 / QMAX,
                                                   ALU.mult, ALU.mult))
                        ck.tell(dve.tensor_tensor(qsc[s][:, :, 6:7], qsc[s][:, :, 4:5], qsc[s][:, :, 5:6], ALU.mult),
                                  "xq_ready", step)
                    elif kind == "gu":
                        t, half = step[3:]
                        g, u = step + ("gate",), step + ("up",)
                        ck.wait("tanh_ready", step)
                        if (t, half) == (1, 0):
                            ck.wait("hq_ready", ("hq", att, s, 0))
                        ins = dve.scalar_tensor_tensor(out=hid[s][:, half], in0=th[s][:, half], scalar=1.0,
                                                       in1=ck.bank(g)[:], op0=ALU.add, op1=ALU.mult)
                        ck.tell(ins, "gated", step)
                        ck.wait("gated", step)
                        ck.wait_bank_full(u)
                        ins = dve.tensor_tensor(hid[s][:, half], hid[s][:, half], ck.bank(u)[:], ALU.mult)
                        ck.tell(ins, "hid_ready", step)
                    elif kind == "hq":
                        t = step[3]
                        q = qsc[s][:, t]
                        ck.wait("hid_ready", ("gu", att, s, t, 1))
                        flat = hid[s][:].rearrange("p a b -> p (a b)")
                        link(ck, dve.tensor_reduce(q[:, 7:8], flat, AX.X, ALU.max, apply_absolute_value=True))
                        link(ck, dve.tensor_scalar(q[:, 8:9], q[:, 7:8], q[:, 6:7], EPS, ALU.mult, ALU.max))
                        link(ck, dve.reciprocal(q[:, 9:10], q[:, 8:9]))
                        link(ck, dve.tensor_scalar(q[:, 11:12], q[:, 9:10], q[:, 6:7], QMAX, ALU.mult, ALU.mult))
                        link(ck, dve.tensor_scalar(q[:, 10:11], q[:, 8:9], wq_inv[:, 2:3], 1.0 / QMAX,
                                                   ALU.mult, ALU.mult))
                        link(ck, dve.tensor_scalar(flat, flat, q[:, 11:12], MAGIC, ALU.mult, ALU.add))
                        if t > 0:
                            ck.wait("hqT_ready", ("hT", att, s, t - 1))
                        ck.tell(dve.tensor_scalar(hq[s][:], flat, MAGIC, QMAX, ALU.subtract, ALU.min), "hq_ready", step)
                        ck.wait("hq_ready", step)
                    elif kind == "dist":
                        ck.wait_bank_full(step)
                        ck.stored(dist_stored[s], step)
                        ins = dve.tensor_scalar(dist[s][:], ck.bank(step)[0:C, 0:S], -2.0, 0.0, ALU.mult, ALU.max)
                        ck.tell(ins, "dist_ready", step)
                    elif kind == "gate":
                        ck.wait_bank_full(step)
                        src = ck.bank(step)[:, 0:QT * (H + 1)].rearrange("p (t n) -> p t n", t=QT)
                        ins = (dve.tensor_tensor(lg[s][:], src, gate_b[:].unsqueeze(1).to_broadcast([P, QT, H + 1]),
                                                 ALU.add))
                        ck.tell(ins, "logits_taken", step)
                        ck.wait("logits_taken", step)
                        nr = H - 1
                        dve.tensor_reduce(gs[s][:, 0, :].unsqueeze(2), lg[s][:, :, 0:nr], AX.X, ALU.max)
                        link(ck, dve.tensor_reduce(gs[s][:, 1, :].unsqueeze(2), lg[s][:, :, nr:H + 1], AX.X, ALU.max))
                        dve.tensor_tensor(lg[s][:, :, 0:nr], lg[s][:, :, 0:nr],
                                          gs[s][:, 0, :].unsqueeze(2).to_broadcast([P, QT, nr]), ALU.subtract)
                        ck.tell(dve.tensor_tensor(lg[s][:, :, nr:H + 1], lg[s][:, :, nr:H + 1],
                                                    gs[s][:, 1, :].unsqueeze(2).to_broadcast([P, QT, 2]), ALU.subtract),
                                  "logits_ready", step)
                        ck.wait("exps_ready", step)
                        alone(dve)
                        for t in range(QT):
                            dve.max(top[s][:, t, :], ex[s][:, t, 0:nr])
                        dve.tensor_reduce(gs[s][:, 2, :].unsqueeze(2), ex[s][:, :, 0:nr], AX.X, ALU.add)
                        link(ck, dve.tensor_reduce(gs[s][:, 3, :].unsqueeze(2), ex[s][:, :, nr:H + 1], AX.X, ALU.add))
                        dve.tensor_reduce(gs[s][:, 4, :].unsqueeze(2), top[s][:, :, 0:ROUTED], AX.X, ALU.add)
                        dve.reciprocal(gs[s][:, 5, :], gs[s][:, 2, :])
                        link(ck, dve.reciprocal(gs[s][:, 6, :], gs[s][:, 3, :]))
                        e0, e1 = (ex[s][:, :, nr + i:nr + i + 1].rearrange("p t o -> p (t o)") for i in range(2))
                        dve.tensor_tensor(gs[s][:, 7, :], e0, gs[s][:, 6, :], ALU.mult)
                        dve.tensor_tensor(gs[s][:, 8, :], e1, gs[s][:, 6, :], ALU.mult)
                        link(ck, dve.tensor_tensor(gs[s][:, 9, :], gs[s][:, 4, :], gs[s][:, 5, :], ALU.mult))
                        dve.tensor_tensor(gs[s][:, 10, :], gs[s][:, 7, :], gs[s][:, 8, :], ALU.add)
                        link(ck, dve.tensor_tensor(gs[s][:, 11, :], gs[s][:, 8, :], gs[s][:, 9, :], ALU.mult))
                        dve.tensor_scalar(gs[s][:, 12, :], gs[s][:, 11, :], 2.0 * ROUTED, None, ALU.mult)
                        link(ck, dve.tensor_tensor(gs[s][:, 13, :], gs[s][:, 7, :], gs[s][:, 10, :], ALU.mult))
                        link(ck, dve.tensor_scalar(gs[s][:, 14, :], gs[s][:, 13, :], 2.0, None, ALU.mult))
                        link(ck, dve.tensor_tensor(gs[s][:, 15, :], gs[s][:, 14, :], gs[s][:, 12, :], ALU.add))

                walk(dve, do)

        pairs = nb // 2
        base = {x: 0 for x in SIGNALS}
        base["bank"] = [0, 0]

        def prime(start_counts, stored):
            with nc.Block() as start:
                @start.sync
                def _(sp):
                    for x in SIGNALS:
                        if start_counts.per[x]:
                            sp.sem_inc(sems[x], start_counts.per[x])
                    for x in stored:
                        sp.sem_inc(x, 16)

        def run(phase, stored):
            before, body, after, ahead = orders(phase)

            def in_body(step, it):
                return it + 1 if step in ahead or step[0] == "load" else it

            with ExitStack() as where:
                tiles = Tiles(phase, where)
                with nc.Block() as fixed:
                    @fixed.vector
                    def _(dve):
                        for s in range(2):
                            dve.memset(tiles.mp[s][:], 0.0)
                            for e in range(2):
                                for g in range(4):
                                    dve.memset(tiles.kz[e][g][s][:], 0.0)
                            dve.memset(tiles.vv[s][:, :, :, HD:HD + 1], 1.0)
                            dve.memset(tiles.vv[s][:, :, :, HD + 1:VW], 0.0)
                segments = [(before, 1, lambda step, it: 0)]
                if pairs > 1:
                    segments.append((body, pairs - 1, in_body))
                segments.append((after, 1, lambda step, it: pairs - 1))
                for n, (order, passes, ordinal) in enumerate(segments):
                    counts = Counts(order)
                    prime(counts, stored if n == 0 else [])
                    with ExitStack() as blocks:
                        segment(phase, tiles, order, passes, ordinal, base, blocks, n == len(segments) - 1)
                    for x in SIGNALS:
                        base[x] += counts.per[x] * (passes + 1)
                    base["bank"] = [base["bank"][i] + counts.banks[i] * passes for i in range(2)]

        run("A", tokens_stored["A"] + dist_stored)

        with ExitStack() as where:
            cost = sb("cost", [nb, C + 1, S + 1], F32, where)
            low = sb("low", [nb, S], F32, where)
            left = sb("left", [nb, S + 1], F32, where)
            diag = sb("diag", [nb, S], F32, where)
            on = sb("on", [nb, S], F32, where)
            enter = sb("enter", [nb, S], F32, where)
            leave = sb("leave", [nb, S], F32, where)
            leave_diag = sb("leave_diag", [nb, S + 1], F32, where)
            leave_up = sb("leave_up", [nb, S], F32, where)
            block = where.enter_context(nc.Block())
            ROWS = 7
            CHUNKS = C // ROWS

            def rows(first, n=1):
                return cost[:, bass.ds(first, n), :]

            @block.sync
            def _(sp):
                for c in range(CHUNKS):
                    if c >= 2:
                        sp.wait_ge(roots_ready, c - 1)
                    sp.dma_start(cost[:, 1 + c * ROWS:1 + (c + 1) * ROWS, 1:S + 1],
                                 dist_dram[:, c * ROWS:(c + 1) * ROWS, :]).then_inc(dist_loaded[c % 2], 16)
                for c in reversed(range(CHUNKS)):
                    sp.wait_ge(path_ready, ROWS * (CHUNKS - c) + 1)
                    sp.dma_start(path_dram[:, c * ROWS:(c + 1) * ROWS, :],
                                 cost[:, 1 + c * ROWS:1 + (c + 1) * ROWS, 1:S + 1]).then_inc(path_stored, 16)
                sp.wait_ge(path_stored, 16 * CHUNKS)

            @block.scalar
            def _(act):
                for c in range(CHUNKS):
                    act.wait_ge(dist_loaded[c % 2], 16 * (c // 2 + 1))
                    part = cost[:, 1 + c * ROWS:1 + (c + 1) * ROWS, 1:S + 1]
                    act.activation(part, part, ACT.Sqrt).then_inc(roots_ready, 1)
                act.sem_inc(path_ready, 1)
                with act.Fori(0, CHUNKS) as c:
                    for u in range(ROWS):
                        here = rows(c * (-ROWS) + (C - u))
                        act.wait_ge(on_ready, c * ROWS + (u + 1))
                        act.activation(flat(here[:, :, 1:S + 1]), on[:], ACT.Copy).then_inc(path_ready, 1)

            @block.vector
            def _(dve):
                dve.memset(cost[:, 0, :], BIG).then_inc(dtw_step, 1)
                dve.memset(cost[:, 1:C + 1, 0:1], BIG).then_inc(dtw_step, 1)
                dve.memset(left[:, S:S + 1], 0.0).then_inc(dtw_step, 1)
                dve.memset(leave_diag[:, S:S + 1], 0.0).then_inc(dtw_step, 1)
                dve.memset(enter[:], 0.0).then_inc(dtw_step, 1)
                dve.wait_ge(dtw_step, 5)
                dve.memset(enter[:, S - 1:S], 1.0).then_inc(dtw_step, 1)
                dve.memset(cost[:, 0, 0:1], 0.0).then_inc(dtw_step, 1)
                dve.wait_ge(dtw_step, 7)
                with dve.Fori(0, CHUNKS) as c:
                    dve.wait_ge(roots_ready, c + 1)
                    for u in range(ROWS):
                        above, here = rows(c * ROWS + u), rows(c * ROWS + (u + 1))
                        n = c * (2 * ROWS) + (7 + 2 * u)
                        dve.tensor_tensor(low[:], flat(above[:, :, 0:S]), flat(above[:, :, 1:S + 1]),
                                          ALU.min).then_inc(dtw_step, 1)
                        dve.wait_ge(dtw_step, n + 1)
                        dve.tensor_tensor_scan(flat(here[:, :, 1:S + 1]), low[:], flat(here[:, :, 1:S + 1]), BIG,
                                               ALU.min, ALU.add).then_inc(dtw_step, 1)
                        dve.wait_ge(dtw_step, n + 2)
                first = 7 + 2 * C
                with dve.Fori(0, CHUNKS) as c:
                    for u in range(ROWS):
                        i = c * (-ROWS) + (C - 1 - u)
                        above, here = rows(i), rows(i + 1)
                        n = c * (6 * ROWS) + (first + 6 * u)
                        up, dg = flat(above[:, :, 1:S + 1]), flat(above[:, :, 0:S])
                        dve.tensor_tensor(diag[:], dg, up, ALU.is_le)
                        dve.tensor_tensor(low[:], dg, up, ALU.min).then_inc(dtw_step, 1)
                        dve.wait_ge(dtw_step, n + 1)
                        dve.tensor_tensor(left[:, 0:S], flat(here[:, :, 0:S]), low[:], ALU.is_lt).then_inc(dtw_step, 1)
                        dve.wait_ge(dtw_step, n + 2)
                        dve.wait_ge(path_ready, c * ROWS + (u + 1))
                        dve.tensor_tensor_scan(on[:, ::-1], left[:, S:0:-1], enter[:, ::-1], 0.0,
                                               ALU.mult, ALU.add).then_inc(on_ready, 1)
                        dve.wait_ge(on_ready, c * ROWS + (u + 1))
                        dve.tensor_tensor(leave[:], on[:], left[:, 0:S], ALU.is_gt).then_inc(dtw_step, 1)
                        dve.wait_ge(dtw_step, n + 3)
                        dve.tensor_tensor(leave_diag[:, 0:S], leave[:], diag[:], ALU.mult).then_inc(dtw_step, 1)
                        dve.wait_ge(dtw_step, n + 4)
                        dve.tensor_tensor(leave_up[:], leave[:], leave_diag[:, 0:S], ALU.subtract).then_inc(dtw_step, 1)
                        dve.wait_ge(dtw_step, n + 5)
                        dve.tensor_tensor(enter[:], leave_up[:], leave_diag[:, 1:S + 1], ALU.add).then_inc(dtw_step, 1)
                        dve.wait_ge(dtw_step, n + 6)

        run("C", tokens_stored["C"])


def flat(ap):
    return ap.rearrange("p o n -> p (o n)")



def chunked(wt):
    k, n = wt.shape
    return wt.reshape(k // P, P, n).transpose(1, 0, 2).reshape(P, k // P * n)


def layouts(a):
    nb = a["x"].shape[0]
    g = {}
    g["x"] = a["x"].reshape(nb, QT, P, D).transpose(0, 2, 1, 3).reshape(nb, P, QT * D)
    g["xT"] = a["x"].transpose(0, 2, 1).reshape(nb, FC, P, S).transpose(0, 2, 1, 3).reshape(nb, P, FC * S)
    g["ctxT"] = a["ctx_1024"].transpose(0, 2, 1).reshape(nb, FC, P, C).transpose(0, 2, 1, 3).reshape(nb, P, FC * C)
    g["ctx"] = a["ctx_1024"]
    qkv, qkv_b = a["L1_attn_qkv_w"], a["L1_attn_qkv_b"]
    square = {"A1_wq": a["L0_attn_Wq"], "A1_wk": a["L0_attn_Wk"], "A1_wv": a["L0_attn_Wv"],
              "A2_wq": a["L0_xattn_wq"], "A2_wk": a["L0_xattn_wk"], "A2_wv": a["L0_xattn_wv"],
              "A2_wo": a["L0_xattn_wo"],
              "A3_wq": qkv[0:D], "A3_wk": qkv[D:2 * D], "A3_wv": qkv[2 * D:3 * D], "A3_wo": a["L1_attn_proj_w"],
              "A4_wq": a["L1_ffn_Wq"], "A4_wk": a["L1_ffn_Wk"], "A4_wv": a["L1_ffn_Wv"], "A4_wo": a["L1_ffn_Wp"]}
    for n, m in square.items():
        g[n] = chunked(m.T)
    g.update(w_gate=chunked(a["L0_ffn_w_gate"].T), w_up=chunked(a["L0_ffn_w_up"].T),
             w_down=chunked(a["L0_ffn_w_down"].T))
    g.update(A2_bq=a["L0_xattn_bq"], A2_bk=a["L0_xattn_bk"], A4_bk=a["L1_ffn_bk"], A2_bv=a["L0_xattn_bv"], A2_bo=a["L0_xattn_bo"], A3_bq=qkv_b[0:D], A3_bk=qkv_b[D:2 * D],
             A3_bv=qkv_b[2 * D:3 * D], A3_bo=a["L1_attn_proj_b"], A4_bq=a["L1_ffn_bq"], A4_bv=a["L1_ffn_bv"],
             A4_bo=a["L1_ffn_bp"])
    g["gate_w"] = chunked(np.concatenate([a["L1_ffn_Wr"], a["L1_ffn_Ws"]], axis=0).T)
    g["gate_b"] = np.concatenate([a["L1_ffn_br"], a["L1_ffn_bs"]])
    g["temperature"] = a["L1_ffn_temperature"].reshape(H)
    g["query_embedding"] = a["L1_ffn_query_embedding"].reshape(H * HD)
    g["ident"] = np.eye(P, dtype=np.float32)
    r = np.arange(P) % 32
    g["mask"] = np.stack([r < 16, r >= 16, r == 16, r == 0], axis=1).astype(np.float32)
    inv_freq = (1.0 / np.float32(10000.0) ** (np.arange(0, HD, 2, dtype=np.float32) / np.float32(HD))).astype(np.float32)
    freqs = np.arange(S, dtype=np.float32)[:, None] * inv_freq[None, :]
    emb = np.concatenate([freqs, freqs], axis=-1)
    sign = np.where(np.arange(HD) % 2 == 0, -1.0, 1.0).astype(np.float32)
    for n, t in (("rope_cos", np.cos(emb)), ("rope_sin", np.sin(emb) * sign)):
        g[n] = t.astype(np.float32).reshape(QT, P, HD).transpose(1, 0, 2).reshape(P, QT * HD)
    return {n: np.ascontiguousarray(v) for n, v in g.items()}, list(square)


def program(nc, arrays, square, nb):
    io = {n: nc.dram_tensor(f"in_{n}", v.shape, mybir.dt.from_np(v.dtype), kind="ExternalInput").ap()
          for n, v in arrays.items()}
    io["square_weights"] = square
    out = nc.dram_tensor("out_0", (nb, P, QT * D), F32, kind="ExternalOutput").ap()
    build(nc, nb, io, out)


def kernel(**inputs):
    import concourse.bacc as bacc
    from concourse.bass_utils import run_bass_kernel_spmd

    arrays, square = layouts({n: np.asarray(v) for n, v in inputs.items()})
    nb = arrays["x"].shape[0]
    nc = bacc.Bacc("TRN2", target_bir_lowering=False, num_devices=1)
    program(nc, arrays, square, nb)
    r = run_bass_kernel_spmd(nc, [{f"in_{n}": v for n, v in arrays.items()}], core_ids=[0])
    got = r.results[0]["out_0"]
    return got.reshape(nb, P, QT, D).transpose(0, 2, 1, 3).reshape(nb, S, D)
```
